# Optimizing a Trainium2 kernel written in Bass

```python
import numpy as np
import jax
import jax.numpy as jnp

def _softmax(x, axis=-1):
    return jax.nn.softmax(x, axis=axis)

def _gelu(x):
    return jax.nn.gelu(x, approximate=True)

def _silu(x):
    return jax.nn.silu(x)

def _sigmoid(x):
    return jax.nn.sigmoid(x)

def _layernorm(x, axis=-1, eps=1e-05):
    m = jnp.mean(x, axis=axis, keepdims=True)
    v = jnp.var(x, axis=axis, keepdims=True)
    return (x - m) / jnp.sqrt(v + eps)

def _scatter_add(tgt, idx, src, axis=0):
    return tgt.at[idx].add(src)

def _segment_sum(src, seg, n):
    return jax.ops.segment_sum(src, seg, n)
kernel_name = 'mk_xattn_ffn_d4_seqx_r8_bcfab8'

def setup_inputs(seed: int=0):
    np.random.seed(seed)
    _w = jnp.asarray

    def _rec_inputs():
        import jax
        import jax.numpy as jnp
        _rk = jax.random.key(seed)
        x = -0.0002928 + 1 * jax.random.normal(jax.random.fold_in(_rk, 1), (8, 256, 128), jnp.float32)
        _lenS = 256 - jax.random.randint(jax.random.fold_in(_rk, 7), (8,), 0, max(1, 256 // 4) + 1, jnp.int32)
        _lenS2 = 512 - jax.random.randint(jax.random.fold_in(_rk, 8), (8,), 0, max(1, 512 // 4) + 1, jnp.int32)
        _ctx_1024P = jax.random.normal(jax.random.fold_in(_rk, 11), (8, 16, 128), jnp.float32)
        _ctx_1024c = jax.random.dirichlet(jax.random.fold_in(_rk, 511), 0.3 * jnp.ones((16,), jnp.float32), (8, 512))
        _ctx_1024t = jnp.einsum('bsk,bkd->bsd', _ctx_1024c, _ctx_1024P)
        _ctx_1024t = _ctx_1024t * jax.lax.rsqrt(jnp.mean(jnp.square(_ctx_1024t)) + 1e-12) * 0.953939
        ctx_1024 = -1.39393e-06 + 0.999914 * (_ctx_1024t + 0.3 * jax.random.normal(jax.random.fold_in(_rk, 611), (8, 512, 128), jnp.float32))
        _validS = jnp.arange(256)[None, :] < _lenS[:, None]
        _validS2 = jnp.arange(512)[None, :] < _lenS2[:, None]
        _causal = jnp.tril(jnp.ones((256, 256), dtype=bool))
        mask_1x1xSxS2_ik0 = jnp.where(jnp.broadcast_to(_validS2[0:1, None, None, :], (1, 1, 256, 512)), 0, 1).astype(jnp.int32)
        mask_Bx1x1xS2_if1 = jnp.where(jnp.ones((8, 1, 1, 512), dtype=bool), 1, 0).astype(jnp.int32)
        return (x, ctx_1024, mask_1x1xSxS2_ik0, mask_Bx1x1xS2_if1)
    x, ctx_1024, mask_1x1xSxS2_ik0, mask_Bx1x1xS2_if1 = _rec_inputs()

    def _L0_xattn_setup():
        import jax, jax.numpy as jnp
        import numpy as np
        N_HEAD = 16
        D_MODEL = 128
        B, S = (2, 256)

        def _split(x):
            b, s, d = x.shape
            return x.reshape(b, s, N_HEAD, d // N_HEAD).transpose(0, 2, 1, 3)
        key = jax.random.key(seed)
        ks = jax.random.split(key, 11)
        s = 1.0 / np.sqrt(D_MODEL)
        inp = {'q': jax.random.normal(ks[0], (B, S, D_MODEL), jnp.float32), 'k': jax.random.normal(ks[1], (B, S, D_MODEL), jnp.float32), 'v': jax.random.normal(ks[2], (B, S, D_MODEL), jnp.float32), 'wq': jax.random.normal(ks[3], (D_MODEL, D_MODEL), jnp.float32) * s, 'bq': jax.random.normal(ks[4], (D_MODEL,), jnp.float32) * 0.01, 'wk': jax.random.normal(ks[5], (D_MODEL, D_MODEL), jnp.float32) * s, 'bk': jax.random.normal(ks[6], (D_MODEL,), jnp.float32) * 0.01, 'wv': jax.random.normal(ks[7], (D_MODEL, D_MODEL), jnp.float32) * s, 'bv': jax.random.normal(ks[8], (D_MODEL,), jnp.float32) * 0.01, 'wo': jax.random.normal(ks[9], (D_MODEL, D_MODEL), jnp.float32) * s, 'bo': jax.random.normal(ks[10], (D_MODEL,), jnp.float32) * 0.01}
        return inp
    _L0_xattn_all = _L0_xattn_setup()
    _L0_xattn_in = {k: v for k, v in _L0_xattn_all.items() if k in ('wq', 'bq', 'wk', 'bk', 'wv', 'bv', 'wo', 'bo')}
    del _L0_xattn_all

    def _L0_ffn_setup():
        import jax, jax.numpy as jnp
        import numpy as np

        def _ste(w, w_q):
            return w + jax.lax.stop_gradient(w_q - w)

        def quantize_w8_per(w, axis):
            amax = jnp.clip(jnp.max(jnp.abs(w), axis=axis, keepdims=True), 1e-08, None)
            scale = 127.0 / amax
            w_q = jnp.clip(jnp.round(w * scale), -128.0, 127.0) / scale
            return _ste(w, w_q)

        def quantize_a16(x):
            amax = jnp.clip(jnp.max(jnp.abs(x)), 1e-08, None)
            scale = 32767.0 / amax
            x_q = jnp.clip(jnp.round(x * scale), -32768.0, 32767.0) / scale
            return _ste(x, x_q)
        key = jax.random.key(seed)
        k1, k2, k3 = jax.random.split(key, 3)
        d_model, d_ff = (128, 512)
        x = jax.random.normal(k1, (4, 256, d_model), dtype=jnp.float32)
        W_in = jax.random.normal(k2, (d_model, d_ff), dtype=jnp.float32) / np.sqrt(d_model)
        b_in = jnp.zeros((d_ff,), dtype=jnp.float32)
        W_out = jax.random.normal(k3, (d_ff, d_model), dtype=jnp.float32) / np.sqrt(d_ff)
        b_out = jnp.zeros((d_model,), dtype=jnp.float32)
        return {'x': x, 'W_in': W_in, 'b_in': b_in, 'W_out': W_out, 'b_out': b_out}
    _L0_ffn_all = _L0_ffn_setup()
    _L0_ffn_in = {k: v for k, v in _L0_ffn_all.items() if k in ('W_in', 'b_in', 'W_out', 'b_out')}
    del _L0_ffn_all

    def _L1_xattn_setup():
        import jax, jax.numpy as jnp
        import numpy as np
        D_MODEL = 128
        NUM_HEADS = 16
        DEPTH = D_MODEL // NUM_HEADS

        def _split_heads(x, B):
            return x.reshape(B, -1, NUM_HEADS, DEPTH).transpose(0, 2, 1, 3)
        key = jax.random.key(seed)
        ks = jax.random.split(key, 10)
        B, LQ, LK = (4, 256, 256)
        bound = float(np.sqrt(6.0 / (D_MODEL + D_MODEL)))

        def w(k):
            return jax.random.uniform(k, (D_MODEL, D_MODEL), jnp.float32, -bound, bound)
        return {'query': jax.random.normal(ks[0], (B, LQ, D_MODEL), jnp.float32), 'value': jax.random.normal(ks[1], (B, LK, D_MODEL), jnp.float32), 'wq': w(ks[2]), 'bq': jnp.zeros((D_MODEL,), jnp.float32), 'wk': w(ks[3]), 'bk': jnp.zeros((D_MODEL,), jnp.float32), 'wv': w(ks[4]), 'bv': jnp.zeros((D_MODEL,), jnp.float32), 'wo': w(ks[5]), 'bo': jnp.zeros((D_MODEL,), jnp.float32)}
    _L1_xattn_all = _L1_xattn_setup()
    _L1_xattn_in = {k: v for k, v in _L1_xattn_all.items() if k in ('wq', 'bq', 'wk', 'bk', 'wv', 'bv', 'wo', 'bo')}
    del _L1_xattn_all

    def _L1_ffn_setup():
        import jax, jax.numpy as jnp
        import numpy as np
        B, S, DIM = (4, 256, 128)
        E, K, HID = (8, 2, 512)
        key = jax.random.key(seed)
        ks = jax.random.split(key, 8)
        init = lambda k, sh: jax.random.normal(k, sh, jnp.float32) * 0.02
        return {'x': jax.random.normal(ks[0], (B, S, DIM), jnp.float32), 'gate_w': init(ks[1], (DIM, E)), 'gate_b': jnp.zeros((E,), jnp.float32), 'w1': init(ks[2], (E, DIM, HID)), 'b1': jnp.zeros((E, HID), jnp.float32), 'w2': init(ks[3], (E, HID, DIM)), 'b2': jnp.zeros((E, DIM), jnp.float32), 'ws1': init(ks[4], (DIM, HID)), 'bs1': jnp.zeros((HID,), jnp.float32), 'ws2': init(ks[5], (HID, DIM)), 'bs2': jnp.zeros((DIM,), jnp.float32)}
    _L1_ffn_all = _L1_ffn_setup()
    _L1_ffn_in = {k: v for k, v in _L1_ffn_all.items() if k in ('gate_w', 'gate_b', 'w1', 'b1', 'w2', 'b2', 'ws1', 'bs1', 'ws2', 'bs2')}
    del _L1_ffn_all

    def _L2_xattn_setup():
        import jax, jax.numpy as jnp
        import numpy as np
        D = 128
        H = 16
        DK = D // H
        B = 1
        S = 512

        def _split_heads(x):
            b, s, _ = x.shape
            return x.reshape(b, s, H, DK).transpose(0, 2, 1, 3)
        key = jax.random.key(seed)
        ks = jax.random.split(key, 12)
        scale = 1.0 / np.sqrt(D)
        inp = {'Q': jax.random.normal(ks[0], (B, S, D), jnp.float32), 'K': jax.random.normal(ks[1], (B, S, D), jnp.float32), 'V': jax.random.normal(ks[2], (B, S, D), jnp.float32), 'Wq_w': jax.random.normal(ks[3], (D, D), jnp.float32) * scale, 'Wq_b': jax.random.normal(ks[4], (D,), jnp.float32) * scale, 'Wk_w': jax.random.normal(ks[5], (D, D), jnp.float32) * scale, 'Wk_b': jax.random.normal(ks[6], (D,), jnp.float32) * scale, 'Wv_w': jax.random.normal(ks[7], (D, D), jnp.float32) * scale, 'Wv_b': jax.random.normal(ks[8], (D,), jnp.float32) * scale, 'Wo_w': jax.random.normal(ks[9], (D, D), jnp.float32) * scale, 'Wo_b': jax.random.normal(ks[10], (D,), jnp.float32) * scale, 'mask': jnp.tril(jnp.ones((S, S), jnp.int32))[None, None, :, :]}
        return inp
    _L2_xattn_all = _L2_xattn_setup()
    _L2_xattn_in = {k: v for k, v in _L2_xattn_all.items() if k in ('Wq_w', 'Wq_b', 'Wk_w', 'Wk_b', 'Wv_w', 'Wv_b', 'Wo_w', 'Wo_b')}
    del _L2_xattn_all

    def _L2_ffn_setup():
        import jax, jax.numpy as jnp
        import numpy as np
        EMB = 128
        HID = 256
        HEADS = 16
        HEAD_DIM = EMB // HEADS
        EXPERTS = 8
        TOPK = 2
        EPS = 1e-05

        def layernorm(x, scale, shift):
            mean = jnp.mean(x, axis=-1, keepdims=True)
            var = jnp.mean((x - mean) ** 2, axis=-1, keepdims=True)
            return scale * (x - mean) / jnp.sqrt(var + EPS) + shift

        def attention(x, wq, wk, wv, wo, bo):
            b, t, _ = x.shape
            q = (x @ wq).reshape(b, t, HEADS, HEAD_DIM)
            k = (x @ wk).reshape(b, t, HEADS, HEAD_DIM)
            v = (x @ wv).reshape(b, t, HEADS, HEAD_DIM)
            scores = jnp.einsum('bqhd,bkhd->bhqk', q, k)
            mask = jnp.arange(t)[:, None] < jnp.arange(t)[None, :]
            scores = jnp.where(mask, -jnp.inf, scores)
            attn = jax.nn.softmax(scores / np.sqrt(HEAD_DIM), axis=-1)
            ctx = jnp.einsum('bhqk,bkhd->bqhd', attn, v).reshape(b, t, EMB)
            return ctx @ wo + bo

        def moe_ff(x, gate_w, w1, w2, w3):
            b, t, d = x.shape
            xf = x.reshape(b * t, d)
            scores = xf @ gate_w
            topk_scores, topk_idx = jax.lax.top_k(scores, TOPK)
            topk_probs = jax.nn.softmax(topk_scores, axis=-1)
            weight = jnp.sum(jax.nn.one_hot(topk_idx, EXPERTS, dtype=xf.dtype) * topk_probs[..., None], axis=1)
            h = jax.nn.silu(jnp.einsum('td,edh->eth', xf, w1)) * jnp.einsum('td,edh->eth', xf, w2)
            out_e = jnp.einsum('eth,ehd->etd', h, w3)
            out = jnp.einsum('etd,te->td', out_e, weight)
            return out.reshape(b, t, d)
        key = jax.random.key(seed)
        ks = jax.random.split(key, 12)
        s = lambda k, shape, fan: jax.random.normal(k, shape, jnp.float32) / np.sqrt(fan)
        return {'x': jax.random.normal(ks[0], (2, 256, EMB), jnp.float32), 'ln1_scale': jnp.ones((EMB,), jnp.float32), 'ln1_shift': jnp.zeros((EMB,), jnp.float32), 'wq': s(ks[1], (EMB, EMB), EMB), 'wk': s(ks[2], (EMB, EMB), EMB), 'wv': s(ks[3], (EMB, EMB), EMB), 'wo': s(ks[4], (EMB, EMB), EMB), 'bo': jnp.zeros((EMB,), jnp.float32), 'ln2_scale': jnp.ones((EMB,), jnp.float32), 'ln2_shift': jnp.zeros((EMB,), jnp.float32), 'gate_w': s(ks[5], (EMB, EXPERTS), EMB), 'w1': s(ks[6], (EXPERTS, EMB, HID), EMB), 'w2': s(ks[7], (EXPERTS, EMB, HID), EMB), 'w3': s(ks[8], (EXPERTS, HID, EMB), HID)}
    _L2_ffn_all = _L2_ffn_setup()
    _L2_ffn_in = {k: v for k, v in _L2_ffn_all.items() if k in ('ln1_scale', 'ln1_shift', 'wq', 'wk', 'wv', 'wo', 'bo', 'ln2_scale', 'ln2_shift', 'gate_w', 'w1', 'w2', 'w3')}
    del _L2_ffn_all

    def _L3_xattn_setup():
        import jax, jax.numpy as jnp
        import numpy as np
        EMBED = 128
        HEADS = 16
        HEAD_DIM = EMBED // HEADS
        B, S = (4, 256)
        key = jax.random.key(seed)
        ks = jax.random.split(key, 8)
        values = jax.random.normal(ks[0], (B, S, EMBED), dtype=jnp.float32)
        keys_in = jax.random.normal(ks[1], (B, S, EMBED), dtype=jnp.float32)
        query = jax.random.normal(ks[2], (B, S, EMBED), dtype=jnp.float32)
        mask = jnp.ones((B, 1, 1, S), dtype=jnp.int32)
        sc = 1.0 / np.sqrt(HEAD_DIM)
        Wv = jax.random.normal(ks[3], (HEAD_DIM, HEAD_DIM), dtype=jnp.float32) * sc
        Wk = jax.random.normal(ks[4], (HEAD_DIM, HEAD_DIM), dtype=jnp.float32) * sc
        Wq = jax.random.normal(ks[5], (HEAD_DIM, HEAD_DIM), dtype=jnp.float32) * sc
        Wo = jax.random.normal(ks[6], (EMBED, EMBED), dtype=jnp.float32) * (1.0 / np.sqrt(EMBED))
        bo = jnp.zeros((EMBED,), dtype=jnp.float32)
        return {'values': values, 'keys': keys_in, 'query': query, 'mask': mask, 'Wv': Wv, 'Wk': Wk, 'Wq': Wq, 'Wo': Wo, 'bo': bo}
    _L3_xattn_all = _L3_xattn_setup()
    _L3_xattn_in = {k: v for k, v in _L3_xattn_all.items() if k in ('Wv', 'Wk', 'Wq', 'Wo', 'bo')}
    del _L3_xattn_all

    def _L3_ffn_setup():
        import jax, jax.numpy as jnp
        import numpy as np
        E = 8
        TOP_K = 2
        H = 128
        F = 512
        LN_EPS = 1e-12
        key = jax.random.key(seed)
        ks = jax.random.split(key, 9)
        s = lambda k, shape, scale: jax.random.normal(k, shape, dtype=jnp.float32) * scale
        return {'hidden_states': s(ks[0], (4, 256, H), 1.0), 'Wr': s(ks[1], (E, H), 0.02), 'br': jnp.zeros((E,), jnp.float32), 'W1': s(ks[2], (E, F, H), 0.02), 'b1': jnp.zeros((E, F), jnp.float32), 'W2': s(ks[3], (E, H, F), 0.02), 'b2': jnp.zeros((E, H), jnp.float32), 'ln_w': jnp.ones((H,), jnp.float32), 'ln_b': jnp.zeros((H,), jnp.float32)}
    _L3_ffn_all = _L3_ffn_setup()
    _L3_ffn_in = {k: v for k, v in _L3_ffn_all.items() if k in ('Wr', 'br', 'W1', 'b1', 'W2', 'b2', 'ln_w', 'ln_b')}
    del _L3_ffn_all
    return {'x': x, 'ctx_1024': ctx_1024, 'mask_1x1xSxS2_ik0': mask_1x1xSxS2_ik0, 'mask_Bx1x1xS2_if1': mask_Bx1x1xS2_if1, 'L0_xattn_wq': _L0_xattn_in['wq'], 'L0_xattn_bq': _L0_xattn_in['bq'], 'L0_xattn_wk': _L0_xattn_in['wk'], 'L0_xattn_bk': _L0_xattn_in['bk'], 'L0_xattn_wv': _L0_xattn_in['wv'], 'L0_xattn_bv': _L0_xattn_in['bv'], 'L0_xattn_wo': _L0_xattn_in['wo'], 'L0_xattn_bo': _L0_xattn_in['bo'], 'L0_ffn_W_in': _L0_ffn_in['W_in'], 'L0_ffn_b_in': _L0_ffn_in['b_in'], 'L0_ffn_W_out': _L0_ffn_in['W_out'], 'L0_ffn_b_out': _L0_ffn_in['b_out'], 'L1_xattn_wq': _L1_xattn_in['wq'], 'L1_xattn_bq': _L1_xattn_in['bq'], 'L1_xattn_wk': _L1_xattn_in['wk'], 'L1_xattn_bk': _L1_xattn_in['bk'], 'L1_xattn_wv': _L1_xattn_in['wv'], 'L1_xattn_bv': _L1_xattn_in['bv'], 'L1_xattn_wo': _L1_xattn_in['wo'], 'L1_xattn_bo': _L1_xattn_in['bo'], 'L1_ffn_gate_w': _L1_ffn_in['gate_w'], 'L1_ffn_gate_b': _L1_ffn_in['gate_b'], 'L1_ffn_w1': _L1_ffn_in['w1'], 'L1_ffn_b1': _L1_ffn_in['b1'], 'L1_ffn_w2': _L1_ffn_in['w2'], 'L1_ffn_b2': _L1_ffn_in['b2'], 'L1_ffn_ws1': _L1_ffn_in['ws1'], 'L1_ffn_bs1': _L1_ffn_in['bs1'], 'L1_ffn_ws2': _L1_ffn_in['ws2'], 'L1_ffn_bs2': _L1_ffn_in['bs2'], 'L2_xattn_Wq_w': _L2_xattn_in['Wq_w'], 'L2_xattn_Wq_b': _L2_xattn_in['Wq_b'], 'L2_xattn_Wk_w': _L2_xattn_in['Wk_w'], 'L2_xattn_Wk_b': _L2_xattn_in['Wk_b'], 'L2_xattn_Wv_w': _L2_xattn_in['Wv_w'], 'L2_xattn_Wv_b': _L2_xattn_in['Wv_b'], 'L2_xattn_Wo_w': _L2_xattn_in['Wo_w'], 'L2_xattn_Wo_b': _L2_xattn_in['Wo_b'], 'L2_ffn_ln1_scale': _L2_ffn_in['ln1_scale'], 'L2_ffn_ln1_shift': _L2_ffn_in['ln1_shift'], 'L2_ffn_wq': _L2_ffn_in['wq'], 'L2_ffn_wk': _L2_ffn_in['wk'], 'L2_ffn_wv': _L2_ffn_in['wv'], 'L2_ffn_wo': _L2_ffn_in['wo'], 'L2_ffn_bo': _L2_ffn_in['bo'], 'L2_ffn_ln2_scale': _L2_ffn_in['ln2_scale'], 'L2_ffn_ln2_shift': _L2_ffn_in['ln2_shift'], 'L2_ffn_gate_w': _L2_ffn_in['gate_w'], 'L2_ffn_w1': _L2_ffn_in['w1'], 'L2_ffn_w2': _L2_ffn_in['w2'], 'L2_ffn_w3': _L2_ffn_in['w3'], 'L3_xattn_Wv': _L3_xattn_in['Wv'], 'L3_xattn_Wk': _L3_xattn_in['Wk'], 'L3_xattn_Wq': _L3_xattn_in['Wq'], 'L3_xattn_Wo': _L3_xattn_in['Wo'], 'L3_xattn_bo': _L3_xattn_in['bo'], 'L3_ffn_Wr': _L3_ffn_in['Wr'], 'L3_ffn_br': _L3_ffn_in['br'], 'L3_ffn_W1': _L3_ffn_in['W1'], 'L3_ffn_b1': _L3_ffn_in['b1'], 'L3_ffn_W2': _L3_ffn_in['W2'], 'L3_ffn_b2': _L3_ffn_in['b2'], 'L3_ffn_ln_w': _L3_ffn_in['ln_w'], 'L3_ffn_ln_b': _L3_ffn_in['ln_b']}

def reference(x, ctx_1024, mask_1x1xSxS2_ik0, mask_Bx1x1xS2_if1, L0_xattn_wq, L0_xattn_bq, L0_xattn_wk, L0_xattn_bk, L0_xattn_wv, L0_xattn_bv, L0_xattn_wo, L0_xattn_bo, L0_ffn_W_in, L0_ffn_b_in, L0_ffn_W_out, L0_ffn_b_out, L1_xattn_wq, L1_xattn_bq, L1_xattn_wk, L1_xattn_bk, L1_xattn_wv, L1_xattn_bv, L1_xattn_wo, L1_xattn_bo, L1_ffn_gate_w, L1_ffn_gate_b, L1_ffn_w1, L1_ffn_b1, L1_ffn_w2, L1_ffn_b2, L1_ffn_ws1, L1_ffn_bs1, L1_ffn_ws2, L1_ffn_bs2, L2_xattn_Wq_w, L2_xattn_Wq_b, L2_xattn_Wk_w, L2_xattn_Wk_b, L2_xattn_Wv_w, L2_xattn_Wv_b, L2_xattn_Wo_w, L2_xattn_Wo_b, L2_ffn_ln1_scale, L2_ffn_ln1_shift, L2_ffn_wq, L2_ffn_wk, L2_ffn_wv, L2_ffn_wo, L2_ffn_bo, L2_ffn_ln2_scale, L2_ffn_ln2_shift, L2_ffn_gate_w, L2_ffn_w1, L2_ffn_w2, L2_ffn_w3, L3_xattn_Wv, L3_xattn_Wk, L3_xattn_Wq, L3_xattn_Wo, L3_xattn_bo, L3_ffn_Wr, L3_ffn_br, L3_ffn_W1, L3_ffn_b1, L3_ffn_W2, L3_ffn_b2, L3_ffn_ln_w, L3_ffn_ln_b):
    import jax
    import jax.numpy as jnp

    def _L0_xattn_ref(q, k, v, wq, bq, wk, bk, wv, bv, wo, bo):
        import jax, jax.numpy as jnp
        import numpy as np
        N_HEAD = 16
        D_MODEL = 128
        B, S = (2, 256)

        def _split(x):
            b, s, d = x.shape
            return x.reshape(b, s, N_HEAD, d // N_HEAD).transpose(0, 2, 1, 3)
        qh = _split(q @ wq.T + bq)
        kh = _split(k @ wk.T + bk)
        vh = _split(v @ wv.T + bv)
        d_head = qh.shape[-1]
        scores = jnp.einsum('bhqd,bhkd->bhqk', qh, kh) / jnp.sqrt(jnp.float32(d_head))
        attn = jax.nn.softmax(scores, axis=-1)
        out = jnp.einsum('bhqk,bhkd->bhqd', attn, vh)
        b, h, s, dh = out.shape
        out = out.transpose(0, 2, 1, 3).reshape(b, s, h * dh)
        return out @ wo.T + bo

    def _L0_ffn_ref(x, W_in, b_in, W_out, b_out):
        import jax, jax.numpy as jnp
        import numpy as np

        def _ste(w, w_q):
            return w + jax.lax.stop_gradient(w_q - w)

        def quantize_w8_per(w, axis):
            amax = jnp.clip(jnp.max(jnp.abs(w), axis=axis, keepdims=True), 1e-08, None)
            scale = 127.0 / amax
            w_q = jnp.clip(jnp.round(w * scale), -128.0, 127.0) / scale
            return _ste(w, w_q)

        def quantize_a16(x):
            amax = jnp.clip(jnp.max(jnp.abs(x)), 1e-08, None)
            scale = 32767.0 / amax
            x_q = jnp.clip(jnp.round(x * scale), -32768.0, 32767.0) / scale
            return _ste(x, x_q)
        W_in_sim = quantize_w8_per(W_in, axis=0)
        W_out_sim = quantize_w8_per(W_out, axis=1)
        x_sim = quantize_a16(x)
        hidden = jax.nn.gelu(x_sim @ W_in_sim + b_in, approximate=False)
        hidden_sim = quantize_a16(hidden)
        out = hidden_sim @ W_out_sim + b_out
        return out

    def _L1_xattn_ref(query, value, wq, bq, wk, bk, wv, bv, wo, bo):
        import jax, jax.numpy as jnp
        import numpy as np
        D_MODEL = 128
        NUM_HEADS = 16
        DEPTH = D_MODEL // NUM_HEADS

        def _split_heads(x, B):
            return x.reshape(B, -1, NUM_HEADS, DEPTH).transpose(0, 2, 1, 3)
        B = query.shape[0]
        q = _split_heads(query @ wq.T + bq, B)
        k = _split_heads(value @ wk.T + bk, B)
        v = _split_heads(value @ wv.T + bv, B)
        scale = jnp.sqrt(jnp.asarray(DEPTH, dtype=q.dtype))
        scores = jnp.einsum('bhqd,bhkd->bhqk', q, k) / scale
        attn = jax.nn.softmax(scores, axis=-1)
        ctx = jnp.einsum('bhqk,bhkd->bhqd', attn, v)
        ctx = ctx.transpose(0, 2, 1, 3).reshape(B, -1, D_MODEL)
        return ctx @ wo.T + bo

    def _L1_ffn_ref(x, gate_w, gate_b, w1, b1, w2, b2, ws1, bs1, ws2, bs2):
        import jax, jax.numpy as jnp
        import numpy as np
        B, S, DIM = (4, 256, 128)
        E, K, HID = (8, 2, 512)
        orig_shape = x.shape
        xf = x.reshape(-1, DIM)
        logits = xf @ gate_w + gate_b
        top_w, top_i = jax.lax.top_k(logits, K)
        gw = jax.nn.softmax(top_w, axis=-1).astype(xf.dtype)
        combine = (gw[:, :, None] * jax.nn.one_hot(top_i, E, dtype=xf.dtype)).sum(axis=1)
        out = jnp.zeros_like(xf)
        for e in range(E):
            h = jax.nn.gelu(xf @ w1[e] + b1[e], approximate=False)
            out = out + combine[:, e:e + 1] * (h @ w2[e] + b2[e])
        shared = jax.nn.gelu(xf @ ws1 + bs1, approximate=False) @ ws2 + bs2
        return (out + shared).reshape(orig_shape)

    def _L2_xattn_ref(Q, K, V, Wq_w, Wq_b, Wk_w, Wk_b, Wv_w, Wv_b, Wo_w, Wo_b, mask):
        import jax, jax.numpy as jnp
        import numpy as np
        D = 128
        H = 16
        DK = D // H
        B = 1
        S = 512

        def _split_heads(x):
            b, s, _ = x.shape
            return x.reshape(b, s, H, DK).transpose(0, 2, 1, 3)
        q = _split_heads(Q @ Wq_w.T + Wq_b)
        k = _split_heads(K @ Wk_w.T + Wk_b)
        v = _split_heads(V @ Wv_w.T + Wv_b)
        scores = jnp.einsum('bhqd,bhkd->bhqk', q, k) / np.sqrt(DK).astype(np.float32)
        scores = jnp.where(mask == 0, jnp.float32(-1000000000.0), scores)
        attn = jax.nn.softmax(scores, axis=-1)
        out = jnp.einsum('bhqk,bhkd->bhqd', attn, v)
        out = out.transpose(0, 2, 1, 3).reshape(Q.shape[0], Q.shape[1], D)
        return out @ Wo_w.T + Wo_b

    def _L2_ffn_ref(x, ln1_scale, ln1_shift, wq, wk, wv, wo, bo, ln2_scale, ln2_shift, gate_w, w1, w2, w3):
        import jax, jax.numpy as jnp
        import numpy as np
        EMB = 128
        HID = 256
        HEADS = 16
        HEAD_DIM = EMB // HEADS
        EXPERTS = 8
        TOPK = 2
        EPS = 1e-05

        def layernorm(x, scale, shift):
            mean = jnp.mean(x, axis=-1, keepdims=True)
            var = jnp.mean((x - mean) ** 2, axis=-1, keepdims=True)
            return scale * (x - mean) / jnp.sqrt(var + EPS) + shift

        def attention(x, wq, wk, wv, wo, bo):
            b, t, _ = x.shape
            q = (x @ wq).reshape(b, t, HEADS, HEAD_DIM)
            k = (x @ wk).reshape(b, t, HEADS, HEAD_DIM)
            v = (x @ wv).reshape(b, t, HEADS, HEAD_DIM)
            scores = jnp.einsum('bqhd,bkhd->bhqk', q, k)
            mask = jnp.arange(t)[:, None] < jnp.arange(t)[None, :]
            scores = jnp.where(mask, -jnp.inf, scores)
            attn = jax.nn.softmax(scores / np.sqrt(HEAD_DIM), axis=-1)
            ctx = jnp.einsum('bhqk,bkhd->bqhd', attn, v).reshape(b, t, EMB)
            return ctx @ wo + bo

        def moe_ff(x, gate_w, w1, w2, w3):
            b, t, d = x.shape
            xf = x.reshape(b * t, d)
            scores = xf @ gate_w
            topk_scores, topk_idx = jax.lax.top_k(scores, TOPK)
            topk_probs = jax.nn.softmax(topk_scores, axis=-1)
            weight = jnp.sum(jax.nn.one_hot(topk_idx, EXPERTS, dtype=xf.dtype) * topk_probs[..., None], axis=1)
            h = jax.nn.silu(jnp.einsum('td,edh->eth', xf, w1)) * jnp.einsum('td,edh->eth', xf, w2)
            out_e = jnp.einsum('eth,ehd->etd', h, w3)
            out = jnp.einsum('etd,te->td', out_e, weight)
            return out.reshape(b, t, d)
        h = layernorm(x, ln1_scale, ln1_shift)
        x = x + attention(h, wq, wk, wv, wo, bo)
        h = layernorm(x, ln2_scale, ln2_shift)
        x = x + moe_ff(h, gate_w, w1, w2, w3)
        return x

    def _L3_xattn_ref(values, keys, query, mask, Wv, Wk, Wq, Wo, bo):
        import jax, jax.numpy as jnp
        import numpy as np
        EMBED = 128
        HEADS = 16
        HEAD_DIM = EMBED // HEADS
        B, S = (4, 256)
        n = query.shape[0]
        vl, kl, ql = (values.shape[1], keys.shape[1], query.shape[1])
        h, d = (HEADS, HEAD_DIM)
        v = values.reshape(n, vl, h, d)
        k = keys.reshape(n, kl, h, d)
        q = query.reshape(n, ql, h, d)
        v = jnp.einsum('nlhd,ed->nlhe', v, Wv)
        k = jnp.einsum('nlhd,ed->nlhe', k, Wk)
        q = jnp.einsum('nlhd,ed->nlhe', q, Wq)
        energy = jnp.einsum('nqhd,nkhd->nhqk', q, k)
        energy = jnp.where(mask == 0, jnp.float32(-1e+20), energy)
        attn = jax.nn.softmax(energy / jnp.sqrt(jnp.float32(EMBED)), axis=3)
        out = jnp.einsum('nhql,nlhd->nqhd', attn, v).reshape(n, ql, h * d)
        return out @ Wo.T + bo

    def _L3_ffn_ref(hidden_states, Wr, br, W1, b1, W2, b2, ln_w, ln_b):
        import jax, jax.numpy as jnp
        import numpy as np
        E = 8
        TOP_K = 2
        H = 128
        F = 512
        LN_EPS = 1e-12
        bsz, seqlen, h = hidden_states.shape
        x = hidden_states.reshape(-1, h)
        logits = x @ Wr.T + br
        topk_vals, topk_idx = jax.lax.top_k(logits, TOP_K)
        topk_w = jax.nn.softmax(topk_vals, axis=-1)
        out = jnp.zeros_like(x)
        for e in range(E):
            cw = jnp.sum(topk_w * (topk_idx == e), axis=-1)
            y = jax.nn.gelu(x @ W1[e].T + b1[e], approximate=False) @ W2[e].T + b2[e]
            out = out + cw[:, None] * y
        z = out + x
        mu = jnp.mean(z, axis=-1, keepdims=True)
        var = jnp.mean(jnp.square(z - mu), axis=-1, keepdims=True)
        z = (z - mu) * jax.lax.rsqrt(var + LN_EPS) * ln_w + ln_b
        return z.reshape(bsz, seqlen, h)
    x = x + _L0_xattn_ref(_layernorm(x, axis=-1), ctx_1024, ctx_1024, L0_xattn_wq, L0_xattn_bq, L0_xattn_wk, L0_xattn_bk, L0_xattn_wv, L0_xattn_bv, L0_xattn_wo, L0_xattn_bo)
    x = x + _L0_ffn_ref(_layernorm(x, axis=-1), L0_ffn_W_in, L0_ffn_b_in, L0_ffn_W_out, L0_ffn_b_out)
    x = x + _L1_xattn_ref(_layernorm(x, axis=-1), ctx_1024, L1_xattn_wq, L1_xattn_bq, L1_xattn_wk, L1_xattn_bk, L1_xattn_wv, L1_xattn_bv, L1_xattn_wo, L1_xattn_bo)
    x = x + _L1_ffn_ref(_layernorm(x, axis=-1), L1_ffn_gate_w, L1_ffn_gate_b, L1_ffn_w1, L1_ffn_b1, L1_ffn_w2, L1_ffn_b2, L1_ffn_ws1, L1_ffn_bs1, L1_ffn_ws2, L1_ffn_bs2)
    x = x + _L2_xattn_ref(_layernorm(x, axis=-1), ctx_1024, ctx_1024, L2_xattn_Wq_w, L2_xattn_Wq_b, L2_xattn_Wk_w, L2_xattn_Wk_b, L2_xattn_Wv_w, L2_xattn_Wv_b, L2_xattn_Wo_w, L2_xattn_Wo_b, mask_1x1xSxS2_ik0)
    x = x + _L2_ffn_ref(_layernorm(x, axis=-1), L2_ffn_ln1_scale, L2_ffn_ln1_shift, L2_ffn_wq, L2_ffn_wk, L2_ffn_wv, L2_ffn_wo, L2_ffn_bo, L2_ffn_ln2_scale, L2_ffn_ln2_shift, L2_ffn_gate_w, L2_ffn_w1, L2_ffn_w2, L2_ffn_w3)
    x = x + _L3_xattn_ref(ctx_1024, ctx_1024, _layernorm(x, axis=-1), mask_Bx1x1xS2_if1, L3_xattn_Wv, L3_xattn_Wk, L3_xattn_Wq, L3_xattn_Wo, L3_xattn_bo)
    x = x + _L3_ffn_ref(_layernorm(x, axis=-1), L3_ffn_Wr, L3_ffn_br, L3_ffn_W1, L3_ffn_b1, L3_ffn_W2, L3_ffn_b2, L3_ffn_ln_w, L3_ffn_ln_b)
    return x

_drawn_inputs = setup_inputs


def setup_inputs(seed=0):
    import zlib

    import numpy as np

    out = dict(_drawn_inputs(seed))
    spreads = {'L0_ffn_b_in': (0.0, 0.1),
     'L0_ffn_b_out': (0.0, 0.1),
     'L1_xattn_bq': (0.0, 0.342),
     'L1_xattn_bk': (0.0, 0.8),
     'L1_xattn_bv': (0.0, 0.1),
     'L1_xattn_bo': (0.0, 0.1),
     'L1_ffn_gate_b': (0.0, 0.1),
     'L1_ffn_b1': (0.0, 0.433),
     'L1_ffn_b2': (0.0, 0.1),
     'L1_ffn_bs1': (0.0, 0.347),
     'L1_ffn_bs2': (0.0, 0.1),
     'L2_ffn_ln1_scale': (1.0, 0.2),
     'L2_ffn_ln1_shift': (0.0, 0.1),
     'L2_ffn_bo': (0.0, 0.1),
     'L2_ffn_ln2_scale': (1.0, 0.2),
     'L2_ffn_ln2_shift': (0.0, 0.1),
     'L3_xattn_bo': (0.0, 0.1),
     'L3_ffn_br': (0.0, 0.551),
     'L3_ffn_b1': (0.0, 0.8),
     'L3_ffn_b2': (0.0, 0.452),
     'L3_ffn_ln_w': (1.0, 0.2),
     'L3_ffn_ln_b': (0.0, 0.324)}
    factors = {'L0_xattn_bq': 8.0,
     'L0_xattn_bk': 8.0,
     'L0_xattn_bv': 3.489,
     'L0_xattn_bo': 3.671,
     'L2_xattn_Wq_b': 2.8,
     'L2_xattn_Wk_b': 8.0,
     'L3_ffn_Wr': 3.294,
     'L3_ffn_W1': 5.598,
     'L3_ffn_W2': 5.047}
    for name, (base, spread) in spreads.items():
        noise = np.random.default_rng([zlib.crc32(name.encode()), seed]).standard_normal(out[name].shape)
        drawn = base * np.exp(spread * noise) if base else spread * noise
        out[name] = jnp.asarray(drawn.astype(out[name].dtype))
    for name, factor in factors.items():
        out[name] = (out[name] * factor).astype(out[name].dtype)
    return out
```

```python
from contextlib import ExitStack

import concourse.bass as bass
from concourse import mybir

F32 = mybir.dt.float32
F32R = mybir.dt.float32r
BF16 = mybir.dt.bfloat16
I32 = mybir.dt.int32
U32 = mybir.dt.uint32
ALU = mybir.AluOpType
ACT = mybir.ActivationFunctionType
AX = mybir.AxisListType

B, S, D, SK = 8, 256, 128, 512
H, DH = 16, 8
NT = B * S // 128
QT = S // 128
HG = 4
NG = H // HG
TB = 4
NBLK = NT // TB
E = 8
MASKED = -float(2 ** 100)
ROUND = 1.5 * 2 ** 23
A8, A16 = 127.0, 32767.0
EPS = 1e-5

ATT = {
    "A0": dict(nk=SK, scale=DH ** -0.5, mask=None),
    "A1": dict(nk=SK, scale=DH ** -0.5, mask=None),
    "A2": dict(nk=SK, scale=DH ** -0.5, mask="full"),
    "AS": dict(nk=S, scale=DH ** -0.5, mask="causal"),
    "A3": dict(nk=SK, scale=D ** -0.5, mask="keys"),
}
PHASES = ["A0", "F0", "A1", "F1", "A2", "AS", "F2", "A3", "F3"]


def att_counts(ph):
    nkt = ATT[ph]["nk"] // 128
    stats = 2 if ph == "AS" else 1
    return dict(
        s_ready=8 * NG, st_ready=nkt * NG, av_ready=nkt * NG, mt_ready=NG, xt_ready=1, q_ready=1,
        k_ready=1, v_ready=1, avt_ready=2, ont_ready=1, o_ready=1,
        exp_done=nkt * NG, mt_read=NG, xt_read=1, q_read=1, k_read=1,
        max_done=8 * NG, msplit=NG, av_read=NG, v_read=1, on_done=2, ont_read=1, x_new=1,
        var_done=stats, xn_done=1, qh_done=1, kh_done=1, ql_done=1,
        rstd_done=stats, qlm_done=1, mask_conv=1 if ph == "A3" else 0,
    )


def ffn_counts(ph):
    if ph == "F0":
        return dict(var_done=1, rstd_done=1, xn_done=1, fxt_ready=1, fxt_read=1, h_ready=4, h_done=4,
                    hq_done=1, y_ready=1, x_new=1)
    shared = ph == "F1"
    n = E + (ph != "F2")
    ne = E + shared
    return dict(
        var_done=1, rstd_done=1, xn_done=1, fxt_ready=1,
        fxt_read=1, lg_ready=1, lg_read=1, th_done=1, comb_done=1,
        h_ready=4 * ne, h_done=4 * ne if ph != "F2" else 2 * ne, g_done=2 * ne if ph == "F2" else 0,
        y_ready=n, acc_done=n, ct_ready=int(ph != "F2"), ct_read=int(ph != "F2"), x_new=1,
        var2_done=int(ph == "F3"), rstd2_done=int(ph == "F3"),
    )


N_LOADED = 9 + 9 + 5 + 4 + 3 + 2 + 2 + 1 + 2
W_PARTS = {"F0": 3, "F1": 15, "F2": 10, "F3": 11}
LINKS = {'A0': 36, 'A1': 36, 'A2': 36, 'AS': 42, 'A3': 36, 'F1': 8, 'F2': 9, 'F3': 14}


class Counts:

    def __init__(self):
        self.credit = {"acc_done": 2, "g_done": 2, "y_ready": 2, "h_done": 4, "h_ready": 1, "fxt_ready": 1,
                       "fxt_read": 1}
        self.per, self.base, total = {}, {}, dict(self.credit)
        for ph in PHASES:
            self.per[ph] = att_counts(ph) if ph in ATT else ffn_counts(ph)
            self.base[ph] = dict(total)
            for name, n in self.per[ph].items():
                total[name] = total.get(name, 0) + n * (B if ph in ATT else NBLK)
        self.names = sorted(total)

    def start(self, name, ph):
        return self.base[ph].get(name, 0)

    def at(self, name, ph, b, k=0):
        b = b.b if isinstance(b, Batch) else b
        return self.base[ph].get(name, 0) + b * self.per[ph][name] + (k + 1)


class Batch:

    def __init__(self, i, off):
        self.i, self.off = i, off
        self.b, self.half, self.parity = i * 2 + off, i + off // 2, off % 2
        self.known = isinstance(i, int)

    def __add__(self, n):
        return Batch(self.i, self.off + n)


class Links:

    def __init__(self, eng, sem):
        self.eng, self.sem, self.n, self.loop = eng, sem, 0, None

    def __call__(self, ins, after=None):
        self.n += 1
        ins.then_inc(self.sem, 1)
        value = self.n if self.loop is None else self.loop[0] * self.loop[1] + self.n
        self.eng.wait_ge(self.sem, value)
        if after:
            after(self.eng)

    def enter(self, i, per):
        self.loop, self.begin = (i, per), self.n

    def leave(self, turns):
        i, per = self.loop
        assert self.n - self.begin == per, ("links in the loop", self.n - self.begin, per)
        self.loop, self.n = None, self.begin + turns * per


def batches(eng, body, links=None, per=0):
    body(Batch(0, 0), True, False)
    with eng.Fori(0, B // 2 - 1) as i:
        if links:
            links.enter(i, per)
        body(Batch(i, 1), False, False)
        body(Batch(i, 2), False, False)
    if links:
        links.leave(B // 2 - 1)
    body(Batch(B // 2 - 1, 1), False, True)


def blocks(eng, n, body, links=None, per=0):
    with eng.Fori(0, n) as i:
        if links:
            links.enter(i, per)
        body(i)
    if links:
        links.leave(n)


def build(nc, t, out):
    cnt = Counts()
    with ExitStack() as ctx:
        def sb(name, shape, dt=F32):
            return ctx.enter_context(nc.sbuf_tensor(name, shape, dt))

        def sem(name):
            return ctx.enter_context(nc.semaphore(name))

        sig = {n: sem(n) for n in cnt.names}

        x_tok = sb("x_tok", [128, NT, D])
        y_tok = sb("y_tok", [128, NT, D])
        ctxT = sb("ctxT", [128, 2, SK])
        xn = sb("xn", [128, QT, D])
        xnT = sb("xnT", [128, S])
        qf = sb("qf", [128, S])
        q_hi = sb("q_hi", [128, S], F32R)
        q_lo = sb("q_lo", [128, S], F32R)
        q_him = sb("q_him", [128, HG, S], F32R)
        q_lom = sb("q_lom", [128, HG, S], F32R)
        kf = sb("kf", [128, SK])
        k_hi = sb("k_hi", [128, SK], F32R)
        k_lo = sb("k_lo", [128, SK], F32R)
        qz = [sb(f"qz{p}", [128, NG, HG, S], F32R) for p in range(2)]
        kst = [sb(f"kst{p}", [128, NG, SK], F32R) for p in range(2)]
        vaug = [sb(f"vaug{p}", [128, 4, H, 32]) for p in range(2)]
        prob = sb("prob", [128, 2, 4, HG * S])
        avs = sb("avs", [128, NG, S])
        o_n = sb("o_n", [128, QT, D])
        o_nT = sb("o_nT", [128, S])
        mx = sb("mx", [128, 2, 8])
        mrest = sb("mrest", [128, 8])
        mpart = sb("mpart", [128, 2, 2, 128], BF16)
        rsum = sb("rsum", [128, H])
        junk = sb("junk", [128, 2, SK], BF16)
        st6 = sb("st6", [128, TB, 6])
        mv = sb("mv", [128, TB, 2])
        st6b = sb("st6b", [128, TB, 6])
        mvb = sb("mvb", [128, TB, 2])
        veps = sb("veps", [128, 2, TB])
        rstd = sb("rstd", [128, 2, TB])
        neg_half = sb("neg_half", [128, TB])
        mask_q = sb("mask_q", [128, 2, SK])
        mask_T = sb("mask_T", [128, 4, S], BF16)
        caus_q = sb("caus_q", [128, 2, S])
        caus_T = sb("caus_T", [128, 2, S], BF16)
        mrow_i = caus_q[:, :, :].rearrange("p c k -> p (c k)").bitcast(I32)
        mrow = mask_q
        mcol_i = sb("mcol_i", [128, 4], I32)
        mcol = sb("mcol", [128, 2, 4])
        ident = sb("ident", [128, 128])
        ident_b = sb("ident_b", [128, 128], BF16)
        headm = sb("headm", [128, HG])
        ones_row = sb("ones_row", [1, 128])
        iota_e = sb("iota_e", [128, E])
        w_att = {a: sb(f"w_{a}", [128, 4, 128]) for a in ("A0", "A1", "A3")}
        w_att |= {"A2": w_att["A0"], "AS": w_att["A1"]}
        b_att = {a: sb(f"b_{a}", [128, 2]) for a in ATT}
        bv_att = {a: sb(f"bv_{a}", [128, D]) for a in ("A0", "A1", "A2")}
        bo_att = {a: sb(f"bo_{a}", [1, D]) for a in ATT}
        ln_cols = sb("ln_cols", [128, 4])
        w_ffn = sb("w_ffn", [128, 9 * 1024])
        xf = avs[:, 0:2, :].rearrange("p g (q d) -> p (g q) d", d=D)
        acc = avs[:, 2:4, :].rearrange("p g (q d) -> p (g q) d", d=D)
        xfT = ctxT[:, 1, :]
        gate = sb("gate", [128, 3, E])
        gate_bb = sb("gate_bb", [128, 2, E])
        lg = sb("lg", [128, TB, E])
        top = sb("top", [128, TB, E])
        topi = sb("topi", [128, TB, E], U32)
        topf = sb("topf", [128, TB, 2])
        dlt = sb("dlt", [128, TB])
        th = sb("th", [128, TB])
        w2 = sb("w2", [128, 2, TB])
        eq = sb("eq", [128, 2, TB, E])
        comb = sb("comb", [128, TB, E + 1])
        combT = kf[0:E + 1, :]
        b1c = sb("b1c", [128, 9 * 4])
        b2r = sb("b2r", [E + 1, D])
        lnw = sb("lnw", [128, 2, D])
        amx = sb("amx", [128, 8])
        aall = sb("aall", [128, 8])
        awq = w_ffn[:, 5120:5632]
        awo = sb("awo", [128, 2, 4])
        svec = sb("svec", [128, 8])
        boutb = sb("boutb", [128, D])

        ps_s = [ctx.enter_context(nc.psum_tensor(f"ps_s{i}", [128, 512], F32)) for i in range(2)]
        ps_t = [ctx.enter_context(nc.psum_tensor(f"ps_t{i}", [128, 1024], F32)) for i in range(2)]
        ps_av = ctx.enter_context(nc.psum_tensor("ps_av", [128, 512], F32))
        ps_m = ctx.enter_context(nc.psum_tensor("ps_m", [128, 512], F32))
        ps_mb = ps_m[:, :].bitcast(BF16)

        ctx_in = [sem(f"ctx_in{p}") for p in range(2)]
        q_stacked = [sem(f"q_stacked{p}") for p in range(2)]
        k_stacked = [sem(f"k_stacked{p}") for p in range(2)]
        mask_in = sem("mask_in")
        loaded = sem("loaded")
        bd_loaded = sem("bd_loaded")
        watt_in = {a: sem(f"watt_in_{a}") for a in ("A2", "AS")}
        w_in = {ph: sem(f"w_in_{ph}") for ph in ("F0", "F1", "F2", "F3")}
        setup_pool = sem("setup_pool")
        pool_chain = sem("pool_chain")
        dve_chain = sem("dve_chain")
        col_absmax = sem("col_absmax")
        w_cols = sem("w_cols")
        max_given = sem("max_given")
        max_all = sem("max_all")
        svec_done = sem("svec_done")
        bias_scaled = sem("bias_scaled")
        x_loaded = sem("x_loaded")
        stored = sem("stored")
        apart_waits = sem("apart_waits")

        ATTS = [p for p in PHASES if p in ATT]

        def stacked(ph, bt):
            return 16 * 3 * NG * (ATTS.index(ph) * (B // 2) + bt.half + 1)

        def context_in(ph, bt):
            n = sum(a != "AS" for a in ATTS[:ATTS.index(ph)])
            return 16 * (n * (B // 2) + bt.half + 1)

        def wait(eng, name, value):
            if not (isinstance(value, int) and value <= 0):
                eng.wait_ge(sig[name], value)

        def apart(eng):
            eng.sem_inc(apart_waits, 1)

        def slots(ph):
            s = {(g, 1): "MT" for g in range(NG)}
            s |= {(0, 2): "XT", (0, 3): "Q", (1, 2): "AVT0", (1, 3): "AVT1", (2, 0): "ONT", (2, 2): "V", (2, 3): "O"}
            s[(1, 0) if ph == "AS" else (0, 0)] = "K"
            return s

        def later(bt, g, n):
            return bt + (g + n) // NG, (g + n) % NG

        def kt_of(ph, k):
            if ATT[ph]["nk"] == SK:
                return k
            return k // 2 if k % 2 == 0 else None

        block = ctx.enter_context(nc.Block())

        @block.sync
        def _(sp):
            sp.dma_start(x_tok[:, :, :], t["x"].rearrange("b (q p) d -> p (b q) d", p=128)).then_inc(x_loaded, 16)
            for a in ATT:
                for i, w in enumerate("qkvo"):
                    if a in ("A0", "A1") or a == "A3" and w == "o":
                        sp.dma_start(w_att[a][:, i, :], t[f"{a}_{w}"]).then_inc(loaded, 16)
                if a in bv_att:
                    for i, w in enumerate("qk"):
                        sp.dma_start(b_att[a][:, i:i + 1], t[f"{a}_b{w}"].rearrange("(d o) -> d o", o=1)).then_inc(loaded, 16)
                    sp.dma_start(bv_att[a][:, :], t[f"{a}_bv"].rearrange("(o d) -> o d", o=1).to_broadcast([128, D])).then_inc(loaded, 16)
                sp.dma_start(bo_att[a][:, :], t[f"{a}_bo"].rearrange("(o d) -> o d", o=1)).then_inc(loaded, 16)
            for i, w in enumerate(("ln1_scale", "ln1_shift", "ln2_scale", "ln2_shift")):
                sp.dma_start(ln_cols[:, i:i + 1], t[w].rearrange("(d o) -> d o", o=1)).then_inc(loaded, 16)
            for i, w in enumerate(("F1_gate", "F2_gate", "F3_gate")):
                sp.dma_start(gate[:, i, :], t[w]).then_inc(loaded, 16)
            for i, w in enumerate(("F1_gate_b", "F3_gate_b")):
                sp.dma_start(gate_bb[:, i, :], t[w].rearrange("(o e) -> o e", o=1).to_broadcast([128, E])).then_inc(loaded, 16)
            for i, w in enumerate(("ln_w", "ln_b")):
                sp.dma_start(lnw[:, i, :], t[w].rearrange("(o e) -> o e", o=1).to_broadcast([128, D])).then_inc(loaded, 16)
            sp.dma_start(boutb[:, :], t["F0_b2"].rearrange("(o e) -> o e", o=1).to_broadcast([128, D])).then_inc(loaded, 16)
            sp.dma_start(prob[:, 1, 0, :].bitcast(I32).rearrange("p (c k) -> p c k", c=2), t["mask_q"].rearrange("(c p) k -> p c k", p=128)).then_inc(loaded, 16)
            sp.dma_start(prob[:, 1, 1, :].bitcast(I32).rearrange("p (c k) -> p c k", c=4), t["mask_T"].rearrange("(c p) q -> p c q", p=128)).then_inc(loaded, 16)
            sp.wait_ge(setup_pool, 1)
            for i, w in enumerate("qkv"):
                for h in range(H):
                    sp.dma_start(w_att["A3"][DH * h:DH * h + DH, i, DH * h:DH * h + DH], t[f"A3_{w}"]).then_inc(bd_loaded, 16)

            def load_ffn(ph):
                wait(sp, "y_ready", cnt.start("y_ready", ph))
                wait(sp, "h_done", cnt.start("h_done", ph))
                done = w_in[ph]
                if ph == "F0":
                    sp.dma_start(w_ffn[:, 0:512], t["F0_w1"]).then_inc(done, 16)
                    sp.dma_start(w_ffn[:, 512:1024].rearrange("p (c d) -> p c d", c=4), t["F0_w2"].rearrange("(c p) d -> p c d", p=128)).then_inc(done, 16)
                    sp.dma_start(b1c[:, 0:4], t["F0_b1"]).then_inc(done, 16)
                if ph in ("F1", "F3"):
                    ne = 9 if ph == "F1" else 8
                    sp.dma_start(w_ffn[:, 0:4096].rearrange("p (e f) -> p e f", e=E), t[f"{ph}_w1"].rearrange("e d f -> d e f")).then_inc(done, 16)
                    for e in range(E):
                        sp.dma_start(w_ffn[:, 512 * (ne + e):512 * (ne + e + 1)].rearrange("p (c d) -> p c d", c=4), t[f"{ph}_w2"][e].rearrange("(c p) d -> p c d", p=128)).then_inc(done, 16)
                    sp.dma_start(b1c[:, 0:32], t[f"{ph}_b1"]).then_inc(done, 16)
                    sp.dma_start(b2r[0:E, :], t[f"{ph}_b2"]).then_inc(done, 16)
                if ph == "F1":
                    sp.dma_start(w_ffn[:, 4096:4608], t["F1_ws1"]).then_inc(done, 16)
                    sp.dma_start(w_ffn[:, 512 * 17:512 * 18].rearrange("p (c d) -> p c d", c=4), t["F1_ws2"].rearrange("(c p) d -> p c d", p=128)).then_inc(done, 16)
                    sp.dma_start(b1c[:, 32:36], t["F1_bs1"]).then_inc(done, 16)
                    sp.dma_start(b2r[E:E + 1, :], t["F1_bs2"].rearrange("(o d) -> o d", o=1)).then_inc(done, 16)
                if ph == "F2":
                    for i, w in enumerate(("F2_w1", "F2_w2")):
                        sp.dma_start(w_ffn[:, 2048 * i:2048 * (i + 1)].rearrange("p (e f) -> p e f", e=E), t[w].rearrange("e d f -> d e f")).then_inc(done, 16)
                    for e in range(E):
                        sp.dma_start(w_ffn[:, 4096 + 256 * e:4096 + 256 * (e + 1)].rearrange("p (c d) -> p c d", c=2), t["F2_w3"][e].rearrange("(c p) d -> p c d", p=128)).then_inc(done, 16)

            def load_context(ph, bt):
                if ph == "AS":
                    return
                p = bt.parity
                sp.dma_start(ctxT[:, p, :], t["ctxT"][bass.ds(bt.b, 1)].rearrange("o d k -> d (o k)")).then_inc(ctx_in[p], 16)
                if ph == "A3":
                    sp.dma_start(mrow_i[:, :], t["mask_k"][bass.ds(bt.b, 1)].to_broadcast([128, SK])).then_inc(mask_in, 16)
                    sp.dma_start(mcol_i[:, :], t["mask_kT"][bass.ds(bt.b, 1)].rearrange("o p c -> p (o c)")).then_inc(mask_in, 16)

            def stack_k(ph, bt):
                p, nk = bt.parity, ATT[ph]["nk"]
                wait(sp, "kh_done", cnt.at("kh_done", ph, bt))
                for blk, src in enumerate((k_hi, k_lo, k_hi)):
                    for g in range(NG):
                        sp.dma_start(kst[p][32 * blk:32 * blk + 32, g, 0:nk].bitcast(F32), src[32 * g:32 * g + 32, 0:nk].bitcast(F32)).then_inc(k_stacked[p], 16)

            def stack_q(ph, bt):
                p = bt.parity
                wait(sp, "qh_done", cnt.at("qh_done", ph, bt))
                for blk in range(2):
                    for g in range(NG):
                        sp.dma_start(qz[p][32 * blk:32 * blk + 32, g, :, :].bitcast(F32), q_him[32 * g:32 * g + 32, :, :].bitcast(F32)).then_inc(q_stacked[p], 16)
                wait(sp, "qlm_done", cnt.at("qlm_done", ph, bt))
                for g in range(NG):
                    sp.dma_start(qz[p][64:96, g, :, :].bitcast(F32), q_lom[32 * g:32 * g + 32, :, :].bitcast(F32)).then_inc(q_stacked[p], 16)

            def stack(ph, bt, released):
                wait(sp, "st_ready", released)
                apart(sp)
                for f in ((stack_q, stack_k) if ph == "AS" else (stack_k, stack_q)):
                    f(ph, bt)

            for ph in PHASES:
                if ph not in ATT:
                    continue
                load_ffn({"A0": "F0", "A1": "F1", "A2": "F2", "AS": None, "A3": "F3"}[ph]) if ph != "AS" else None
                units_before = cnt.start("st_ready", ph)
                wait(sp, "k_ready", cnt.start("k_ready", ph))
                wait(sp, "v_ready", cnt.start("v_ready", ph))
                if ph == "A3":
                    wait(sp, "max_done", cnt.start("max_done", ph))
                if ph in ("A1", "A2"):
                    wait(sp, "o_ready", cnt.start("o_ready", ph))
                    a = {"A1": "A2", "A2": "AS"}[ph]
                    for i, w in enumerate("qkvo"):
                        sp.dma_start(w_att[a][:, i, :], t[f"{a}_{w}"]).then_inc(watt_in[a], 16)
                load_context(ph, Batch(0, 0))
                stack(ph, Batch(0, 0), units_before)

                def body(bt, first, last):
                    if last:
                        return
                    if not first:
                        wait(sp, "v_ready", cnt.at("v_ready", ph, bt + -1))
                        apart(sp)
                    if ph == "A3":
                        wait(sp, "mask_conv", cnt.at("mask_conv", ph, bt))
                    load_context(ph, bt + 1)
                    stack(ph, bt + 1, units_before if first else cnt.at("st_ready", ph, bt + -1, cnt.per[ph]["st_ready"] - 1))

                batches(sp, body)
            out_tiles = out.rearrange("b (q p) d -> p (b q) d", p=128)
            with sp.Fori(0, NBLK) as blk:
                sp.wait_ge(sig["x_new"], cnt.at("x_new", "F3", blk))
                sp.dma_start(out_tiles[:, bass.ds(blk * TB, TB), :], x_tok[:, bass.ds(blk * TB, TB), :]).then_inc(stored, 16)
            sp.wait_ge(stored, 16 * NBLK)

        @block.gpsimd
        def _(pool):
            link = Links(pool, pool_chain)

            pool.memset(w_att["A3"][:, 0:3, :], 0.0).then_inc(setup_pool, 1)
            link(pool.memset(ident[:, :], 0.0))
            link(pool.affine_select(out=ident[:, :], in_=ident[:, :], compare_op=ALU.not_equal, fill=1.0, base=0, pattern=[[-1, 128]], channel_multiplier=1))
            link(pool.memset(ident_b[:, :], 0.0))
            link(pool.affine_select(out=ident_b[:, :], in_=ident_b[:, :], compare_op=ALU.not_equal, fill=1.0, base=0, pattern=[[-1, 128]], channel_multiplier=1))
            link(pool.memset(headm[:, :], 1.0))
            for g in range(NG):
                part = headm[32 * g:32 * g + 32, :]
                link(pool.affine_select(out=part, in_=part, compare_op=ALU.is_ge, fill=0.0, base=0, pattern=[[-DH, HG]], channel_multiplier=1))
                link(pool.affine_select(out=part, in_=part, compare_op=ALU.is_ge, fill=0.0, base=DH - 1, pattern=[[DH, HG]], channel_multiplier=-1))
            link(pool.memset(caus_q[:, :, :], 0.0))
            link(pool.memset(caus_T[:, :, :], 0.0))
            link(pool.affine_select(out=caus_q[:, :, :], in_=caus_q[:, :, :], compare_op=ALU.is_ge, fill=MASKED, base=0, pattern=[[128, 2], [-1, S]], channel_multiplier=1))
            link(pool.affine_select(out=caus_T[:, :, :], in_=caus_T[:, :, :], compare_op=ALU.is_ge, fill=MASKED, base=0, pattern=[[-128, 2], [1, S]], channel_multiplier=-1))
            link(pool.iota(iota_e[:, :], pattern=[[1, E]], base=0, channel_multiplier=0, allow_small_or_imprecise_dtypes=True))
            link(pool.memset(neg_half[:, :], -0.5))
            link(pool.memset(ones_row[:, :], 1.0))
            for a in ("AS", "A3"):
                link(pool.memset(b_att[a][:, :], 0.0))
            for p in range(2):
                link(pool.memset(kst[p][96:128, :, :].bitcast(F32), 1.0))
                link(pool.memset(vaug[p][:, :, :, :], 0.0))
                link(pool.memset(vaug[p][:, :, :, DH:DH + 1], 1.0))
            link(pool.memset(mpart[:, :, :, :], 0.0))
            pool.memset(comb[:, :, E:E + 1], 1.0).then_inc(setup_pool, 1)

            def power(ph, b, k, n):
                pool.wait_ge(sig["var_done"], cnt.at("var_done", ph, b, k))
                pool.tensor_tensor(rstd[:, 0, 0:n], veps[:, 0, 0:n], neg_half[:, 0:n], ALU.pow).then_inc(sig["rstd_done"], 1)

            def power_of_result(blk):
                pool.wait_ge(sig["var2_done"], cnt.at("var2_done", "F3", blk))
                pool.tensor_tensor(rstd[:, 1, :], veps[:, 1, :], neg_half[:, :], ALU.pow).then_inc(sig["rstd2_done"], 1)

            def prepare(ph, bt):
                for k in range(cnt.per[ph]["var_done"]):
                    power(ph, bt, k, QT)
                if ph == "A3":
                    pool.wait_ge(mask_in, 32 * (bt.b + 1))
                    if not bt.known or bt.b >= 2:
                        pool.wait_ge(sig["max_done"], cnt.at("max_done", ph, bt + -2, 8 * NG - 1))
                        pool.wait_ge(sig["exp_done"], cnt.at("exp_done", ph, bt + -2, 4 * NG - 1))
                    apart(pool)
                    pool.tensor_scalar(mrow[:, bt.parity, :], mrow_i[:, :], 0.0, MASKED, ALU.is_equal, ALU.mult)
                    pool.tensor_scalar(mcol[:, bt.parity, :], mcol_i[:, :], 0.0, MASKED, ALU.is_equal, ALU.mult).then_inc(sig["mask_conv"], 1)
                pool.wait_ge(sig["ql_done"], cnt.at("ql_done", ph, bt))
                pool.tensor_tensor(q_lom[:, :, :], q_lo[:, :].bitcast(F32).rearrange("p (o s) -> p o s", o=1).to_broadcast([128, HG, S]),
                                   headm[:, :].rearrange("p (j o) -> p j o", o=1).to_broadcast([128, HG, S]), ALU.mult).then_inc(sig["qlm_done"], 1)

            for ph in PHASES:
                if ph in ATT:
                    if ph == "A3":
                        pool.wait_ge(sig["max_done"], cnt.start("max_done", ph))
                    prepare(ph, Batch(0, 0))
                    batches(pool, lambda bt, first, last: None if last else prepare(ph, bt + 1))
                elif ph == "F0":
                    pool.wait_ge(w_in["F0"], 48)
                    pool.partition_all_reduce(awq[:, :], w_ffn[:, 0:512], 128, bass.bass_isa.ReduceOp.absmax).then_inc(col_absmax, 1)
                    blocks(pool, NBLK, lambda blk: power("F0", blk, 0, TB))
                    for i in range(2):
                        pool.wait_ge(max_given, i + 1)
                        pool.partition_all_reduce(aall[:, i:i + 1], amx[:, i:i + 1], 128, bass.bass_isa.ReduceOp.absmax).then_inc(max_all, 1)
                else:
                    def body(blk):
                        power(ph, blk + 1, 0, TB)
                        if ph == "F3":
                            power_of_result(blk)
                    power(ph, 0, 0, TB)
                    blocks(pool, NBLK - 1, body)
                    if ph == "F3":
                        power_of_result(NBLK - 1)

        @block.scalar
        def _(act):
            def exponentials(ph, bt, g, kt):
                p, nkt = bt.parity, ATT[ph]["nk"] // 128
                wait(act, "st_ready", cnt.at("st_ready", ph, bt, nkt * g + kt))
                wait(act, "av_ready", cnt.at("av_ready", ph, bt, nkt * g + kt) - 2 * nkt)
                bias = mcol[:, p, kt:kt + 1] if ATT[ph]["mask"] == "keys" else 0.0
                nc.scalar.activation(prob[:, g % 2, kt, :], ps_t[kt % 2][:, :], ACT.Exp, bias=bias).then_inc(sig["exp_done"], 1)

            def misc(what, ph, bt):
                nk = ATT[ph]["nk"]
                if what == "XT":
                    wait(act, "xt_ready", cnt.at("xt_ready", ph, bt))
                    wait(act, "v_ready", cnt.at("v_ready", ph, bt) - 1)
                    wait(act, "q_ready", cnt.at("q_ready", ph, bt) - 1)
                    if ph == "AS":
                        nc.scalar.activation(xnT[:, :], ps_m[:, 0:S], ACT.Identity, bias=ln_cols[:, 1:2],
                                             scale=ln_cols[:, 0:1]).then_inc(sig["xt_read"], 1)
                    else:
                        nc.scalar.activation(xnT[:, :], ps_m[:, 0:S], ACT.Copy).then_inc(sig["xt_read"], 1)
                elif what == "Q":
                    wait(act, "q_ready", cnt.at("q_ready", ph, bt))
                    wait(act, "ql_done", cnt.at("ql_done", ph, bt) - 1)
                    nc.scalar.activation(qf[:, :], ps_m[:, 0:S], ACT.Identity, bias=b_att[ph][:, 0:1],
                                         scale=ATT[ph]["scale"]).then_inc(sig["q_read"], 1)
                elif what == "K":
                    wait(act, "k_ready", cnt.at("k_ready", ph, bt))
                    wait(act, "kh_done", cnt.at("kh_done", ph, bt) - 1)
                    nc.scalar.activation(kf[:, 0:nk], ps_m[:, 0:nk], ACT.Identity, bias=b_att[ph][:, 1:2]).then_inc(sig["k_read"], 1)

            def maxima_T(ph, bt, g):
                wait(act, "mt_ready", cnt.at("mt_ready", ph, bt, g))
                nc.scalar.activation(qz[bt.parity][96:128, g, :, :], ps_mb[96:128, :].rearrange("p (j s) -> p j s", j=HG),
                                     ACT.Copy).then_inc(sig["mt_read"], 1)

            def attention(ph):
                b0 = Batch(0, 0)
                for what in (("XT", "Q", "K") if ph == "AS" else ("K", "XT", "Q")):
                    misc(what, ph, b0)
                maxima_T(ph, b0, 0)
                table = slots(ph)

                def body(bt, first, last):
                    for g in range(NG):
                        nxt, g_nxt = later(bt, g, 1)
                        for k in range(4):
                            kt = kt_of(ph, k)
                            if kt is not None:
                                exponentials(ph, bt, g, kt)
                            what = table.get((g, k))
                            if what == "MT":
                                if not (last and g == 3):
                                    maxima_T(ph, nxt, g_nxt)
                            elif what in ("XT", "Q", "K") and not last:
                                misc(what, ph, bt + 1)

                batches(act, body)

            def read_block(ph, blk):
                wait(act, "fxt_ready", cnt.at("fxt_ready", ph, blk))
                wait(act, "h_ready", cnt.at("h_ready", ph, blk, -1))
                if ph == "F2":
                    nc.scalar.activation(xfT[:, :], ps_m[:, :], ACT.Identity, bias=ln_cols[:, 3:4],
                                         scale=ln_cols[:, 2:3]).then_inc(sig["fxt_read"], 1)
                else:
                    nc.scalar.activation(xfT[:, :], ps_m[:, :], ACT.Copy).then_inc(sig["fxt_read"], 1)

            def quantised_ffn():
                ph = "F0"
                hid = prob[:, :, :, :].rearrange("p a c s -> p (a c s)").rearrange("p (c s) -> p c s", c=4)
                act.wait_ge(max_all, 1)
                act.wait_ge(svec_done, 1)

                def body(blk):
                    for c in range(4):
                        wait(act, "h_ready", cnt.at("h_ready", ph, blk, c))
                        nc.scalar.activation(hid[:, c, bass.ds(blk * 512, 512)], ps_t[c // 2][:, 512 * (c % 2):512 * (c % 2 + 1)],
                                             ACT.Gelu, bias=b1c[:, c:c + 1], scale=svec[:, c:c + 1]).then_inc(sig["h_done"], 1)

                blocks(act, NBLK, body)

            def experts(ph):
                ne = 9 if ph == "F1" else 8

                def body(blk):
                    read_block(ph, blk)
                    for e in range(ne):
                        h = prob[:, e % 2, :, :].rearrange("p c s -> p (c s)")[:, 0:2048].rearrange("p (c s) -> p c s", c=4)
                        for c in range(2 if ph == "F2" else 4):
                            wait(act, "h_ready", cnt.at("h_ready", ph, blk, 4 * e + c))
                            if c == 0:
                                wait(act, "y_ready", cnt.at("y_ready", ph, blk, e) - 2)
                            src = ps_t[c // 2][:, 512 * (c % 2):512 * (c % 2 + 1)]
                            if ph == "F2":
                                nc.scalar.activation(h[:, 2 + c, :], src, ACT.Silu).then_inc(sig["h_done"], 1)
                            else:
                                nc.scalar.activation(h[:, c, :], src, ACT.Gelu, bias=b1c[:, 4 * e + c:4 * e + c + 1]).then_inc(sig["h_done"], 1)
                        if e == 0:
                            wait(act, "lg_read", cnt.at("lg_read", ph, blk))
                            nc.scalar.activation(th[:, :], dlt[:, :], ACT.Tanh, scale=0.5).then_inc(sig["th_done"], 1)

                act.wait_ge(w_in[ph], W_PARTS[ph] * 16)
                blocks(act, NBLK, body)

            act.wait_ge(loaded, 16 * N_LOADED)
            act.wait_ge(setup_pool, 2)
            act.wait_ge(bias_scaled, 3)
            for ph in PHASES:
                if ph in ATT:
                    attention(ph)
                elif ph == "F0":
                    quantised_ffn()
                else:
                    experts(ph)

        @block.tensor
        def _(pe):
            misc_reader = [None]

            def take_misc(reader, value):
                if misc_reader[0]:
                    wait(pe, *misc_reader[0])
                misc_reader[0] = (reader, value)

            def scores(ph, bt, g, i):
                p, nk, j, q = bt.parity, ATT[ph]["nk"], i // 2, i % 2
                if g == 0 and i == 0:
                    pe.wait_ge(q_stacked[p], stacked(ph, bt))
                    pe.wait_ge(k_stacked[p], stacked(ph, bt))
                wait(pe, "max_done", cnt.at("max_done", ph, bt, 8 * g + i) - 2)
                pe.matmul(ps_s[i % 2][:, 0:nk], qz[p][0:96, g, j, q * 128:(q + 1) * 128], kst[p][0:96, g, 0:nk],
                          start=True, stop=True).then_inc(sig["s_ready"], 1)

            def scores_T(ph, bt, g, kt):
                p, nkt, mask = bt.parity, ATT[ph]["nk"] // 128, ATT[ph]["mask"]
                if kt == 0:
                    wait(pe, "mt_read", cnt.at("mt_read", ph, bt, g))
                wait(pe, "exp_done", cnt.at("exp_done", ph, bt, nkt * g + kt) - 2)
                mask_T_ap = {"full": mask_T, "causal": caus_T}.get(mask)
                for n in range(2):
                    dst = ps_t[kt % 2][:, 512 * n:512 * (n + 1)]
                    mm = pe.matmul(dst, kst[p][:, g, kt * 128:(kt + 1) * 128], qz[p][:, g, 2 * n:2 * n + 2, :],
                                   start=True, stop=mask_T_ap is None)
                    if mask_T_ap is not None:
                        mm = pe.matmul(dst, ident_b[:, :], mask_T_ap[:, kt:kt + 1, :].to_broadcast([128, 2, S]),
                                       start=False, stop=True)
                mm.then_inc(sig["st_ready"], 1)

            def values(ph, bt, g, kt):
                p, nkt = bt.parity, ATT[ph]["nk"] // 128
                if kt == 0:
                    wait(pe, "av_read", cnt.at("av_read", ph, bt, g) - 1)
                    if g == 0:
                        wait(pe, "v_read", cnt.at("v_read", ph, bt))
                wait(pe, "exp_done", cnt.at("exp_done", ph, bt, nkt * g + kt))
                buf = g % 2
                for j in range(HG):
                    mm = pe.matmul(ps_av[32 * j:32 * j + 32, 0:S], vaug[p][:, kt, HG * g + j, :],
                                   prob[:, buf, kt, S * j:S * (j + 1)], start=(kt == 0), stop=(kt == nkt - 1))
                mm.then_inc(sig["av_ready"], 1)

            def maxima_T(ph, bt, g):
                take_misc("mt_read", cnt.at("mt_read", ph, bt, g))
                wait(pe, "msplit", cnt.at("msplit", ph, bt, g))
                for j in range(HG):
                    for q in range(QT):
                        mm = pe.transpose(ps_mb[96:128, S * j + 128 * q:S * j + 128 * (q + 1)],
                                          mpart[:, g % 2, q, 32 * j:32 * j + 32], ident_b[:, :])
                mm.then_inc(sig["mt_ready"], 1)

            def misc(what, ph, bt):
                nk, p = ATT[ph]["nk"], bt.parity
                w = w_att[ph]
                if what == "XT":
                    take_misc("xt_read", cnt.at("xt_read", ph, bt))
                    wait(pe, "xn_done", cnt.at("xn_done", ph, bt))
                    for q in range(QT):
                        mm = pe.transpose(ps_m[:, 128 * q:128 * (q + 1)], xn[:, q, :], ident[:, :])
                    mm.then_inc(sig["xt_ready"], 1)
                elif what == "Q":
                    take_misc("q_read", cnt.at("q_read", ph, bt))
                    wait(pe, "xt_read", cnt.at("xt_read", ph, bt))
                    pe.matmul(ps_m[:, 0:S], w[:, 0, :], xnT[:, :], start=True, stop=True).then_inc(sig["q_ready"], 1)
                elif what == "K":
                    take_misc("k_read", cnt.at("k_read", ph, bt))
                    if ph == "AS":
                        wait(pe, "xt_read", cnt.at("xt_read", ph, bt))
                    else:
                        pe.wait_ge(ctx_in[p], context_in(ph, bt))
                    pe.matmul(ps_m[:, 0:nk], w[:, 1, :], xnT[:, :] if ph == "AS" else ctxT[:, p, :],
                              start=True, stop=True).then_inc(sig["k_ready"], 1)
                elif what == "V":
                    take_misc("v_read", cnt.at("v_read", ph, bt))
                    for kt in range(nk // 128):
                        src = (xnT if ph == "AS" else ctxT[:, p, :])
                        mm = pe.matmul(ps_m[:, 128 * kt:128 * (kt + 1)], src[:, 128 * kt:128 * (kt + 1)], w[:, 2, :],
                                       start=True, stop=True)
                    mm.then_inc(sig["v_ready"], 1)
                elif what in ("AVT0", "AVT1"):
                    q = int(what[-1])
                    take_misc("on_done", cnt.at("on_done", ph, bt, q))
                    wait(pe, "av_read", cnt.at("av_read", ph, bt, NG - 1))
                    for g in range(NG):
                        mm = pe.transpose(ps_m[:, 128 * g:128 * (g + 1)], avs[:, g, 128 * q:128 * (q + 1)], ident[:, :])
                    mm.then_inc(sig["avt_ready"], 1)
                elif what == "ONT":
                    take_misc("ont_read", cnt.at("ont_read", ph, bt))
                    wait(pe, "on_done", cnt.at("on_done", ph, bt, 1))
                    for q in range(QT):
                        mm = pe.transpose(ps_m[:, 128 * q:128 * (q + 1)], o_n[:, q, :], ident[:, :])
                    mm.then_inc(sig["ont_ready"], 1)
                elif what == "O":
                    take_misc("x_new", cnt.at("x_new", ph, bt))
                    wait(pe, "ont_read", cnt.at("ont_read", ph, bt))
                    for q in range(QT):
                        dst = ps_m[:, 128 * q:128 * (q + 1)]
                        pe.matmul(dst, o_nT[:, 128 * q:128 * (q + 1)], w[:, 3, :], start=True, stop=False)
                        mm = pe.matmul(dst, ones_row[:, :], bo_att[ph][:, :], start=False, stop=True)
                    mm.then_inc(sig["o_ready"], 1)

            def attention(ph):
                wait(pe, "acc_done", cnt.start("acc_done", ph))
                wait(pe, "h_done", cnt.start("h_done", ph))
                wait(pe, "x_new", cnt.start("x_new", ph))
                misc_reader[0] = None
                if ph in watt_in:
                    pe.wait_ge(watt_in[ph], 64)
                b0 = Batch(0, 0)
                for what in (("XT", "Q", "K", "V") if ph == "AS" else ("K", "XT", "Q", "V")):
                    misc(what, ph, b0)
                for g in range(2):
                    for i in range(8):
                        scores(ph, b0, g, i)
                maxima_T(ph, b0, 0)
                table = slots(ph)

                def body(bt, first, last):
                    for g in range(NG):
                        ahead, g_ahead = later(bt, g, 2)
                        past, g_past = later(bt, g, -1)
                        nxt, g_nxt = later(bt, g, 1)
                        for k in range(4):
                            kt = kt_of(ph, k)
                            if not (last and g >= 2):
                                scores(ph, ahead, g_ahead, 2 * k)
                                scores(ph, ahead, g_ahead, 2 * k + 1)
                            if kt is not None:
                                scores_T(ph, bt, g, kt)
                                if not (first and g == 0):
                                    values(ph, past, g_past, kt)
                            what = table.get((g, k))
                            if what == "MT":
                                if not (last and g == 3):
                                    maxima_T(ph, nxt, g_nxt)
                            elif what in ("XT", "Q", "K", "V"):
                                if not last:
                                    misc(what, ph, bt + 1)
                            elif what and not first:
                                misc(what, ph, bt + -1)

                def loop_body(bt, first, last):
                    misc_reader[0] = ("mt_read", cnt.at("mt_read", ph, bt, 0))
                    body(bt, first, last)

                batches(pe, loop_body)
                end = Batch(B // 2 - 1, 1)
                for kt in range(ATT[ph]["nk"] // 128):
                    values(ph, end, NG - 1, kt)
                for what in ("AVT0", "AVT1", "ONT", "O"):
                    misc(what, ph, end)

            def turn_block(ph, blk):
                wait(pe, "xn_done", cnt.at("xn_done", ph, blk))
                for q in range(TB):
                    mm = pe.transpose(ps_m[:, 128 * q:128 * (q + 1)], xf[:, q, :], ident[:, :])
                mm.then_inc(sig["fxt_ready"], 1)

            def quantised_ffn():
                ph = "F0"
                pe.wait_ge(col_absmax, 1)
                for c in range(4):
                    mm = pe.matmul(ps_av[:, c:c + 1], awq[0:1, 128 * c:128 * (c + 1)], ones_row[:, 0:1], start=True, stop=True)
                mm.then_inc(w_cols, 1)

                def hidden(blk):
                    wait(pe, "fxt_read", cnt.at("fxt_read", ph, blk) - 1)
                    turn_block(ph, blk)
                    wait(pe, "fxt_read", cnt.at("fxt_read", ph, blk))
                    for c in range(4):
                        wait(pe, "h_done", cnt.at("h_done", ph, blk, c) - 4)
                        pe.matmul(ps_t[c // 2][:, 512 * (c % 2):512 * (c % 2 + 1)], w_ffn[:, 128 * c:128 * (c + 1)],
                                  xfT[:, :], start=True, stop=True).then_inc(sig["h_ready"], 1)

                blocks(pe, NBLK, hidden)

                def output(blk, p):
                    hq = w_ffn[:, 1024 + 2048 * p:1024 + 2048 * (p + 1)].rearrange("p (c s) -> p c s", c=4)
                    wait(pe, "hq_done", cnt.at("hq_done", ph, blk))
                    wait(pe, "x_new", cnt.at("x_new", ph, blk) - 2)
                    for q in range(TB):
                        for c in range(4):
                            mm = pe.matmul(ps_s[p][:, 128 * q:128 * (q + 1)], hq[:, c, 128 * q:128 * (q + 1)],
                                           w_ffn[:, 512 + 128 * c:512 + 128 * (c + 1)], start=(c == 0), stop=(c == 3))
                    mm.then_inc(sig["y_ready"], 1)

                with pe.Fori(0, NBLK, 2) as blk:
                    output(blk, 0)
                    output(blk + 1, 1)

            def experts(ph):
                ne = 9 if ph == "F1" else 8
                nc_h = 2 if ph == "F2" else 4
                gi = {"F1": 0, "F2": 1, "F3": 2}[ph]
                w2_at = {"F1": 4608, "F2": 4096, "F3": 4096}[ph]

                def first_product(blk, e):
                    for c in range(4):
                        if ph == "F2":
                            src = 2048 * (c // 2) + 256 * e + 128 * (c % 2)
                            free = ("h_done" if c < 2 else "g_done", 2 * e + c % 2, 2)
                        else:
                            src = 512 * e + 128 * c
                            free = ("h_done", 4 * e + c, 4)
                        wait(pe, free[0], cnt.at(free[0], ph, blk, free[1]) - free[2])
                        pe.matmul(ps_t[c // 2][:, 512 * (c % 2):512 * (c % 2 + 1)], w_ffn[:, src:src + 128],
                                  xfT[:, :], start=True, stop=True).then_inc(sig["h_ready"], 1)

                def second_product(blk, n, e):
                    wait(pe, "acc_done", cnt.at("acc_done", ph, blk, n) - (1 if n == 0 and ph != "F2" else 2))
                    bias = n == E
                    if bias:
                        wait(pe, "ct_read", cnt.at("ct_read", ph, blk))
                    if e is not None:
                        name, at = ("g_done", 2 * e + 1) if ph == "F2" else ("h_done", 4 * e + 3)
                        wait(pe, name, cnt.at(name, ph, blk, at))
                        h = prob[:, e % 2, :, :].rearrange("p c s -> p (c s)")[:, 0:2048].rearrange("p (c s) -> p c s", c=4)
                    for q in range(TB):
                        dst = ps_s[n % 2][:, 128 * q:128 * (q + 1)]
                        if bias:
                            mm = pe.matmul(dst, combT[:, 128 * q:128 * (q + 1)] if ph == "F1" else combT[0:E, 128 * q:128 * (q + 1)],
                                           b2r[:, :] if ph == "F1" else b2r[0:E, :], start=True, stop=e is None)
                        for c in range(nc_h if e is not None else 0):
                            w2c = w_ffn[:, w2_at + 128 * (nc_h * e + c):w2_at + 128 * (nc_h * e + c + 1)]
                            mm = pe.matmul(dst, h[:, c, 128 * q:128 * (q + 1)], w2c,
                                           start=(c == 0 and not bias), stop=(c == nc_h - 1))
                    mm.then_inc(sig["y_ready"], 1)

                def body(blk, last):
                    wait(pe, "fxt_read", cnt.at("fxt_read", ph, blk))
                    wait(pe, "lg_read", cnt.at("lg_read", ph, blk) - 1)
                    for q in range(TB):
                        mm = pe.matmul(ps_av[:, E * q:E * (q + 1)], xfT[:, 128 * q:128 * (q + 1)], gate[:, gi, :], start=True, stop=True)
                    mm.then_inc(sig["lg_ready"], 1)
                    first_product(blk, 0)
                    for e in range(ne):
                        if e + 1 < ne:
                            first_product(blk, e + 1)
                        if e == 5 and ph != "F2":
                            wait(pe, "comb_done", cnt.at("comb_done", ph, blk))
                            for q in range(TB):
                                mm = pe.transpose(ps_av[0:E + 1, 128 * q:128 * (q + 1)], comb[:, q, :], ident[:, :])
                            mm.then_inc(sig["ct_ready"], 1)
                        second_product(blk, e, e)
                        if e == 4 and not last:
                            turn_block(ph, blk + 1)
                    if ph == "F3":
                        second_product(blk, E, None)

                pe.wait_ge(w_in[ph], W_PARTS[ph] * 16)
                turn_block(ph, 0)
                blocks(pe, NBLK - 1, lambda blk: body(blk, False))
                body(NBLK - 1, True)

            pe.wait_ge(setup_pool, 2)
            pe.wait_ge(loaded, 16 * N_LOADED)
            pe.wait_ge(bd_loaded, 16 * 3 * H)
            for ph in PHASES:
                if ph in ATT:
                    attention(ph)
                elif ph == "F0":
                    quantised_ffn()
                else:
                    experts(ph)

        @block.vector
        def _(dve):
            link = Links(dve, dve_chain)

            def tile_of(buf, b, q):
                return buf[:, bass.ds(b * QT + q, 1), :].rearrange("p o d -> p (o d)")

            def variances(srcs, st, m, v, eps, done):
                apart(dve)
                for q, s in enumerate(srcs):
                    ins = dve.bn_stats(st[:, q, :], s)
                    if q == len(srcs) - 1:
                        link(ins, apart)
                for q in range(len(srcs)):
                    ins = dve.bn_aggr(m[:, q, :], st[:, q, :])
                    if q == len(srcs) - 1:
                        link(ins)
                dve.tensor_scalar(v, m[:, 0:len(srcs), 1], eps, None, ALU.add).then_inc(sig[done], 1)

            def normalise(srcs, dsts, m, r):
                for q, (s, d) in enumerate(zip(srcs, dsts)):
                    ins = dve.tensor_scalar(d, s, m[:, q, 0:1], r[:, q:q + 1], ALU.subtract, ALU.mult)
                return ins

            def ln_variances(ph, bt, k):
                src = y_tok if k else x_tok
                variances([tile_of(src, bt.b, q) for q in range(QT)], st6, mv, veps[:, 0, 0:QT], EPS, "var_done")

            def ln_normalise(ph, bt, k):
                wait(dve, "rstd_done", cnt.at("rstd_done", ph, bt, k))
                src = [tile_of(y_tok if k else x_tok, bt.b, q) for q in range(QT)]
                if ph == "AS" and k == 0:
                    link(normalise(src, [tile_of(y_tok, bt.b, q) for q in range(QT)], mv, rstd[:, 0, :]))
                else:
                    wait(dve, "xt_ready", cnt.at("xt_ready", ph, bt) - 1)
                    normalise(src, [xn[:, q, :] for q in range(QT)], mv, rstd[:, 0, :]).then_inc(sig["xn_done"], 1)

            def split_k(ph, bt):
                nk = ATT[ph]["nk"]
                wait(dve, "k_read", cnt.at("k_read", ph, bt))
                link(dve.tensor_copy(k_hi[:, 0:nk], kf[:, 0:nk]))
                dve.tensor_tensor(k_lo[:, 0:nk], kf[:, 0:nk], k_hi[:, 0:nk].bitcast(F32), ALU.subtract).then_inc(sig["kh_done"], 1)

            def split_q(ph, bt):
                wait(dve, "q_read", cnt.at("q_read", ph, bt))
                wait(dve, "qlm_done", cnt.at("qlm_done", ph, bt) - 1)
                link(dve.tensor_copy(q_hi[:, :], qf[:, :]))
                dve.tensor_tensor(q_lo[:, :], qf[:, :], q_hi[:, :].bitcast(F32), ALU.subtract).then_inc(sig["ql_done"], 1)
                for j in range(HG):
                    ins = dve.tensor_scalar(q_him[:, j, :], qf[:, :], headm[:, j:j + 1], None, ALU.mult)
                ins.then_inc(sig["qh_done"], 1)

            def lay_v(ph, bt):
                p, nkt = bt.parity, ATT[ph]["nk"] // 128
                wait(dve, "v_ready", cnt.at("v_ready", ph, bt))
                src = ps_m[:, 0:128 * nkt].rearrange("p (k h d) -> p k h d", k=nkt, h=H)
                dst = vaug[p][:, 0:nkt, :, 0:DH]
                if ph in bv_att:
                    bias = bv_att[ph][:, :].rearrange("p (o h d) -> p o h d", o=1, h=H).to_broadcast([128, nkt, H, DH])
                    dve.tensor_tensor(dst, src, bias, ALU.add).then_inc(sig["v_read"], 1)
                else:
                    dve.tensor_copy(dst, src).then_inc(sig["v_read"], 1)

            def maximum(ph, bt, g, i):
                nk, mask, q, buf = ATT[ph]["nk"], ATT[ph]["mask"], i % 2, g % 2
                wait(dve, "s_ready", cnt.at("s_ready", ph, bt, 8 * g + i))
                src = ps_s[i % 2][:, 0:nk]
                if mask is None:
                    dve.tensor_reduce(mx[:, buf, i:i + 1], src, AX.X, ALU.max).then_inc(sig["max_done"], 1)
                    return
                if mask == "keys":
                    if g == 0 and i == 0:
                        wait(dve, "mask_conv", cnt.at("mask_conv", ph, bt))
                    m = mrow[:, bt.parity, :]
                else:
                    m = (mask_q if mask == "full" else caus_q)[:, q, :]
                apart(dve)
                dve.tensor_tensor_reduce(junk[:, i % 2, 0:nk], src, m, 1.0, -3.0e38, ALU.add, ALU.max, mx[:, buf, i:i + 1])\
                   .then_inc(sig["max_done"], 1)

            def split_maxima(ph, bt, g):
                buf = g % 2
                wait(dve, "max_done", cnt.at("max_done", ph, bt, 8 * g + 7))
                wait(dve, "mt_ready", cnt.at("mt_ready", ph, bt, g) - 2)
                m = mx[:, buf, :].rearrange("p (j q) -> p q j", q=QT)
                rest = mrest[:, :].rearrange("p (j q) -> p q j", q=QT)
                part = [mpart[:, buf, :, c:c + 3 * (32 + DH) + 1:32 + DH] for c in range(3)]
                link(dve.tensor_scalar(part[0], m, -1.0, None, ALU.mult))
                link(dve.scalar_tensor_tensor(out=rest, in0=m, scalar=-1.0, in1=part[0], op0=ALU.mult, op1=ALU.subtract))
                link(dve.tensor_copy(part[1], rest))
                dve.tensor_tensor(part[2], rest, part[1], ALU.subtract).then_inc(sig["msplit"], 1)

            def read_values(ph, bt, g):
                wait(dve, "av_ready", cnt.at("av_ready", ph, bt, (g + 1) * (ATT[ph]["nk"] // 128) - 1))
                dve.tensor_copy(avs[:, g, :], ps_av[:, 0:S]).then_inc(sig["av_read"], 1)

            def misc(what, ph, bt):
                if what in ("AVT0", "AVT1"):
                    q = int(what[-1])
                    wait(dve, "avt_ready", cnt.at("avt_ready", ph, bt, q))
                    src = ps_m[:, :].rearrange("p (h r) -> p h r", h=H)
                    link(dve.reciprocal(rsum[:, :].rearrange("p (h o) -> p h o", o=1), src[:, :, DH:DH + 1]))
                    dve.tensor_tensor(o_n[:, q, :].rearrange("p (h d) -> p h d", h=H), src[:, :, 0:DH],
                                      rsum[:, :].rearrange("p (h o) -> p h o", o=1).to_broadcast([128, H, DH]), ALU.mult)\
                       .then_inc(sig["on_done"], 1)
                elif what == "ONT":
                    wait(dve, "ont_ready", cnt.at("ont_ready", ph, bt))
                    dve.tensor_copy(o_nT[:, :], ps_m[:, 0:S]).then_inc(sig["ont_read"], 1)
                elif what == "O":
                    wait(dve, "o_ready", cnt.at("o_ready", ph, bt))
                    dst = (y_tok if ph == "AS" else x_tok)[:, bass.ds(bt.b * QT, QT), :]
                    dve.tensor_tensor(dst, ps_m[:, 0:S].rearrange("p (q d) -> p q d", q=QT), dst, ALU.add).then_inc(sig["x_new"], 1)

            def attention(ph):
                n_ln = 2 if ph == "AS" else 1
                b0 = Batch(0, 0)
                wait(dve, "x_new", cnt.start("x_new", ph))
                if ph != "AS":
                    split_k(ph, b0)
                for k in range(n_ln):
                    ln_variances(ph, b0, k)
                    ln_normalise(ph, b0, k)
                split_q(ph, b0)
                if ph == "AS":
                    split_k(ph, b0)
                lay_v(ph, b0)
                for g in range(2):
                    for i in range(8):
                        maximum(ph, b0, g, i)
                    split_maxima(ph, b0, g)
                table = slots(ph)

                def body(bt, first, last):
                    for g in range(NG):
                        ahead, g_ahead = later(bt, g, 2)
                        past, g_past = later(bt, g, -2)
                        for k in range(4):
                            if k == 0 and not (first and g < 2):
                                read_values(ph, past, g_past)
                            if not last and (g, k) == (0, 0):
                                ln_variances(ph, bt + 1, 0)
                            if not last and (g, k) == (1, 0):
                                split_q(ph, bt + 1)
                            if not (last and g >= 2):
                                maximum(ph, ahead, g_ahead, 2 * k)
                            if not last and g == 0 and 1 <= k <= n_ln:
                                ln_normalise(ph, bt + 1, k - 1)
                                if k < n_ln:
                                    ln_variances(ph, bt + 1, k)
                            if not (last and g >= 2):
                                maximum(ph, ahead, g_ahead, 2 * k + 1)
                            if not last and (g, k) == ((1, 1) if ph == "AS" else (0, 1)):
                                split_k(ph, bt + 1)
                            what = table.get((g, k))
                            if what == "V" and not last:
                                lay_v(ph, bt + 1)
                            elif what in ("AVT0", "AVT1", "ONT", "O") and not first:
                                misc(what, ph, bt + -1)
                            if k == 3 and not (last and g >= 2):
                                split_maxima(ph, ahead, g_ahead)

                batches(dve, body, link, LINKS[ph])
                end = Batch(B // 2 - 1, 1)
                for g in (2, 3):
                    read_values(ph, end, g)
                for what in ("AVT0", "AVT1", "ONT", "O"):
                    misc(what, ph, end)

            def block_tiles(buf, blk):
                return [buf[:, bass.ds(blk * TB + q, 1), :].rearrange("p o d -> p (o d)") for q in range(TB)]

            def rounded(dst, src, scale):
                link(dve.tensor_scalar(dst, src, scale, -A16 - 1.0, ALU.mult, ALU.max))
                link(dve.tensor_scalar(dst, dst, A16, ROUND, ALU.min, ALU.add))
                return dve.tensor_scalar(dst, dst, ROUND, None, ALU.subtract)

            def quantised_ffn():
                ph = "F0"
                hid = prob[:, :, :, :].rearrange("p a c s -> p (a c s)").rearrange("p (c s) -> p c s", c=4)
                w1, w2w = w_ffn[:, 0:512], w_ffn[:, 512:1024]
                w2v = w2w.rearrange("p (c d) -> p c d", c=4)
                dve.wait_ge(w_in["F0"], 48)
                dve.wait_ge(col_absmax, 1)
                dve.wait_ge(w_cols, 1)
                link(dve.tensor_scalar(svec[:, 0:4], ps_av[:, 0:4], 1e-8, 1.0 / A8, ALU.max, ALU.mult))
                link(dve.tensor_scalar(awq[:, :], awq[:, :], 1e-8, None, ALU.max))
                link(dve.reciprocal(awq[:, :], awq[:, :]))
                link(dve.tensor_scalar(awq[:, :], awq[:, :], A8, None, ALU.mult))
                link(dve.tensor_tensor(w1, w1, awq[:, :], ALU.mult))
                link(dve.tensor_scalar(w1, w1, ROUND, ROUND, ALU.add, ALU.subtract))
                link(dve.tensor_scalar(w1, w1, -A8 - 1.0, A8, ALU.max, ALU.min))
                link(dve.tensor_reduce(awo[:, 0, :], w2v, AX.X, ALU.max, apply_absolute_value=True))
                link(dve.tensor_scalar(awo[:, 0, :], awo[:, 0, :], 1e-8, None, ALU.max))
                link(dve.reciprocal(awo[:, 1, :], awo[:, 0, :]))
                link(dve.tensor_scalar(awo[:, 1, :], awo[:, 1, :], A8, None, ALU.mult))
                link(dve.tensor_tensor(w2v, w2v, awo[:, 1, :].rearrange("p (c o) -> p c o", o=1).to_broadcast([128, 4, D]), ALU.mult))
                link(dve.tensor_scalar(w2w, w2w, ROUND, ROUND, ALU.add, ALU.subtract))
                link(dve.tensor_scalar(w2w, w2w, -A8 - 1.0, A8, ALU.max, ALU.min))
                link(dve.tensor_scalar(awo[:, 0, :], awo[:, 0, :], 1.0 / A8, None, ALU.mult))
                link(dve.tensor_tensor(w2v, w2v, awo[:, 0, :].rearrange("p (c o) -> p c o", o=1).to_broadcast([128, 4, D]), ALU.mult))
                link(dve.memset(amx[:, :], 0.0))

                def norm(blk):
                    variances(block_tiles(x_tok, blk), st6, mv, veps[:, 0, :], EPS, "var_done")
                    wait(dve, "rstd_done", cnt.at("rstd_done", ph, blk))
                    link(normalise(block_tiles(x_tok, blk), block_tiles(y_tok, blk), mv, rstd[:, 0, :]), apart)
                    link(dve.tensor_reduce(amx[:, 2:3], y_tok[:, bass.ds(blk * TB, TB), :], AX.XY, ALU.max, apply_absolute_value=True))
                    link(dve.tensor_tensor(amx[:, 0:1], amx[:, 0:1], amx[:, 2:3], ALU.max))

                blocks(dve, NBLK, norm, link, 5)
                dve.tensor_copy(amx[:, 3:4], amx[:, 0:1]).then_inc(max_given, 1)

                def step(i):
                    dve.wait_ge(max_all, i + 1)
                    link(dve.tensor_scalar(aall[:, 2:3], aall[:, i:i + 1], 1e-8, None, ALU.max))
                    link(dve.reciprocal(svec[:, 4:5], aall[:, 2:3]))
                    link(dve.tensor_scalar(svec[:, 4:5], svec[:, 4:5], A16, None, ALU.mult))
                    link(dve.tensor_scalar(svec[:, 5:6], aall[:, 2:3], 1.0 / A16, None, ALU.mult))

                step(0)
                dve.tensor_scalar(svec[:, 0:4], svec[:, 0:4], svec[:, 5:6], None, ALU.mult).then_inc(svec_done, 1)

                def quantise_x(blk):
                    wait(dve, "fxt_ready", cnt.at("fxt_ready", ph, blk) - 1)
                    rounded(xf[:, :, :], y_tok[:, bass.ds(blk * TB, TB), :], svec[:, 4:5]).then_inc(sig["xn_done"], 1)
                    wait(dve, "fxt_ready", cnt.at("fxt_ready", ph, blk))
                    wait(dve, "h_ready", cnt.at("h_ready", ph, blk, -1))
                    dve.tensor_copy(xfT[:, :], ps_m[:, :]).then_inc(sig["fxt_read"], 1)

                blocks(dve, NBLK, quantise_x, link, 2)
                wait(dve, "h_done", cnt.at("h_done", ph, NBLK - 1, 3))
                for c in range(4):
                    link(dve.tensor_reduce(amx[:, 4 + c:5 + c], hid[:, c, :], AX.X, ALU.max, apply_absolute_value=True))
                dve.tensor_reduce(amx[:, 1:2], amx[:, 4:8], AX.X, ALU.max).then_inc(max_given, 1)
                step(1)

                def quantise_h(blk, p):
                    hq = w_ffn[:, 1024 + 2048 * p:1024 + 2048 * (p + 1)].rearrange("p (c s) -> p c s", c=4)
                    wait(dve, "y_ready", cnt.at("y_ready", ph, blk) - 2)
                    rounded(hq, hid[:, :, bass.ds(blk * 512, 512)], svec[:, 4:5]).then_inc(sig["hq_done"], 1)

                def add(blk, p):
                    wait(dve, "y_ready", cnt.at("y_ready", ph, blk))
                    wait(dve, "x_new", cnt.at("x_new", ph, blk) - 1)
                    dst = x_tok[:, bass.ds(blk * TB, TB), :]
                    link(dve.scalar_tensor_tensor(out=acc[:, :, :], in0=ps_s[p][:, :].rearrange("p (q d) -> p q d", q=TB), scalar=svec[:, 5:6],
                                                  in1=boutb[:, :].rearrange("p (o d) -> p o d", o=1).to_broadcast([128, TB, D]),
                                                  op0=ALU.mult, op1=ALU.add))
                    dve.tensor_tensor(dst, dst, acc[:, :, :], ALU.add).then_inc(sig["x_new"], 1)

                with dve.Fori(0, NBLK // 2) as i:
                    link.enter(i, 6)
                    quantise_h(i * 2, 0)
                    quantise_h(i * 2 + 1, 1)
                    add(i * 2, 0)
                    add(i * 2 + 1, 1)
                link.leave(NBLK // 2)

            def experts(ph):
                ne = 9 if ph == "F1" else 8
                src_of = y_tok if ph == "F2" else x_tok
                gb = {"F1": 0, "F2": None, "F3": 1}[ph]

                def norm_variances(blk):
                    variances(block_tiles(src_of, blk), st6, mv, veps[:, 0, :], EPS, "var_done")

                def norm(blk):
                    wait(dve, "rstd_done", cnt.at("rstd_done", ph, blk))
                    wait(dve, "fxt_ready", cnt.at("fxt_ready", ph, blk) - 1)
                    ins = normalise(block_tiles(src_of, blk), [xf[:, q, :] for q in range(TB)], mv, rstd[:, 0, :])
                    ins.then_inc(sig["xn_done"], 1)
                    if ph == "F3":
                        wait(dve, "xn_done", cnt.at("xn_done", ph, blk))
                        dve.tensor_copy(y_tok[:, bass.ds(blk * TB, TB), :], xf[:, :, :])

                def gates(blk):
                    wait(dve, "lg_ready", cnt.at("lg_ready", ph, blk))
                    logits = ps_av[:, 0:TB * E].rearrange("p (q e) -> p q e", q=TB)
                    if gb is None:
                        link(dve.tensor_copy(lg[:, :, :], logits), apart)
                    else:
                        link(dve.tensor_tensor(lg[:, :, :], logits, gate_bb[:, gb:gb + 1, :].to_broadcast([128, TB, E]), ALU.add), apart)
                    for q in range(TB):
                        ins = dve.max(top[:, q, :], lg[:, q, :])
                    link(ins, apart)
                    for q in range(TB):
                        ins = dve.max_index(topi[:, q, :], top[:, q, :], lg[:, q, :])
                    link(ins)
                    dve.tensor_tensor(dlt[:, :], top[:, :, 1], top[:, :, 0], ALU.subtract).then_inc(sig["lg_read"], 1)
                    link(dve.tensor_copy(topf[:, :, :], topi[:, :, 0:2]))
                    for n in range(2):
                        ins = dve.tensor_tensor(eq[:, n, :, :], iota_e[:, :].rearrange("p (o e) -> p o e", o=1).to_broadcast([128, TB, E]),
                                                topf[:, :, n:n + 1].to_broadcast([128, TB, E]), ALU.is_equal)
                    wait(dve, "th_done", cnt.at("th_done", ph, blk))
                    dve.tensor_scalar(w2[:, 0, :], th[:, :], -0.5, 0.5, ALU.mult, ALU.add)
                    link(dve.tensor_scalar(w2[:, 1, :], th[:, :], 0.5, 0.5, ALU.mult, ALU.add))
                    for n in range(2):
                        ins = dve.tensor_tensor(eq[:, n, :, :], eq[:, n, :, :],
                                                w2[:, n, :].rearrange("p (q o) -> p q o", o=1).to_broadcast([128, TB, E]), ALU.mult)
                    link(ins)
                    dve.tensor_tensor(comb[:, :, 0:E], eq[:, 0, :, :], eq[:, 1, :, :], ALU.add).then_inc(sig["comb_done"], 1)
                    wait(dve, "comb_done", cnt.at("comb_done", ph, blk))

                def gated(blk, e):
                    h = prob[:, e % 2, :, :].rearrange("p c s -> p (c s)")[:, 0:2048].rearrange("p (c s) -> p c s", c=4)
                    wait(dve, "h_ready", cnt.at("h_ready", ph, blk, 4 * e + 3))
                    for c in range(2):
                        wait(dve, "h_done", cnt.at("h_done", ph, blk, 2 * e + c))
                        dve.tensor_tensor(h[:, c, :], ps_t[1][:, 512 * c:512 * (c + 1)], h[:, 2 + c, :], ALU.mult).then_inc(sig["g_done"], 1)

                def accumulate(blk, n):
                    wait(dve, "y_ready", cnt.at("y_ready", ph, blk, n))
                    if n:
                        wait(dve, "acc_done", cnt.at("acc_done", ph, blk, n) - 1)
                    if n == E:
                        dve.tensor_tensor(acc[:, :, :], ps_s[n % 2][:, :].rearrange("p (q d) -> p q d", q=TB), acc[:, :, :], ALU.add)\
                           .then_inc(sig["acc_done"], 1)
                        return
                    for q in range(TB):
                        src = ps_s[n % 2][:, 128 * q:128 * (q + 1)]
                        if n == 0:
                            ins = dve.tensor_scalar(acc[:, q, :], src, comb[:, q, 0:1], None, ALU.mult)
                        else:
                            ins = dve.scalar_tensor_tensor(out=acc[:, q, :], in0=src, scalar=comb[:, q, n:n + 1], in1=acc[:, q, :],
                                                           op0=ALU.mult, op1=ALU.add)
                    ins.then_inc(sig["acc_done"], 1)

                def result(blk, n_last):
                    dst = x_tok[:, bass.ds(blk * TB, TB), :]
                    inner = y_tok[:, bass.ds(blk * TB, TB), :]
                    wait(dve, "acc_done", cnt.at("acc_done", ph, blk, n_last))
                    if ph != "F1":
                        link(dve.tensor_tensor(acc[:, :, :], acc[:, :, :], inner, ALU.add))
                    if ph == "F3":
                        tiles = [acc[:, q, :] for q in range(TB)]
                        variances(tiles, st6b, mvb, veps[:, 1, :], 1e-12, "var2_done")
                        wait(dve, "rstd2_done", cnt.at("rstd2_done", ph, blk))
                        link(normalise(tiles, tiles, mvb, rstd[:, 1, :]))
                        for i, op in enumerate((ALU.mult, ALU.add)):
                            link(dve.tensor_tensor(acc[:, :, :], acc[:, :, :], lnw[:, i:i + 1, :].to_broadcast([128, TB, D]), op))
                    dve.tensor_tensor(dst, dst, acc[:, :, :], ALU.add).then_inc(sig["x_new"], 1)

                def body(blk, last):
                    gates(blk)
                    if ph == "F2":
                        gated(blk, 0)
                    for e in range(ne):
                        if ph == "F2" and e + 1 < ne:
                            gated(blk, e + 1)
                        if e == 5 and ph != "F2":
                            wait(dve, "ct_ready", cnt.at("ct_ready", ph, blk))
                            dve.tensor_copy(combT[:, :], ps_av[0:E + 1, :]).then_inc(sig["ct_read"], 1)
                        accumulate(blk, e)
                        if not last and e == 2:
                            norm_variances(blk + 1)
                        if not last and e == 3:
                            norm(blk + 1)
                    if ph == "F3":
                        accumulate(blk, E)
                    result(blk, E if ph != "F2" else E - 1)

                wait(dve, "x_new", cnt.start("x_new", ph))
                norm_variances(0)
                norm(0)
                blocks(dve, NBLK - 1, lambda blk: body(blk, False), link, LINKS[ph])
                body(NBLK - 1, True)

            dve.wait_ge(setup_pool, 2)
            dve.wait_ge(loaded, 16 * N_LOADED)
            for a in ("A0", "A1", "A2"):
                dve.tensor_scalar(b_att[a][:, 0:1], b_att[a][:, 0:1], ATT[a]["scale"], None, ALU.mult).then_inc(bias_scaled, 1)
            dve.tensor_scalar(mask_q[:, :, :], prob[:, 1, 0, :].bitcast(I32).rearrange("p (c k) -> p c k", c=2), 0.0, MASKED, ALU.is_equal, ALU.mult)
            link(dve.tensor_scalar(mask_T[:, :, :], prob[:, 1, 1, :].bitcast(I32).rearrange("p (c q) -> p c q", c=4), 0.0, MASKED, ALU.is_equal, ALU.mult))
            dve.memset(mrest[:, :], 0.0)
            dve.memset(junk[:, :, :], 0.0)
            for name, n in cnt.credit.items():
                dve.sem_inc(sig[name], n)
            dve.wait_ge(x_loaded, 16)
            for ph in PHASES:
                if ph in ATT:
                    attention(ph)
                elif ph == "F0":
                    quantised_ffn()
                else:
                    experts(ph)




def kernel(**inputs):
    import numpy as np

    import concourse.bacc as bacc
    from concourse import mybir as mb
    from concourse.bass_utils import run_bass_kernel_spmd

    a = {k: np.asarray(v) for k, v in inputs.items()}
    c = np.ascontiguousarray
    t = {
        "x": a["x"],
        "ctxT": c(a["ctx_1024"].transpose(0, 2, 1)),
        "mask_q": c(a["mask_1x1xSxS2_ik0"][0, 0]),
        "mask_T": c(a["mask_1x1xSxS2_ik0"][0, 0].T),
        "mask_k": c(a["mask_Bx1x1xS2_if1"][:, 0, 0]),
        "mask_kT": c(a["mask_Bx1x1xS2_if1"][:, 0, 0].reshape(8, 4, 128).transpose(0, 2, 1)),
        "ln1_scale": a["L2_ffn_ln1_scale"], "ln1_shift": a["L2_ffn_ln1_shift"],
        "ln2_scale": a["L2_ffn_ln2_scale"], "ln2_shift": a["L2_ffn_ln2_shift"],
        "ln_w": a["L3_ffn_ln_w"], "ln_b": a["L3_ffn_ln_b"],
        "F0_w1": a["L0_ffn_W_in"], "F0_b1": c(a["L0_ffn_b_in"].reshape(4, 128).T),
        "F0_w2": a["L0_ffn_W_out"], "F0_b2": a["L0_ffn_b_out"],
        "F1_gate": a["L1_ffn_gate_w"], "F1_gate_b": a["L1_ffn_gate_b"],
        "F1_w1": a["L1_ffn_w1"], "F1_b1": c(a["L1_ffn_b1"].reshape(8, 4, 128).transpose(2, 0, 1).reshape(128, 32)),
        "F1_w2": a["L1_ffn_w2"], "F1_b2": a["L1_ffn_b2"],
        "F1_ws1": a["L1_ffn_ws1"], "F1_bs1": c(a["L1_ffn_bs1"].reshape(4, 128).T),
        "F1_ws2": a["L1_ffn_ws2"], "F1_bs2": a["L1_ffn_bs2"],
        "F2_gate": a["L2_ffn_gate_w"], "F2_w1": a["L2_ffn_w1"], "F2_w2": a["L2_ffn_w2"], "F2_w3": a["L2_ffn_w3"],
        "F3_gate": c(a["L3_ffn_Wr"].T), "F3_gate_b": a["L3_ffn_br"],
        "F3_w1": c(a["L3_ffn_W1"].transpose(0, 2, 1)),
        "F3_b1": c(a["L3_ffn_b1"].reshape(8, 4, 128).transpose(2, 0, 1).reshape(128, 32)),
        "F3_w2": c(a["L3_ffn_W2"].transpose(0, 2, 1)), "F3_b2": a["L3_ffn_b2"],
    }
    for ph, pre in (("A0", "L0_xattn_w{}"), ("A1", "L1_xattn_w{}"), ("A2", "L2_xattn_W{}_w")):
        for w in "qkvo":
            t[f"{ph}_{w}"] = c(a[pre.format(w)].T)
    for ph, pre in (("A0", "L0_xattn_b{}"), ("A1", "L1_xattn_b{}"), ("A2", "L2_xattn_W{}_b")):
        for w in "qkvo":
            t[f"{ph}_b{w}"] = a[pre.format(w)]
    for w in "qkvo":
        t[f"AS_{w}"] = a[f"L2_ffn_w{w}"]
    t["AS_bo"] = a["L2_ffn_bo"]
    for w in "qkv":
        t[f"A3_{w}"] = c(a[f"L3_xattn_W{w}"].T)
    t["A3_o"], t["A3_bo"] = c(a["L3_xattn_Wo"].T), a["L3_xattn_bo"]

    nc = bacc.Bacc("TRN2", target_bir_lowering=False, num_devices=1)
    arrays = {f"in_{n}": np.ascontiguousarray(v) for n, v in t.items()}
    aps = {n: nc.dram_tensor(f"in_{n}", v.shape, mb.dt.from_np(v.dtype), kind="ExternalInput").ap() for n, v in
           ((n[3:], v) for n, v in arrays.items())}
    out = nc.dram_tensor("out_x", (8, 256, 128), mb.dt.float32, kind="ExternalOutput").ap()
    build(nc, aps, out)
    r = run_bass_kernel_spmd(nc, [arrays], core_ids=[0])
    return r.results[0]["out_x"]
```

```python
from contextlib import ExitStack

import concourse.bass as bass
from concourse import mybir

F32 = mybir.dt.float32
F32R = mybir.dt.float32r
BF16 = mybir.dt.bfloat16
I32 = mybir.dt.int32
U32 = mybir.dt.uint32
ALU = mybir.AluOpType
ACT = mybir.ActivationFunctionType
AX = mybir.AxisListType

B, S, D, SK = 8, 256, 128, 512
H, DH = 16, 8
NT = B * S // 128
QT = S // 128
HG = 4
ROWS = 3 * DH
NG = H // HG
TB = 4
NBLK = NT // TB
E = 8
MASKED = -float(2 ** 100)
ROUND = 1.5 * 2 ** 23
A8, A16 = 127.0, 32767.0
EPS = 1e-5

ATT = {
    "A0": dict(nk=SK, scale=DH ** -0.5, mask=None),
    "A1": dict(nk=SK, scale=DH ** -0.5, mask=None),
    "A2": dict(nk=SK, scale=DH ** -0.5, mask="full"),
    "AS": dict(nk=S, scale=DH ** -0.5, mask="causal"),
    "A3": dict(nk=SK, scale=D ** -0.5, mask="keys"),
}
TURN = [0, 1, 2, 0, 1, 2, 0, 1]
BACK = [2, 2, 5, 3, 3, 3, 3, 3]
PHASES = ["A0", "F0", "A1", "F1", "A2", "AS", "F2", "A3", "F3"]


def att_counts(ph):
    nkt = ATT[ph]["nk"] // 128
    stats = 2 if ph == "AS" else 1
    return dict(
        s_ready=8 * NG, st_ready=2 * nkt * NG, av_ready=nkt * NG, mt_ready=NG, xt_ready=1, q_ready=1,
        k_ready=1, v_ready=1, avt_ready=2, ont_ready=1, o_ready=1,
        exp_done=2 * nkt * NG, mt_read=NG, xt_read=1, q_read=1, k_read=1,
        max_done=8 * NG, msplit=NG, av_read=NG, v_read=1, on_done=2, ont_read=1, x_new=1,
        var_done=stats, xn_done=1, kh_done=1, ql_done=1,
        y_done=stats - 1, mask_conv=1 if ph == "A3" else 0,
    )


def ffn_counts(ph):
    if ph == "F0":
        return dict(var_done=1, rstd_done=1, xn_done=1, fxt_ready=1, fxt_read=1, h_ready=4, h_done=4,
                    hq_done=1, y_ready=1, x_new=1)
    shared = ph == "F1"
    n = E + (ph != "F2")
    ne = E + shared
    return dict(
        var_done=1, rstd_done=1, xn_done=1, fxt_ready=1,
        fxt_read=1, lg_ready=1, lg_read=1, th_done=1, comb_done=1,
        h_ready=4 * ne, h_done=4 * ne if ph != "F2" else 2 * ne, g_done=2 * ne if ph == "F2" else 0,
        y_ready=n, acc_done=n, ct_ready=int(ph != "F2"), ct_read=int(ph != "F2"), x_new=1,
        var2_done=int(ph == "F3"), rstd2_done=int(ph == "F3"),
    )


N_LOADED = 9 + 9 + 5 + 4 + 3 + 2 + 2 + 1 + 2
W_PARTS = {"F0": 3, "F1": 15, "F2": 10, "F3": 11}
LINKS = {'A0': 8, 'A1': 8, 'A2': 8, 'AS': 12, 'A3': 8, 'F1': 8, 'F2': 9, 'F3': 14}
POOL_LINKS = {'A0': 36, 'A1': 36, 'A2': 36, 'AS': 40, 'A3': 36}


class Counts:

    def __init__(self):
        self.credit = {"acc_done": 2, "g_done": 2, "y_ready": 2, "h_done": 4, "h_ready": 1, "fxt_ready": 1,
                       "fxt_read": 1}
        self.per, self.base, total = {}, {}, dict(self.credit)
        for ph in PHASES:
            self.per[ph] = att_counts(ph) if ph in ATT else ffn_counts(ph)
            self.base[ph] = dict(total)
            for name, n in self.per[ph].items():
                total[name] = total.get(name, 0) + n * (B if ph in ATT else NBLK)
        self.names = sorted(total)

    def start(self, name, ph):
        return self.base[ph].get(name, 0)

    def at(self, name, ph, b, k=0):
        b = b.b if isinstance(b, Batch) else b
        return self.base[ph].get(name, 0) + b * self.per[ph][name] + (k + 1)


class Batch:

    def __init__(self, i, off):
        self.i, self.off = i, off
        self.b, self.half, self.parity = i * 2 + off, i + off // 2, off % 2
        self.known = isinstance(i, int)

    def __add__(self, n):
        return Batch(self.i, self.off + n)


class Links:

    def __init__(self, eng, sem):
        self.eng, self.sem, self.n, self.loop = eng, sem, 0, None

    def __call__(self, ins, after=None):
        self.n += 1
        ins.then_inc(self.sem, 1)
        value = self.n if self.loop is None else self.loop[0] * self.loop[1] + self.n
        self.eng.wait_ge(self.sem, value)
        if after:
            after(self.eng)

    def enter(self, i, per):
        self.loop, self.begin = (i, per), self.n

    def leave(self, turns):
        i, per = self.loop
        assert self.n - self.begin == per, ("links in the loop", self.n - self.begin, per)
        self.loop, self.n = None, self.begin + turns * per


def batches(eng, body, links=None, per=0):
    body(Batch(0, 0), True, False)
    with eng.Fori(0, B // 2 - 1) as i:
        if links:
            links.enter(i, per)
        body(Batch(i, 1), False, False)
        body(Batch(i, 2), False, False)
    if links:
        links.leave(B // 2 - 1)
    body(Batch(B // 2 - 1, 1), False, True)


def blocks(eng, n, body, links=None, per=0):
    with eng.Fori(0, n) as i:
        if links:
            links.enter(i, per)
        body(i)
    if links:
        links.leave(n)


def build(nc, t, out):
    cnt = Counts()
    with ExitStack() as ctx:
        def sb(name, shape, dt=F32):
            return ctx.enter_context(nc.sbuf_tensor(name, shape, dt))

        def sem(name):
            return ctx.enter_context(nc.semaphore(name))

        sig = {n: sem(n) for n in cnt.names}

        x_tok = sb("x_tok", [128, NT, D])
        y_tok = sb("y_tok", [128, NT, D])
        ctxT = sb("ctxT", [128, 2, SK])
        xn = sb("xn", [128, QT, D])
        xnT = sb("xnT", [128, S])
        qf = sb("qf", [128, S])
        q_hi = sb("q_hi", [128, S], F32R)
        q_lo = sb("q_lo", [128, S], F32R)
        kf = sb("kf", [128, SK])
        k_hi = sb("k_hi", [128, SK], F32R)
        k_lo = sb("k_lo", [128, SK], F32R)
        qz = [sb(f"qz{p}", [128, NG, HG, S], F32R) for p in range(2)]
        kst = [sb(f"kst{p}", [128, NG, SK], F32R) for p in range(2)]
        vaug = [sb(f"vaug{p}", [128, 4, H, 32]) for p in range(2)]
        prob = sb("prob", [128, 2, 4, HG * S])
        avs = sb("avs", [128, NG, S])
        o_n = sb("o_n", [128, QT, D])
        o_nT = sb("o_nT", [128, S])
        mx = sb("mx", [128, 2, 8])
        mrest = sb("mrest", [128, 2, 8])
        mpart = sb("mpart", [128, 2, 2, 128], BF16)
        rsum = sb("rsum", [128, H])
        junk = sb("junk", [128, 3, SK], BF16)
        st6 = sb("st6", [128, TB, 6])
        mv = sb("mv", [128, TB, 2])
        st6b = sb("st6b", [128, TB, 6])
        mvb = sb("mvb", [128, TB, 2])
        veps = sb("veps", [128, 2, TB])
        rstd = sb("rstd", [128, 2, TB])
        neg_half = sb("neg_half", [128, TB])
        mask_q = sb("mask_q", [128, 2, SK])
        mask_T = sb("mask_T", [128, 4, S], BF16)
        caus_q = sb("caus_q", [128, 2, S])
        caus_T = sb("caus_T", [128, 2, S], BF16)
        mrow_i = caus_q[:, :, :].rearrange("p c k -> p (c k)").bitcast(I32)
        mrow = mask_q
        mcol_i = sb("mcol_i", [128, 4], I32)
        mcol = sb("mcol", [128, 2, 4])
        ident = sb("ident", [128, 128])
        ident_b = sb("ident_b", [128, 128], BF16)
        ones_row = sb("ones_row", [1, 128])
        iota_e = sb("iota_e", [128, E])
        w_att = {a: sb(f"w_{a}", [128, 4, 128]) for a in ("A0", "A1", "A3")}
        w_att |= {"A2": w_att["A0"], "AS": w_att["A1"]}
        b_att = {a: sb(f"b_{a}", [128, 2]) for a in ATT}
        bv_att = {a: sb(f"bv_{a}", [128, D]) for a in ("A0", "A1", "A2")}
        bo_att = {a: sb(f"bo_{a}", [1, D]) for a in ATT}
        ln_cols = sb("ln_cols", [128, 4])
        w_ffn = sb("w_ffn", [128, 9 * 1024])
        xf = avs[:, 0:2, :].rearrange("p g (q d) -> p (g q) d", d=D)
        acc = avs[:, 2:4, :].rearrange("p g (q d) -> p (g q) d", d=D)
        xfT = ctxT[:, 1, :]
        gate = sb("gate", [128, 3, E])
        gate_bb = sb("gate_bb", [128, 2, E])
        lg = sb("lg", [128, TB, E])
        top = sb("top", [128, TB, E])
        topi = sb("topi", [128, TB, E], U32)
        topf = sb("topf", [128, TB, 2])
        dlt = sb("dlt", [128, TB])
        th = sb("th", [128, TB])
        w2 = sb("w2", [128, 2, TB])
        eq = sb("eq", [128, 2, TB, E])
        comb = sb("comb", [128, TB, E + 1])
        combT = kf[0:E + 1, :]
        b1c = sb("b1c", [128, 9 * 4])
        b2r = sb("b2r", [E + 1, D])
        lnw = sb("lnw", [128, 2, D])
        amx = sb("amx", [128, 8])
        aall = sb("aall", [128, 8])
        awq = w_ffn[:, 5120:5632]
        awo = sb("awo", [128, 2, 4])
        svec = sb("svec", [128, 8])
        boutb = sb("boutb", [128, D])

        ps_s = [ctx.enter_context(nc.psum_tensor(f"ps_s{i}", [128, 512], F32)) for i in range(3)]
        ps_t = [ctx.enter_context(nc.psum_tensor(f"ps_t{i}", [128, 512], F32)) for i in range(3)]
        ps_h = [*ps_t, ps_s[2]]
        ps_av = ctx.enter_context(nc.psum_tensor("ps_av", [128, 512], F32))
        ps_m = ctx.enter_context(nc.psum_tensor("ps_m", [128, 512], F32))
        ps_mb = ps_m[:, :].bitcast(BF16)

        scratch = {n: nc.dram_tensor(f"{n}_parts", (2, 3 * 128, w), F32).ap() for n, w in (("q", S), ("k", SK))}
        ctx_in = [sem(f"ctx_in{p}") for p in range(2)]
        q_saved = [sem(f"q_saved{p}") for p in range(2)]
        k_saved = [sem(f"k_saved{p}") for p in range(2)]
        q_stacked = [sem(f"q_stacked{p}") for p in range(2)]
        k_stacked = [sem(f"k_stacked{p}") for p in range(2)]
        mask_in = sem("mask_in")
        loaded = sem("loaded")
        bd_loaded = sem("bd_loaded")
        watt_in = {a: sem(f"watt_in_{a}") for a in ("A2", "AS")}
        w_in = {ph: sem(f"w_in_{ph}") for ph in ("F0", "F1", "F2", "F3")}
        setup_pool = sem("setup_pool")
        pool_chain = sem("pool_chain")
        dve_chain = sem("dve_chain")
        col_absmax = sem("col_absmax")
        w_cols = sem("w_cols")
        max_given = sem("max_given")
        max_all = sem("max_all")
        svec_done = sem("svec_done")
        bias_scaled = sem("bias_scaled")
        x_loaded = sem("x_loaded")
        stored = sem("stored")
        apart_waits = sem("apart_waits")

        ATTS = [p for p in PHASES if p in ATT]

        def stacked(ph, bt, dmas):
            return 16 * dmas * (ATTS.index(ph) * (B // 2) + bt.half + 1)

        def saved(ph, bt):
            return 16 * 3 * (ATTS.index(ph) * (B // 2) + bt.half + 1)

        def context_in(ph, bt):
            n = sum(a != "AS" for a in ATTS[:ATTS.index(ph)])
            return 16 * (n * (B // 2) + bt.half + 1)

        def wait(eng, name, value):
            if not (isinstance(value, int) and value <= 0):
                eng.wait_ge(sig[name], value)

        def apart(eng):
            eng.sem_inc(apart_waits, 1)

        def seen(ph, kt):
            return 128 * kt if ph == "AS" else 0

        def turn_of(ph, g, kt, half):
            return (2 * (ATT[ph]["nk"] // 128 * g + kt) + half) % 8

        def slots(ph):
            s = {(g, 1): "MT" for g in range(NG)}
            s |= {(0, 2): "XT", (0, 3): "Q", (1, 2): "AVT0", (1, 3): "AVT1", (2, 0): "ONT", (2, 2): "V", (2, 3): "O"}
            s[(1, 0) if ph == "AS" else (0, 0)] = "K"
            return s

        def later(bt, g, n):
            return bt + (g + n) // NG, (g + n) % NG

        def kt_of(ph, k):
            if ATT[ph]["nk"] == SK:
                return k
            return k // 2 if k % 2 == 0 else None

        block = ctx.enter_context(nc.Block())

        @block.sync
        def _(sp):
            sp.dma_start(x_tok[:, :, :], t["x"].rearrange("b (q p) d -> p (b q) d", p=128)).then_inc(x_loaded, 16)
            for a in ATT:
                for i, w in enumerate("qkvo"):
                    if a in ("A0", "A1") or a == "A3" and w == "o":
                        sp.dma_start(w_att[a][:, i, :], t[f"{a}_{w}"]).then_inc(loaded, 16)
                if a in bv_att:
                    for i, w in enumerate("qk"):
                        sp.dma_start(b_att[a][:, i:i + 1], t[f"{a}_b{w}"].rearrange("(d o) -> d o", o=1)).then_inc(loaded, 16)
                    sp.dma_start(bv_att[a][:, :], t[f"{a}_bv"].rearrange("(o d) -> o d", o=1).to_broadcast([128, D])).then_inc(loaded, 16)
                sp.dma_start(bo_att[a][:, :], t[f"{a}_bo"].rearrange("(o d) -> o d", o=1)).then_inc(loaded, 16)
            for i, w in enumerate(("ln1_scale", "ln1_shift", "ln2_scale", "ln2_shift")):
                sp.dma_start(ln_cols[:, i:i + 1], t[w].rearrange("(d o) -> d o", o=1)).then_inc(loaded, 16)
            for i, w in enumerate(("F1_gate", "F2_gate", "F3_gate")):
                sp.dma_start(gate[:, i, :], t[w]).then_inc(loaded, 16)
            for i, w in enumerate(("F1_gate_b", "F3_gate_b")):
                sp.dma_start(gate_bb[:, i, :], t[w].rearrange("(o e) -> o e", o=1).to_broadcast([128, E])).then_inc(loaded, 16)
            for i, w in enumerate(("ln_w", "ln_b")):
                sp.dma_start(lnw[:, i, :], t[w].rearrange("(o e) -> o e", o=1).to_broadcast([128, D])).then_inc(loaded, 16)
            sp.dma_start(boutb[:, :], t["F0_b2"].rearrange("(o e) -> o e", o=1).to_broadcast([128, D])).then_inc(loaded, 16)
            sp.dma_start(prob[:, 1, 0, :].bitcast(I32).rearrange("p (c k) -> p c k", c=2), t["mask_q"].rearrange("(c p) k -> p c k", p=128)).then_inc(loaded, 16)
            sp.dma_start(prob[:, 1, 1, :].bitcast(I32).rearrange("p (c k) -> p c k", c=4), t["mask_T"].rearrange("(c p) q -> p c q", p=128)).then_inc(loaded, 16)
            sp.wait_ge(setup_pool, 1)
            for i, w in enumerate("qkv"):
                for h in range(H):
                    sp.dma_start(w_att["A3"][DH * h:DH * h + DH, i, DH * h:DH * h + DH], t[f"A3_{w}"]).then_inc(bd_loaded, 16)

            def load_ffn(ph):
                wait(sp, "y_ready", cnt.start("y_ready", ph))
                wait(sp, "h_done", cnt.start("h_done", ph))
                done = w_in[ph]
                if ph == "F0":
                    sp.dma_start(w_ffn[:, 0:512], t["F0_w1"]).then_inc(done, 16)
                    sp.dma_start(w_ffn[:, 512:1024].rearrange("p (c d) -> p c d", c=4), t["F0_w2"].rearrange("(c p) d -> p c d", p=128)).then_inc(done, 16)
                    sp.dma_start(b1c[:, 0:4], t["F0_b1"]).then_inc(done, 16)
                if ph in ("F1", "F3"):
                    ne = 9 if ph == "F1" else 8
                    sp.dma_start(w_ffn[:, 0:4096].rearrange("p (e f) -> p e f", e=E), t[f"{ph}_w1"].rearrange("e d f -> d e f")).then_inc(done, 16)
                    for e in range(E):
                        sp.dma_start(w_ffn[:, 512 * (ne + e):512 * (ne + e + 1)].rearrange("p (c d) -> p c d", c=4), t[f"{ph}_w2"][e].rearrange("(c p) d -> p c d", p=128)).then_inc(done, 16)
                    sp.dma_start(b1c[:, 0:32], t[f"{ph}_b1"]).then_inc(done, 16)
                    sp.dma_start(b2r[0:E, :], t[f"{ph}_b2"]).then_inc(done, 16)
                if ph == "F1":
                    sp.dma_start(w_ffn[:, 4096:4608], t["F1_ws1"]).then_inc(done, 16)
                    sp.dma_start(w_ffn[:, 512 * 17:512 * 18].rearrange("p (c d) -> p c d", c=4), t["F1_ws2"].rearrange("(c p) d -> p c d", p=128)).then_inc(done, 16)
                    sp.dma_start(b1c[:, 32:36], t["F1_bs1"]).then_inc(done, 16)
                    sp.dma_start(b2r[E:E + 1, :], t["F1_bs2"].rearrange("(o d) -> o d", o=1)).then_inc(done, 16)
                if ph == "F2":
                    for i, w in enumerate(("F2_w1", "F2_w2")):
                        sp.dma_start(w_ffn[:, 2048 * i:2048 * (i + 1)].rearrange("p (e f) -> p e f", e=E), t[w].rearrange("e d f -> d e f")).then_inc(done, 16)
                    for e in range(E):
                        sp.dma_start(w_ffn[:, 4096 + 256 * e:4096 + 256 * (e + 1)].rearrange("p (c d) -> p c d", c=2), t["F2_w3"][e].rearrange("(c p) d -> p c d", p=128)).then_inc(done, 16)

            def load_context(ph, bt):
                if ph == "AS":
                    return
                p = bt.parity
                sp.dma_start(ctxT[:, p, :], t["ctxT"][bass.ds(bt.b, 1)].rearrange("o d k -> d (o k)")).then_inc(ctx_in[p], 16)
                if ph == "A3":
                    sp.dma_start(mrow_i[:, :], t["mask_k"][bass.ds(bt.b, 1)].to_broadcast([128, SK])).then_inc(mask_in, 16)
                    sp.dma_start(mcol_i[:, :], t["mask_kT"][bass.ds(bt.b, 1)].rearrange("o p c -> p (o c)")).then_inc(mask_in, 16)

            def save(n, p, part, width, src, done):
                rows = scratch[n][p].rearrange("(h b c) w -> b h c w", h=H, b=3)[part][:, :, 0:width]
                sp.dma_start(rows, src[:, 0:width].bitcast(F32)).then_inc(done[p], 16)

            def stack_k(ph, bt):
                p, nk = bt.parity, ATT[ph]["nk"]
                wait(sp, "k_read", cnt.at("k_read", ph, bt))
                save("k", p, 0, nk, k_hi, k_saved)
                save("k", p, 2, nk, k_hi, k_saved)
                wait(sp, "kh_done", cnt.at("kh_done", ph, bt))
                save("k", p, 1, nk, k_lo, k_saved)
                sp.wait_ge(k_saved[p], saved(ph, bt))
                rows = scratch["k"][p].rearrange("(g r) w -> r g w", g=NG)[:, :, 0:nk]
                sp.dma_start(kst[p][0:HG * ROWS, :, 0:nk].bitcast(F32), rows).then_inc(k_stacked[p], 16)

            def stack_q(ph, bt):
                p = bt.parity
                wait(sp, "q_read", cnt.at("q_read", ph, bt))
                save("q", p, 0, S, q_hi, q_saved)
                save("q", p, 1, S, q_hi, q_saved)
                wait(sp, "ql_done", cnt.at("ql_done", ph, bt))
                save("q", p, 2, S, q_lo, q_saved)
                sp.wait_ge(q_saved[p], saved(ph, bt))
                for j in range(HG):
                    rows = scratch["q"][p].rearrange("(g j r) w -> j r g w", g=NG, j=HG)[j]
                    sp.dma_start(qz[p][ROWS * j:ROWS * (j + 1), :, j, :].bitcast(F32), rows).then_inc(q_stacked[p], 16)

            def stack(ph, bt, released):
                wait(sp, "st_ready", released)
                apart(sp)
                for f in ((stack_q, stack_k) if ph == "AS" else (stack_k, stack_q)):
                    f(ph, bt)

            for ph in PHASES:
                if ph not in ATT:
                    continue
                load_ffn({"A0": "F0", "A1": "F1", "A2": "F2", "AS": None, "A3": "F3"}[ph]) if ph != "AS" else None
                units_before = cnt.start("st_ready", ph)
                wait(sp, "k_ready", cnt.start("k_ready", ph))
                wait(sp, "v_ready", cnt.start("v_ready", ph))
                if ph == "A3":
                    wait(sp, "max_done", cnt.start("max_done", ph))
                if ph in ("A1", "A2"):
                    wait(sp, "o_ready", cnt.start("o_ready", ph))
                    a = {"A1": "A2", "A2": "AS"}[ph]
                    for i, w in enumerate("qkvo"):
                        sp.dma_start(w_att[a][:, i, :], t[f"{a}_{w}"]).then_inc(watt_in[a], 16)
                load_context(ph, Batch(0, 0))
                stack(ph, Batch(0, 0), units_before)

                def body(bt, first, last):
                    if last:
                        return
                    if not first:
                        wait(sp, "v_ready", cnt.at("v_ready", ph, bt + -1))
                        apart(sp)
                    if ph == "A3":
                        wait(sp, "mask_conv", cnt.at("mask_conv", ph, bt))
                    load_context(ph, bt + 1)
                    stack(ph, bt + 1, units_before if first else cnt.at("st_ready", ph, bt + -1, cnt.per[ph]["st_ready"] - 1))

                batches(sp, body)
            out_tiles = out.rearrange("b (q p) d -> p (b q) d", p=128)
            with sp.Fori(0, NBLK) as blk:
                sp.wait_ge(sig["x_new"], cnt.at("x_new", "F3", blk))
                sp.dma_start(out_tiles[:, bass.ds(blk * TB, TB), :], x_tok[:, bass.ds(blk * TB, TB), :]).then_inc(stored, 16)
            sp.wait_ge(stored, 16 * NBLK)

        @block.gpsimd
        def _(pool):
            link = Links(pool, pool_chain)

            pool.memset(w_att["A3"][:, 0:3, :], 0.0).then_inc(setup_pool, 1)
            link(pool.memset(ident[:, :], 0.0))
            link(pool.affine_select(out=ident[:, :], in_=ident[:, :], compare_op=ALU.not_equal, fill=1.0, base=0, pattern=[[-1, 128]], channel_multiplier=1))
            link(pool.memset(ident_b[:, :], 0.0))
            link(pool.affine_select(out=ident_b[:, :], in_=ident_b[:, :], compare_op=ALU.not_equal, fill=1.0, base=0, pattern=[[-1, 128]], channel_multiplier=1))
            link(pool.memset(caus_q[:, :, :], 0.0))
            link(pool.memset(caus_T[:, :, :], 0.0))
            link(pool.affine_select(out=caus_q[:, :, :], in_=caus_q[:, :, :], compare_op=ALU.is_ge, fill=MASKED, base=0, pattern=[[128, 2], [-1, S]], channel_multiplier=1))
            link(pool.affine_select(out=caus_T[:, :, :], in_=caus_T[:, :, :], compare_op=ALU.is_ge, fill=MASKED, base=0, pattern=[[-128, 2], [1, S]], channel_multiplier=-1))
            link(pool.iota(iota_e[:, :], pattern=[[1, E]], base=0, channel_multiplier=0, allow_small_or_imprecise_dtypes=True))
            link(pool.memset(neg_half[:, :], -0.5))
            link(pool.memset(ones_row[:, :], 1.0))
            for a in ("AS", "A3"):
                link(pool.memset(b_att[a][:, :], 0.0))
            for p in range(2):
                link(pool.memset(qz[p][:, :, :, :].bitcast(F32), 0.0))
                link(pool.memset(kst[p][96:128, :, :].bitcast(F32), 1.0))
                link(pool.memset(vaug[p][:, :, :, :], 0.0))
                link(pool.memset(vaug[p][:, :, :, DH:DH + 1], 1.0))
            link(pool.memset(mpart[:, :, :, :], 0.0))
            pool.memset(comb[:, :, E:E + 1], 1.0).then_inc(setup_pool, 1)

            def power(ph, b, k, n):
                pool.wait_ge(sig["var_done"], cnt.at("var_done", ph, b, k))
                pool.tensor_tensor(rstd[:, 0, 0:n], veps[:, 0, 0:n], neg_half[:, 0:n], ALU.pow).then_inc(sig["rstd_done"], 1)

            def power_of_result(blk):
                pool.wait_ge(sig["var2_done"], cnt.at("var2_done", "F3", blk))
                pool.tensor_tensor(rstd[:, 1, :], veps[:, 1, :], neg_half[:, :], ALU.pow).then_inc(sig["rstd2_done"], 1)

            def normalise(ph, bt, k):
                pool.wait_ge(sig["var_done"], cnt.at("var_done", ph, bt, k))
                link(pool.tensor_tensor(rstd[:, 0, 0:QT], veps[:, 0, 0:QT], neg_half[:, 0:QT], ALU.pow), apart)
                src = (y_tok if k else x_tok)[:, bass.ds(bt.b * QT, QT), :]
                mean, power_ = (a.rearrange("p (q o) -> p q o", o=1).to_broadcast([128, QT, D]) for a in (mv[:, 0:QT, 0], rstd[:, 0, 0:QT]))
                if ph == "AS" and k == 0:
                    dst, done = y_tok[:, bass.ds(bt.b * QT, QT), :], "y_done"
                else:
                    dst, done = xn[:, :, :], "xn_done"
                    wait(pool, "xt_ready", cnt.at("xt_ready", ph, bt) - 1)
                    apart(pool)
                link(pool.tensor_tensor(dst, src, mean, ALU.subtract), apart)
                pool.tensor_tensor(dst, dst, power_, ALU.mult).then_inc(sig[done], 1)

            def prepare_masks(bt):
                ph = "A3"
                if True:
                    pool.wait_ge(mask_in, 32 * (bt.b + 1))
                    if not bt.known or bt.b >= 2:
                        pool.wait_ge(sig["max_done"], cnt.at("max_done", ph, bt + -2, 8 * NG - 1))
                        pool.wait_ge(sig["exp_done"], cnt.at("exp_done", ph, bt + -2, 8 * NG - 1))
                    apart(pool)
                    pool.tensor_scalar(mrow[:, bt.parity, :], mrow_i[:, :], 0.0, MASKED, ALU.is_equal, ALU.mult)
                    pool.tensor_scalar(mcol[:, bt.parity, :], mcol_i[:, :], 0.0, MASKED, ALU.is_equal, ALU.mult).then_inc(sig["mask_conv"], 1)

            def split_k(ph, bt):
                nk = ATT[ph]["nk"]
                pool.wait_ge(sig["k_read"], cnt.at("k_read", ph, bt))
                pool.tensor_tensor(k_lo[:, 0:nk], kf[:, 0:nk], k_hi[:, 0:nk].bitcast(F32), ALU.subtract).then_inc(sig["kh_done"], 1)

            def split_q(ph, bt):
                pool.wait_ge(sig["q_read"], cnt.at("q_read", ph, bt))
                pool.tensor_tensor(q_lo[:, :], qf[:, :], q_hi[:, :].bitcast(F32), ALU.subtract).then_inc(sig["ql_done"], 1)

            def split_maxima(ph, bt, g):
                buf = g % 2
                m = mx[:, buf, :].rearrange("p (j q) -> p q j", q=QT)
                neg, rest = (mrest[:, i, :].rearrange("p (j q) -> p q j", q=QT) for i in range(2))
                part = [mpart[:, buf, :, c:c + 3 * (32 + DH) + 1:32 + DH] for c in range(3)]
                pool.wait_ge(sig["max_done"], cnt.at("max_done", ph, bt, 8 * g + 7))
                wait(pool, "mt_ready", cnt.at("mt_ready", ph, bt, g) - 2)
                apart(pool)
                link(pool.tensor_scalar(neg, m, -1.0, None, ALU.mult), apart)
                link(pool.tensor_copy(part[0], neg))
                link(pool.tensor_tensor(rest, neg, part[0], ALU.subtract), apart)
                link(pool.tensor_copy(part[1], rest))
                pool.tensor_tensor(part[2], rest, part[1], ALU.subtract).then_inc(sig["msplit"], 1)

            def attention(ph):
                b0 = Batch(0, 0)
                if ph == "A3":
                    pool.wait_ge(sig["max_done"], cnt.start("max_done", ph))
                    prepare_masks(b0)
                if ph != "AS":
                    split_k(ph, b0)
                for k in range(cnt.per[ph]["var_done"]):
                    normalise(ph, b0, k)
                split_q(ph, b0)
                if ph == "AS":
                    split_k(ph, b0)
                for g in range(2):
                    split_maxima(ph, b0, g)

                def body(bt, first, last):
                    for g in range(NG):
                        ahead, g_ahead = later(bt, g, 2)
                        if not last and g == 0:
                            for k in range(cnt.per[ph]["var_done"]):
                                normalise(ph, bt + 1, k)
                            if ph != "AS":
                                split_k(ph, bt + 1)
                            if ph == "A3":
                                prepare_masks(bt + 1)
                        if not last and g == 1:
                            split_q(ph, bt + 1)
                            if ph == "AS":
                                split_k(ph, bt + 1)
                        if not (last and g >= 2):
                            split_maxima(ph, ahead, g_ahead)

                batches(pool, body, link, POOL_LINKS[ph])

            for ph in PHASES:
                if ph in ATT:
                    attention(ph)
                elif ph == "F0":
                    pool.wait_ge(w_in["F0"], 48)
                    pool.partition_all_reduce(awq[:, :], w_ffn[:, 0:512], 128, bass.bass_isa.ReduceOp.absmax).then_inc(col_absmax, 1)
                    blocks(pool, NBLK, lambda blk: power("F0", blk, 0, TB))
                    for i in range(2):
                        pool.wait_ge(max_given, i + 1)
                        pool.partition_all_reduce(aall[:, i:i + 1], amx[:, i:i + 1], 128, bass.bass_isa.ReduceOp.absmax).then_inc(max_all, 1)
                else:
                    def body(blk):
                        power(ph, blk + 1, 0, TB)
                        if ph == "F3":
                            power_of_result(blk)
                    power(ph, 0, 0, TB)
                    blocks(pool, NBLK - 1, body)
                    if ph == "F3":
                        power_of_result(NBLK - 1)

        @block.scalar
        def _(act):
            def exponentials(ph, bt, g, kt):
                p, nkt, q0 = bt.parity, ATT[ph]["nk"] // 128, seen(ph, kt)
                bias = mcol[:, p, kt:kt + 1] if ATT[ph]["mask"] == "keys" else 0.0
                for half in range(2):
                    wait(act, "st_ready", cnt.at("st_ready", ph, bt, 2 * (nkt * g + kt) + half))
                    if half == 0:
                        wait(act, "av_ready", cnt.at("av_ready", ph, bt, nkt * g + kt) - 2 * nkt)
                    dst = prob[:, g % 2, kt, 2 * S * half:2 * S * (half + 1)].rearrange("p (j s) -> p j s", j=2)[:, :, q0:]
                    src = ps_t[TURN[turn_of(ph, g, kt, half)]][:, 0:2 * (S - q0)].rearrange("p (j s) -> p j s", j=2)
                    nc.scalar.activation(dst, src, ACT.Exp, bias=bias).then_inc(sig["exp_done"], 1)

            def misc(what, ph, bt):
                nk = ATT[ph]["nk"]
                if what == "XT":
                    wait(act, "xt_ready", cnt.at("xt_ready", ph, bt))
                    wait(act, "v_ready", cnt.at("v_ready", ph, bt) - 1)
                    wait(act, "q_ready", cnt.at("q_ready", ph, bt) - 1)
                    if ph == "AS":
                        nc.scalar.activation(xnT[:, :], ps_m[:, 0:S], ACT.Identity, bias=ln_cols[:, 1:2],
                                             scale=ln_cols[:, 0:1]).then_inc(sig["xt_read"], 1)
                    else:
                        nc.scalar.activation(xnT[:, :], ps_m[:, 0:S], ACT.Copy).then_inc(sig["xt_read"], 1)
                elif what == "Q":
                    wait(act, "q_ready", cnt.at("q_ready", ph, bt))
                    wait(act, "ql_done", cnt.at("ql_done", ph, bt) - 1)
                    nc.scalar.activation(q_hi[:, :], ps_m[:, 0:S], ACT.Identity, bias=b_att[ph][:, 0:1], scale=ATT[ph]["scale"])
                    nc.scalar.activation(qf[:, :], ps_m[:, 0:S], ACT.Identity, bias=b_att[ph][:, 0:1],
                                         scale=ATT[ph]["scale"]).then_inc(sig["q_read"], 1)
                elif what == "K":
                    wait(act, "k_ready", cnt.at("k_ready", ph, bt))
                    wait(act, "kh_done", cnt.at("kh_done", ph, bt) - 1)
                    nc.scalar.activation(k_hi[:, 0:nk], ps_m[:, 0:nk], ACT.Identity, bias=b_att[ph][:, 1:2])
                    nc.scalar.activation(kf[:, 0:nk], ps_m[:, 0:nk], ACT.Identity, bias=b_att[ph][:, 1:2]).then_inc(sig["k_read"], 1)

                elif what == "ONT":
                    wait(act, "ont_ready", cnt.at("ont_ready", ph, bt))
                    wait(act, "o_ready", cnt.at("o_ready", ph, bt) - 1)
                    nc.scalar.activation(o_nT[:, :], ps_m[:, 0:S], ACT.Copy).then_inc(sig["ont_read"], 1)

            def read_values(ph, bt, g):
                wait(act, "av_ready", cnt.at("av_ready", ph, bt, (g + 1) * (ATT[ph]["nk"] // 128) - 1))
                if g == 0:
                    wait(act, "avt_ready", cnt.at("avt_ready", ph, bt) - 1)
                nc.scalar.activation(avs[:, g, :], ps_av[:, 0:S], ACT.Copy).then_inc(sig["av_read"], 1)

            def maxima_T(ph, bt, g):
                wait(act, "mt_ready", cnt.at("mt_ready", ph, bt, g))
                nc.scalar.activation(qz[bt.parity][96:128, g, :, :], ps_mb[96:128, :].rearrange("p (j s) -> p j s", j=HG),
                                     ACT.Copy).then_inc(sig["mt_read"], 1)

            def attention(ph):
                b0 = Batch(0, 0)
                for what in (("XT", "Q", "K") if ph == "AS" else ("K", "XT", "Q")):
                    misc(what, ph, b0)
                maxima_T(ph, b0, 0)
                table = slots(ph)

                def body(bt, first, last):
                    for g in range(NG):
                        nxt, g_nxt = later(bt, g, 1)
                        past, g_past = later(bt, g, -2)
                        if not (first and g < 2):
                            read_values(ph, past, g_past)
                        for k in range(4):
                            kt = kt_of(ph, k)
                            if kt is not None:
                                exponentials(ph, bt, g, kt)
                            what = table.get((g, k))
                            if what == "MT":
                                if not (last and g == 3):
                                    maxima_T(ph, nxt, g_nxt)
                            elif what in ("XT", "Q", "K") and not last:
                                misc(what, ph, bt + 1)
                            elif what == "ONT" and not first:
                                misc(what, ph, bt + -1)

                batches(act, body)
                end = Batch(B // 2 - 1, 1)
                for g in (2, 3):
                    read_values(ph, end, g)
                misc("ONT", ph, end)

            def read_block(ph, blk):
                wait(act, "fxt_ready", cnt.at("fxt_ready", ph, blk))
                wait(act, "h_ready", cnt.at("h_ready", ph, blk, -1))
                if ph == "F2":
                    nc.scalar.activation(xfT[:, :], ps_m[:, :], ACT.Identity, bias=ln_cols[:, 3:4],
                                         scale=ln_cols[:, 2:3]).then_inc(sig["fxt_read"], 1)
                else:
                    nc.scalar.activation(xfT[:, :], ps_m[:, :], ACT.Copy).then_inc(sig["fxt_read"], 1)

            def quantised_ffn():
                ph = "F0"
                hid = prob[:, :, :, :].rearrange("p a c s -> p (a c s)").rearrange("p (c s) -> p c s", c=4)
                act.wait_ge(max_all, 1)
                act.wait_ge(svec_done, 1)

                def body(blk):
                    for c in range(4):
                        wait(act, "h_ready", cnt.at("h_ready", ph, blk, c))
                        nc.scalar.activation(hid[:, c, bass.ds(blk * 512, 512)], ps_h[c][:, :],
                                             ACT.Gelu, bias=b1c[:, c:c + 1], scale=svec[:, c:c + 1]).then_inc(sig["h_done"], 1)

                blocks(act, NBLK, body)

            def experts(ph):
                ne = 9 if ph == "F1" else 8

                def body(blk):
                    read_block(ph, blk)
                    for e in range(ne):
                        h = prob[:, e % 2, :, :].rearrange("p c s -> p (c s)")[:, 0:2048].rearrange("p (c s) -> p c s", c=4)
                        for c in range(2 if ph == "F2" else 4):
                            wait(act, "h_ready", cnt.at("h_ready", ph, blk, 4 * e + c))
                            if c == 0:
                                wait(act, "y_ready", cnt.at("y_ready", ph, blk, e) - 2)
                            src = ps_h[c][:, :]
                            if ph == "F2":
                                nc.scalar.activation(h[:, 2 + c, :], src, ACT.Silu).then_inc(sig["h_done"], 1)
                            else:
                                nc.scalar.activation(h[:, c, :], src, ACT.Gelu, bias=b1c[:, 4 * e + c:4 * e + c + 1]).then_inc(sig["h_done"], 1)
                        if e == 0:
                            wait(act, "lg_read", cnt.at("lg_read", ph, blk))
                            nc.scalar.activation(th[:, :], dlt[:, :], ACT.Tanh, scale=0.5).then_inc(sig["th_done"], 1)

                act.wait_ge(w_in[ph], W_PARTS[ph] * 16)
                blocks(act, NBLK, body)

            act.wait_ge(loaded, 16 * N_LOADED)
            act.wait_ge(setup_pool, 2)
            act.wait_ge(bias_scaled, 3)
            for ph in PHASES:
                if ph in ATT:
                    attention(ph)
                elif ph == "F0":
                    quantised_ffn()
                else:
                    experts(ph)

        @block.tensor
        def _(pe):
            misc_reader = [None]

            def take_misc(reader, value):
                if misc_reader[0]:
                    wait(pe, *misc_reader[0])
                misc_reader[0] = (reader, value)

            def scores(ph, bt, g, i):
                p, nk, j, q = bt.parity, ATT[ph]["nk"], i // 2, i % 2
                if g == 0 and i == 0:
                    pe.wait_ge(q_stacked[p], stacked(ph, bt, HG))
                    pe.wait_ge(k_stacked[p], stacked(ph, bt, 1))
                if ph == "AS":
                    nk = 128 * (q + 1)
                wait(pe, "max_done", cnt.at("max_done", ph, bt, 8 * g + i) - BACK[i])
                pe.matmul(ps_s[TURN[i]][:, 0:nk], qz[p][0:96, g, j, q * 128:(q + 1) * 128], kst[p][0:96, g, 0:nk],
                          start=True, stop=True).then_inc(sig["s_ready"], 1)

            def scores_T(ph, bt, g, kt, half):
                p, nkt, mask = bt.parity, ATT[ph]["nk"] // 128, ATT[ph]["mask"]
                turn, q0 = turn_of(ph, g, kt, half), seen(ph, kt)
                if kt == 0 and half == 0:
                    wait(pe, "mt_read", cnt.at("mt_read", ph, bt, g))
                wait(pe, "exp_done", cnt.at("exp_done", ph, bt, 2 * (nkt * g + kt) + half) - BACK[turn])
                dst = ps_t[TURN[turn]][:, 0:2 * (S - q0)].rearrange("p (j s) -> p j s", j=2)
                mm = pe.matmul(dst, kst[p][:, g, kt * 128:(kt + 1) * 128], qz[p][:, g, 2 * half:2 * half + 2, q0:],
                               start=True, stop=mask in (None, "keys"))
                if mask == "full":
                    mm = pe.matmul(dst, ident_b[:, :], mask_T[:, kt:kt + 1, :].to_broadcast([128, 2, S]), start=False, stop=True)
                if mask == "causal":
                    mm = pe.matmul(dst[:, :, 0:128], ident_b[:, :], caus_T[:, kt:kt + 1, q0:q0 + 128].to_broadcast([128, 2, 128]),
                                   start=False, stop=True)
                mm.then_inc(sig["st_ready"], 1)

            def values(ph, bt, g, kt):
                p, nkt, q0 = bt.parity, ATT[ph]["nk"] // 128, seen(ph, kt)
                if kt == 0:
                    wait(pe, "av_read", cnt.at("av_read", ph, bt, g) - 1)
                    if g == 0:
                        wait(pe, "v_read", cnt.at("v_read", ph, bt))
                wait(pe, "exp_done", cnt.at("exp_done", ph, bt, 2 * (nkt * g + kt) + 1))
                buf = g % 2
                for j in range(HG):
                    mm = pe.matmul(ps_av[32 * j:32 * j + 32, q0:S], vaug[p][:, kt, HG * g + j, :],
                                   prob[:, buf, kt, S * j + q0:S * (j + 1)], start=(kt == 0), stop=(kt == nkt - 1))
                mm.then_inc(sig["av_ready"], 1)

            def maxima_T(ph, bt, g):
                take_misc("mt_read", cnt.at("mt_read", ph, bt, g))
                wait(pe, "msplit", cnt.at("msplit", ph, bt, g))
                for j in range(HG):
                    for q in range(QT):
                        mm = pe.transpose(ps_mb[96:128, S * j + 128 * q:S * j + 128 * (q + 1)],
                                          mpart[:, g % 2, q, 32 * j:32 * j + 32], ident_b[:, :])
                mm.then_inc(sig["mt_ready"], 1)

            def misc(what, ph, bt):
                nk, p = ATT[ph]["nk"], bt.parity
                w = w_att[ph]
                if what == "XT":
                    take_misc("xt_read", cnt.at("xt_read", ph, bt))
                    wait(pe, "xn_done", cnt.at("xn_done", ph, bt))
                    for q in range(QT):
                        mm = pe.transpose(ps_m[:, 128 * q:128 * (q + 1)], xn[:, q, :], ident[:, :])
                    mm.then_inc(sig["xt_ready"], 1)
                elif what == "Q":
                    take_misc("q_read", cnt.at("q_read", ph, bt))
                    wait(pe, "xt_read", cnt.at("xt_read", ph, bt))
                    pe.matmul(ps_m[:, 0:S], w[:, 0, :], xnT[:, :], start=True, stop=True).then_inc(sig["q_ready"], 1)
                elif what == "K":
                    take_misc("k_read", cnt.at("k_read", ph, bt))
                    if ph == "AS":
                        wait(pe, "xt_read", cnt.at("xt_read", ph, bt))
                    else:
                        pe.wait_ge(ctx_in[p], context_in(ph, bt))
                    pe.matmul(ps_m[:, 0:nk], w[:, 1, :], xnT[:, :] if ph == "AS" else ctxT[:, p, :],
                              start=True, stop=True).then_inc(sig["k_ready"], 1)
                elif what == "V":
                    take_misc("v_read", cnt.at("v_read", ph, bt))
                    for kt in range(nk // 128):
                        src = (xnT if ph == "AS" else ctxT[:, p, :])
                        mm = pe.matmul(ps_m[:, 128 * kt:128 * (kt + 1)], src[:, 128 * kt:128 * (kt + 1)], w[:, 2, :],
                                       start=True, stop=True)
                    mm.then_inc(sig["v_ready"], 1)
                elif what in ("AVT0", "AVT1"):
                    q = int(what[-1])
                    take_misc("on_done", cnt.at("on_done", ph, bt, q))
                    wait(pe, "av_read", cnt.at("av_read", ph, bt, NG - 1))
                    for g in range(NG):
                        mm = pe.transpose(ps_m[:, 128 * g:128 * (g + 1)], avs[:, g, 128 * q:128 * (q + 1)], ident[:, :])
                    mm.then_inc(sig["avt_ready"], 1)
                elif what == "ONT":
                    take_misc("ont_read", cnt.at("ont_read", ph, bt))
                    wait(pe, "on_done", cnt.at("on_done", ph, bt, 1))
                    for q in range(QT):
                        mm = pe.transpose(ps_m[:, 128 * q:128 * (q + 1)], o_n[:, q, :], ident[:, :])
                    mm.then_inc(sig["ont_ready"], 1)
                elif what == "O":
                    take_misc("x_new", cnt.at("x_new", ph, bt))
                    wait(pe, "ont_read", cnt.at("ont_read", ph, bt))
                    for q in range(QT):
                        dst = ps_m[:, 128 * q:128 * (q + 1)]
                        pe.matmul(dst, o_nT[:, 128 * q:128 * (q + 1)], w[:, 3, :], start=True, stop=False)
                        mm = pe.matmul(dst, ones_row[:, :], bo_att[ph][:, :], start=False, stop=True)
                    mm.then_inc(sig["o_ready"], 1)

            def attention(ph):
                wait(pe, "acc_done", cnt.start("acc_done", ph))
                wait(pe, "h_done", cnt.start("h_done", ph))
                wait(pe, "x_new", cnt.start("x_new", ph))
                misc_reader[0] = None
                if ph in watt_in:
                    pe.wait_ge(watt_in[ph], 64)
                b0 = Batch(0, 0)
                for what in (("XT", "Q", "K", "V") if ph == "AS" else ("K", "XT", "Q", "V")):
                    misc(what, ph, b0)
                for g in range(2):
                    for i in range(8):
                        scores(ph, b0, g, i)
                maxima_T(ph, b0, 0)
                table = slots(ph)

                def body(bt, first, last):
                    for g in range(NG):
                        ahead, g_ahead = later(bt, g, 2)
                        past, g_past = later(bt, g, -1)
                        nxt, g_nxt = later(bt, g, 1)
                        for k in range(4):
                            kt = kt_of(ph, k)
                            for half in range(2):
                                if not (last and g >= 2):
                                    scores(ph, ahead, g_ahead, 2 * k + half)
                                if kt is not None:
                                    scores_T(ph, bt, g, kt, half)
                            if kt is not None and not (first and g == 0):
                                values(ph, past, g_past, kt)
                            what = table.get((g, k))
                            if what == "MT":
                                if not (last and g == 3):
                                    maxima_T(ph, nxt, g_nxt)
                            elif what in ("XT", "Q", "K", "V"):
                                if not last:
                                    misc(what, ph, bt + 1)
                            elif what and not first:
                                misc(what, ph, bt + -1)

                def loop_body(bt, first, last):
                    misc_reader[0] = ("mt_read", cnt.at("mt_read", ph, bt, 0))
                    body(bt, first, last)

                batches(pe, loop_body)
                end = Batch(B // 2 - 1, 1)
                for kt in range(ATT[ph]["nk"] // 128):
                    values(ph, end, NG - 1, kt)
                for what in ("AVT0", "AVT1", "ONT", "O"):
                    misc(what, ph, end)

            def turn_block(ph, blk):
                wait(pe, "xn_done", cnt.at("xn_done", ph, blk))
                for q in range(TB):
                    mm = pe.transpose(ps_m[:, 128 * q:128 * (q + 1)], xf[:, q, :], ident[:, :])
                mm.then_inc(sig["fxt_ready"], 1)

            def quantised_ffn():
                ph = "F0"
                pe.wait_ge(col_absmax, 1)
                for c in range(4):
                    mm = pe.matmul(ps_av[:, c:c + 1], awq[0:1, 128 * c:128 * (c + 1)], ones_row[:, 0:1], start=True, stop=True)
                mm.then_inc(w_cols, 1)

                def hidden(blk):
                    wait(pe, "fxt_read", cnt.at("fxt_read", ph, blk) - 1)
                    turn_block(ph, blk)
                    wait(pe, "fxt_read", cnt.at("fxt_read", ph, blk))
                    for c in range(4):
                        wait(pe, "h_done", cnt.at("h_done", ph, blk, c) - 4)
                        pe.matmul(ps_h[c][:, :], w_ffn[:, 128 * c:128 * (c + 1)],
                                  xfT[:, :], start=True, stop=True).then_inc(sig["h_ready"], 1)

                blocks(pe, NBLK, hidden)

                def output(blk, p):
                    hq = w_ffn[:, 1024 + 2048 * p:1024 + 2048 * (p + 1)].rearrange("p (c s) -> p c s", c=4)
                    wait(pe, "hq_done", cnt.at("hq_done", ph, blk))
                    wait(pe, "x_new", cnt.at("x_new", ph, blk) - 2)
                    for q in range(TB):
                        for c in range(4):
                            mm = pe.matmul(ps_s[p][:, 128 * q:128 * (q + 1)], hq[:, c, 128 * q:128 * (q + 1)],
                                           w_ffn[:, 512 + 128 * c:512 + 128 * (c + 1)], start=(c == 0), stop=(c == 3))
                    mm.then_inc(sig["y_ready"], 1)

                with pe.Fori(0, NBLK, 2) as blk:
                    output(blk, 0)
                    output(blk + 1, 1)

            def experts(ph):
                ne = 9 if ph == "F1" else 8
                nc_h = 2 if ph == "F2" else 4
                gi = {"F1": 0, "F2": 1, "F3": 2}[ph]
                w2_at = {"F1": 4608, "F2": 4096, "F3": 4096}[ph]

                def first_product(blk, e):
                    for c in range(4):
                        if ph == "F2":
                            src = 2048 * (c // 2) + 256 * e + 128 * (c % 2)
                            free = ("h_done" if c < 2 else "g_done", 2 * e + c % 2, 2)
                        else:
                            src = 512 * e + 128 * c
                            free = ("h_done", 4 * e + c, 4)
                        wait(pe, free[0], cnt.at(free[0], ph, blk, free[1]) - free[2])
                        pe.matmul(ps_h[c][:, :], w_ffn[:, src:src + 128],
                                  xfT[:, :], start=True, stop=True).then_inc(sig["h_ready"], 1)

                def second_product(blk, n, e):
                    wait(pe, "acc_done", cnt.at("acc_done", ph, blk, n) - (1 if n == 0 and ph != "F2" else 2))
                    bias = n == E
                    if bias:
                        wait(pe, "ct_read", cnt.at("ct_read", ph, blk))
                    if e is not None:
                        name, at = ("g_done", 2 * e + 1) if ph == "F2" else ("h_done", 4 * e + 3)
                        wait(pe, name, cnt.at(name, ph, blk, at))
                        h = prob[:, e % 2, :, :].rearrange("p c s -> p (c s)")[:, 0:2048].rearrange("p (c s) -> p c s", c=4)
                    for q in range(TB):
                        dst = ps_s[n % 2][:, 128 * q:128 * (q + 1)]
                        if bias:
                            mm = pe.matmul(dst, combT[:, 128 * q:128 * (q + 1)] if ph == "F1" else combT[0:E, 128 * q:128 * (q + 1)],
                                           b2r[:, :] if ph == "F1" else b2r[0:E, :], start=True, stop=e is None)
                        for c in range(nc_h if e is not None else 0):
                            w2c = w_ffn[:, w2_at + 128 * (nc_h * e + c):w2_at + 128 * (nc_h * e + c + 1)]
                            mm = pe.matmul(dst, h[:, c, 128 * q:128 * (q + 1)], w2c,
                                           start=(c == 0 and not bias), stop=(c == nc_h - 1))
                    mm.then_inc(sig["y_ready"], 1)

                def body(blk, last):
                    wait(pe, "fxt_read", cnt.at("fxt_read", ph, blk))
                    wait(pe, "lg_read", cnt.at("lg_read", ph, blk) - 1)
                    for q in range(TB):
                        mm = pe.matmul(ps_av[:, E * q:E * (q + 1)], xfT[:, 128 * q:128 * (q + 1)], gate[:, gi, :], start=True, stop=True)
                    mm.then_inc(sig["lg_ready"], 1)
                    first_product(blk, 0)
                    for e in range(ne):
                        if e + 1 < ne:
                            first_product(blk, e + 1)
                        if e == 5 and ph != "F2":
                            wait(pe, "comb_done", cnt.at("comb_done", ph, blk))
                            for q in range(TB):
                                mm = pe.transpose(ps_av[0:E + 1, 128 * q:128 * (q + 1)], comb[:, q, :], ident[:, :])
                            mm.then_inc(sig["ct_ready"], 1)
                        second_product(blk, e, e)
                        if e == 4 and not last:
                            turn_block(ph, blk + 1)
                    if ph == "F3":
                        second_product(blk, E, None)

                pe.wait_ge(w_in[ph], W_PARTS[ph] * 16)
                turn_block(ph, 0)
                blocks(pe, NBLK - 1, lambda blk: body(blk, False))
                body(NBLK - 1, True)

            pe.wait_ge(setup_pool, 2)
            pe.wait_ge(loaded, 16 * N_LOADED)
            pe.wait_ge(bd_loaded, 16 * 3 * H)
            for ph in PHASES:
                if ph in ATT:
                    attention(ph)
                elif ph == "F0":
                    quantised_ffn()
                else:
                    experts(ph)

        @block.vector
        def _(dve):
            link = Links(dve, dve_chain)

            def tile_of(buf, b, q):
                return buf[:, bass.ds(b * QT + q, 1), :].rearrange("p o d -> p (o d)")

            def variances(srcs, st, m, v, eps, done):
                apart(dve)
                for q, s in enumerate(srcs):
                    ins = dve.bn_stats(st[:, q, :], s)
                    if q == len(srcs) - 1:
                        link(ins, apart)
                for q in range(len(srcs)):
                    ins = dve.bn_aggr(m[:, q, :], st[:, q, :])
                    if q == len(srcs) - 1:
                        link(ins)
                dve.tensor_scalar(v, m[:, 0:len(srcs), 1], eps, None, ALU.add).then_inc(sig[done], 1)

            def normalise(srcs, dsts, m, r):
                for q, (s, d) in enumerate(zip(srcs, dsts)):
                    ins = dve.tensor_scalar(d, s, m[:, q, 0:1], r[:, q:q + 1], ALU.subtract, ALU.mult)
                return ins

            def ln_variances(ph, bt, k):
                if k:
                    wait(dve, "y_done", cnt.at("y_done", ph, bt))
                else:
                    wait(dve, "xn_done", cnt.at("xn_done", ph, bt) - 1)
                apart(dve)
                src = y_tok if k else x_tok
                variances([tile_of(src, bt.b, q) for q in range(QT)], st6, mv, veps[:, 0, 0:QT], EPS, "var_done")

            def lay_v(ph, bt):
                p, nkt = bt.parity, ATT[ph]["nk"] // 128
                wait(dve, "v_ready", cnt.at("v_ready", ph, bt))
                src = ps_m[:, 0:128 * nkt].rearrange("p (k h d) -> p k h d", k=nkt, h=H)
                dst = vaug[p][:, 0:nkt, :, 0:DH]
                if ph in bv_att:
                    bias = bv_att[ph][:, :].rearrange("p (o h d) -> p o h d", o=1, h=H).to_broadcast([128, nkt, H, DH])
                    dve.tensor_tensor(dst, src, bias, ALU.add).then_inc(sig["v_read"], 1)
                else:
                    dve.tensor_copy(dst, src).then_inc(sig["v_read"], 1)

            def maximum(ph, bt, g, i):
                nk, mask, q, buf = ATT[ph]["nk"], ATT[ph]["mask"], i % 2, g % 2
                if i == 0:
                    wait(dve, "msplit", cnt.at("msplit", ph, bt, g) - 2)
                wait(dve, "s_ready", cnt.at("s_ready", ph, bt, 8 * g + i))
                if ph == "AS":
                    nk = 128 * (q + 1)
                src = ps_s[TURN[i]][:, 0:nk]
                if mask is None:
                    dve.tensor_reduce(mx[:, buf, i:i + 1], src, AX.X, ALU.max).then_inc(sig["max_done"], 1)
                    return
                if mask == "keys":
                    if g == 0 and i == 0:
                        wait(dve, "mask_conv", cnt.at("mask_conv", ph, bt))
                    m = mrow[:, bt.parity, :]
                else:
                    m = (mask_q if mask == "full" else caus_q)[:, q, 0:nk]
                apart(dve)
                dve.tensor_tensor_reduce(junk[:, TURN[i], 0:nk], src, m, 1.0, -3.0e38, ALU.add, ALU.max, mx[:, buf, i:i + 1])\
                   .then_inc(sig["max_done"], 1)

            def misc(what, ph, bt):
                if what in ("AVT0", "AVT1"):
                    q = int(what[-1])
                    wait(dve, "avt_ready", cnt.at("avt_ready", ph, bt, q))
                    src = ps_m[:, :].rearrange("p (h r) -> p h r", h=H)
                    link(dve.reciprocal(rsum[:, :].rearrange("p (h o) -> p h o", o=1), src[:, :, DH:DH + 1]))
                    dve.tensor_tensor(o_n[:, q, :].rearrange("p (h d) -> p h d", h=H), src[:, :, 0:DH],
                                      rsum[:, :].rearrange("p (h o) -> p h o", o=1).to_broadcast([128, H, DH]), ALU.mult)\
                       .then_inc(sig["on_done"], 1)
                elif what == "O":
                    wait(dve, "o_ready", cnt.at("o_ready", ph, bt))
                    dst = (y_tok if ph == "AS" else x_tok)[:, bass.ds(bt.b * QT, QT), :]
                    dve.tensor_tensor(dst, ps_m[:, 0:S].rearrange("p (q d) -> p q d", q=QT), dst, ALU.add).then_inc(sig["x_new"], 1)

            def attention(ph):
                n_ln = 2 if ph == "AS" else 1
                b0 = Batch(0, 0)
                wait(dve, "x_new", cnt.start("x_new", ph))
                for k in range(n_ln):
                    ln_variances(ph, b0, k)
                lay_v(ph, b0)
                for g in range(2):
                    for i in range(8):
                        maximum(ph, b0, g, i)
                table = slots(ph)

                def body(bt, first, last):
                    for g in range(NG):
                        ahead, g_ahead = later(bt, g, 2)
                        for k in range(4):
                            if not last and g == 0 and k < n_ln:
                                ln_variances(ph, bt + 1, k)
                            if not (last and g >= 2):
                                maximum(ph, ahead, g_ahead, 2 * k)
                                maximum(ph, ahead, g_ahead, 2 * k + 1)
                            what = table.get((g, k))
                            if what == "V" and not last:
                                lay_v(ph, bt + 1)
                            elif what in ("AVT0", "AVT1", "O") and not first:
                                misc(what, ph, bt + -1)

                batches(dve, body, link, LINKS[ph])
                end = Batch(B // 2 - 1, 1)
                for what in ("AVT0", "AVT1", "O"):
                    misc(what, ph, end)

            def block_tiles(buf, blk):
                return [buf[:, bass.ds(blk * TB + q, 1), :].rearrange("p o d -> p (o d)") for q in range(TB)]

            def rounded(dst, src, scale):
                link(dve.tensor_scalar(dst, src, scale, -A16 - 1.0, ALU.mult, ALU.max))
                link(dve.tensor_scalar(dst, dst, A16, ROUND, ALU.min, ALU.add))
                return dve.tensor_scalar(dst, dst, ROUND, None, ALU.subtract)

            def quantised_ffn():
                ph = "F0"
                hid = prob[:, :, :, :].rearrange("p a c s -> p (a c s)").rearrange("p (c s) -> p c s", c=4)
                w1, w2w = w_ffn[:, 0:512], w_ffn[:, 512:1024]
                w2v = w2w.rearrange("p (c d) -> p c d", c=4)
                dve.wait_ge(w_in["F0"], 48)
                dve.wait_ge(col_absmax, 1)
                dve.wait_ge(w_cols, 1)
                link(dve.tensor_scalar(svec[:, 0:4], ps_av[:, 0:4], 1e-8, 1.0 / A8, ALU.max, ALU.mult))
                link(dve.tensor_scalar(awq[:, :], awq[:, :], 1e-8, None, ALU.max))
                link(dve.reciprocal(awq[:, :], awq[:, :]))
                link(dve.tensor_scalar(awq[:, :], awq[:, :], A8, None, ALU.mult))
                link(dve.tensor_tensor(w1, w1, awq[:, :], ALU.mult))
                link(dve.tensor_scalar(w1, w1, ROUND, ROUND, ALU.add, ALU.subtract))
                link(dve.tensor_scalar(w1, w1, -A8 - 1.0, A8, ALU.max, ALU.min))
                link(dve.tensor_reduce(awo[:, 0, :], w2v, AX.X, ALU.max, apply_absolute_value=True))
                link(dve.tensor_scalar(awo[:, 0, :], awo[:, 0, :], 1e-8, None, ALU.max))
                link(dve.reciprocal(awo[:, 1, :], awo[:, 0, :]))
                link(dve.tensor_scalar(awo[:, 1, :], awo[:, 1, :], A8, None, ALU.mult))
                link(dve.tensor_tensor(w2v, w2v, awo[:, 1, :].rearrange("p (c o) -> p c o", o=1).to_broadcast([128, 4, D]), ALU.mult))
                link(dve.tensor_scalar(w2w, w2w, ROUND, ROUND, ALU.add, ALU.subtract))
                link(dve.tensor_scalar(w2w, w2w, -A8 - 1.0, A8, ALU.max, ALU.min))
                link(dve.tensor_scalar(awo[:, 0, :], awo[:, 0, :], 1.0 / A8, None, ALU.mult))
                link(dve.tensor_tensor(w2v, w2v, awo[:, 0, :].rearrange("p (c o) -> p c o", o=1).to_broadcast([128, 4, D]), ALU.mult))
                link(dve.memset(amx[:, :], 0.0))

                def norm(blk):
                    variances(block_tiles(x_tok, blk), st6, mv, veps[:, 0, :], EPS, "var_done")
                    wait(dve, "rstd_done", cnt.at("rstd_done", ph, blk))
                    link(normalise(block_tiles(x_tok, blk), block_tiles(y_tok, blk), mv, rstd[:, 0, :]), apart)
                    link(dve.tensor_reduce(amx[:, 2:3], y_tok[:, bass.ds(blk * TB, TB), :], AX.XY, ALU.max, apply_absolute_value=True))
                    link(dve.tensor_tensor(amx[:, 0:1], amx[:, 0:1], amx[:, 2:3], ALU.max))

                blocks(dve, NBLK, norm, link, 5)
                dve.tensor_copy(amx[:, 3:4], amx[:, 0:1]).then_inc(max_given, 1)

                def step(i):
                    dve.wait_ge(max_all, i + 1)
                    link(dve.tensor_scalar(aall[:, 2:3], aall[:, i:i + 1], 1e-8, None, ALU.max))
                    link(dve.reciprocal(svec[:, 4:5], aall[:, 2:3]))
                    link(dve.tensor_scalar(svec[:, 4:5], svec[:, 4:5], A16, None, ALU.mult))
                    link(dve.tensor_scalar(svec[:, 5:6], aall[:, 2:3], 1.0 / A16, None, ALU.mult))

                step(0)
                dve.tensor_scalar(svec[:, 0:4], svec[:, 0:4], svec[:, 5:6], None, ALU.mult).then_inc(svec_done, 1)

                def quantise_x(blk):
                    wait(dve, "fxt_ready", cnt.at("fxt_ready", ph, blk) - 1)
                    rounded(xf[:, :, :], y_tok[:, bass.ds(blk * TB, TB), :], svec[:, 4:5]).then_inc(sig["xn_done"], 1)
                    wait(dve, "fxt_ready", cnt.at("fxt_ready", ph, blk))
                    wait(dve, "h_ready", cnt.at("h_ready", ph, blk, -1))
                    dve.tensor_copy(xfT[:, :], ps_m[:, :]).then_inc(sig["fxt_read"], 1)

                blocks(dve, NBLK, quantise_x, link, 2)
                wait(dve, "h_done", cnt.at("h_done", ph, NBLK - 1, 3))
                for c in range(4):
                    link(dve.tensor_reduce(amx[:, 4 + c:5 + c], hid[:, c, :], AX.X, ALU.max, apply_absolute_value=True))
                dve.tensor_reduce(amx[:, 1:2], amx[:, 4:8], AX.X, ALU.max).then_inc(max_given, 1)
                step(1)

                def quantise_h(blk, p):
                    hq = w_ffn[:, 1024 + 2048 * p:1024 + 2048 * (p + 1)].rearrange("p (c s) -> p c s", c=4)
                    wait(dve, "y_ready", cnt.at("y_ready", ph, blk) - 2)
                    rounded(hq, hid[:, :, bass.ds(blk * 512, 512)], svec[:, 4:5]).then_inc(sig["hq_done"], 1)

                def add(blk, p):
                    wait(dve, "y_ready", cnt.at("y_ready", ph, blk))
                    wait(dve, "x_new", cnt.at("x_new", ph, blk) - 1)
                    dst = x_tok[:, bass.ds(blk * TB, TB), :]
                    link(dve.scalar_tensor_tensor(out=acc[:, :, :], in0=ps_s[p][:, :].rearrange("p (q d) -> p q d", q=TB), scalar=svec[:, 5:6],
                                                  in1=boutb[:, :].rearrange("p (o d) -> p o d", o=1).to_broadcast([128, TB, D]),
                                                  op0=ALU.mult, op1=ALU.add))
                    dve.tensor_tensor(dst, dst, acc[:, :, :], ALU.add).then_inc(sig["x_new"], 1)

                with dve.Fori(0, NBLK // 2) as i:
                    link.enter(i, 6)
                    quantise_h(i * 2, 0)
                    quantise_h(i * 2 + 1, 1)
                    add(i * 2, 0)
                    add(i * 2 + 1, 1)
                link.leave(NBLK // 2)

            def experts(ph):
                ne = 9 if ph == "F1" else 8
                src_of = y_tok if ph == "F2" else x_tok
                gb = {"F1": 0, "F2": None, "F3": 1}[ph]

                def norm_variances(blk):
                    variances(block_tiles(src_of, blk), st6, mv, veps[:, 0, :], EPS, "var_done")

                def norm(blk):
                    wait(dve, "rstd_done", cnt.at("rstd_done", ph, blk))
                    wait(dve, "fxt_ready", cnt.at("fxt_ready", ph, blk) - 1)
                    ins = normalise(block_tiles(src_of, blk), [xf[:, q, :] for q in range(TB)], mv, rstd[:, 0, :])
                    ins.then_inc(sig["xn_done"], 1)
                    if ph == "F3":
                        wait(dve, "xn_done", cnt.at("xn_done", ph, blk))
                        dve.tensor_copy(y_tok[:, bass.ds(blk * TB, TB), :], xf[:, :, :])

                def gates(blk):
                    wait(dve, "lg_ready", cnt.at("lg_ready", ph, blk))
                    logits = ps_av[:, 0:TB * E].rearrange("p (q e) -> p q e", q=TB)
                    if gb is None:
                        link(dve.tensor_copy(lg[:, :, :], logits), apart)
                    else:
                        link(dve.tensor_tensor(lg[:, :, :], logits, gate_bb[:, gb:gb + 1, :].to_broadcast([128, TB, E]), ALU.add), apart)
                    for q in range(TB):
                        ins = dve.max(top[:, q, :], lg[:, q, :])
                    link(ins, apart)
                    for q in range(TB):
                        ins = dve.max_index(topi[:, q, :], top[:, q, :], lg[:, q, :])
                    link(ins)
                    dve.tensor_tensor(dlt[:, :], top[:, :, 1], top[:, :, 0], ALU.subtract).then_inc(sig["lg_read"], 1)
                    link(dve.tensor_copy(topf[:, :, :], topi[:, :, 0:2]))
                    for n in range(2):
                        ins = dve.tensor_tensor(eq[:, n, :, :], iota_e[:, :].rearrange("p (o e) -> p o e", o=1).to_broadcast([128, TB, E]),
                                                topf[:, :, n:n + 1].to_broadcast([128, TB, E]), ALU.is_equal)
                    wait(dve, "th_done", cnt.at("th_done", ph, blk))
                    dve.tensor_scalar(w2[:, 0, :], th[:, :], -0.5, 0.5, ALU.mult, ALU.add)
                    link(dve.tensor_scalar(w2[:, 1, :], th[:, :], 0.5, 0.5, ALU.mult, ALU.add))
                    for n in range(2):
                        ins = dve.tensor_tensor(eq[:, n, :, :], eq[:, n, :, :],
                                                w2[:, n, :].rearrange("p (q o) -> p q o", o=1).to_broadcast([128, TB, E]), ALU.mult)
                    link(ins)
                    dve.tensor_tensor(comb[:, :, 0:E], eq[:, 0, :, :], eq[:, 1, :, :], ALU.add).then_inc(sig["comb_done"], 1)
                    wait(dve, "comb_done", cnt.at("comb_done", ph, blk))

                def gated(blk, e):
                    h = prob[:, e % 2, :, :].rearrange("p c s -> p (c s)")[:, 0:2048].rearrange("p (c s) -> p c s", c=4)
                    wait(dve, "h_ready", cnt.at("h_ready", ph, blk, 4 * e + 3))
                    for c in range(2):
                        wait(dve, "h_done", cnt.at("h_done", ph, blk, 2 * e + c))
                        dve.tensor_tensor(h[:, c, :], ps_h[2 + c][:, :], h[:, 2 + c, :], ALU.mult).then_inc(sig["g_done"], 1)

                def accumulate(blk, n):
                    wait(dve, "y_ready", cnt.at("y_ready", ph, blk, n))
                    if n:
                        wait(dve, "acc_done", cnt.at("acc_done", ph, blk, n) - 1)
                    if n == E:
                        dve.tensor_tensor(acc[:, :, :], ps_s[n % 2][:, :].rearrange("p (q d) -> p q d", q=TB), acc[:, :, :], ALU.add)\
                           .then_inc(sig["acc_done"], 1)
                        return
                    for q in range(TB):
                        src = ps_s[n % 2][:, 128 * q:128 * (q + 1)]
                        if n == 0:
                            ins = dve.tensor_scalar(acc[:, q, :], src, comb[:, q, 0:1], None, ALU.mult)
                        else:
                            ins = dve.scalar_tensor_tensor(out=acc[:, q, :], in0=src, scalar=comb[:, q, n:n + 1], in1=acc[:, q, :],
                                                           op0=ALU.mult, op1=ALU.add)
                    ins.then_inc(sig["acc_done"], 1)

                def result(blk, n_last):
                    dst = x_tok[:, bass.ds(blk * TB, TB), :]
                    inner = y_tok[:, bass.ds(blk * TB, TB), :]
                    wait(dve, "acc_done", cnt.at("acc_done", ph, blk, n_last))
                    if ph != "F1":
                        link(dve.tensor_tensor(acc[:, :, :], acc[:, :, :], inner, ALU.add))
                    if ph == "F3":
                        tiles = [acc[:, q, :] for q in range(TB)]
                        variances(tiles, st6b, mvb, veps[:, 1, :], 1e-12, "var2_done")
                        wait(dve, "rstd2_done", cnt.at("rstd2_done", ph, blk))
                        link(normalise(tiles, tiles, mvb, rstd[:, 1, :]))
                        for i, op in enumerate((ALU.mult, ALU.add)):
                            link(dve.tensor_tensor(acc[:, :, :], acc[:, :, :], lnw[:, i:i + 1, :].to_broadcast([128, TB, D]), op))
                    dve.tensor_tensor(dst, dst, acc[:, :, :], ALU.add).then_inc(sig["x_new"], 1)

                def body(blk, last):
                    gates(blk)
                    if ph == "F2":
                        gated(blk, 0)
                    for e in range(ne):
                        if ph == "F2" and e + 1 < ne:
                            gated(blk, e + 1)
                        if e == 5 and ph != "F2":
                            wait(dve, "ct_ready", cnt.at("ct_ready", ph, blk))
                            dve.tensor_copy(combT[:, :], ps_av[0:E + 1, :]).then_inc(sig["ct_read"], 1)
                        accumulate(blk, e)
                        if not last and e == 2:
                            norm_variances(blk + 1)
                        if not last and e == 3:
                            norm(blk + 1)
                    if ph == "F3":
                        accumulate(blk, E)
                    result(blk, E if ph != "F2" else E - 1)

                wait(dve, "x_new", cnt.start("x_new", ph))
                norm_variances(0)
                norm(0)
                blocks(dve, NBLK - 1, lambda blk: body(blk, False), link, LINKS[ph])
                body(NBLK - 1, True)

            dve.wait_ge(setup_pool, 2)
            dve.wait_ge(loaded, 16 * N_LOADED)
            for a in ("A0", "A1", "A2"):
                dve.tensor_scalar(b_att[a][:, 0:1], b_att[a][:, 0:1], ATT[a]["scale"], None, ALU.mult).then_inc(bias_scaled, 1)
            dve.tensor_scalar(mask_q[:, :, :], prob[:, 1, 0, :].bitcast(I32).rearrange("p (c k) -> p c k", c=2), 0.0, MASKED, ALU.is_equal, ALU.mult)
            link(dve.tensor_scalar(mask_T[:, :, :], prob[:, 1, 1, :].bitcast(I32).rearrange("p (c q) -> p c q", c=4), 0.0, MASKED, ALU.is_equal, ALU.mult))
            dve.memset(junk[:, :, :], 0.0)
            for name, n in cnt.credit.items():
                dve.sem_inc(sig[name], n)
            dve.wait_ge(x_loaded, 16)
            for ph in PHASES:
                if ph in ATT:
                    attention(ph)
                elif ph == "F0":
                    quantised_ffn()
                else:
                    experts(ph)




def kernel(**inputs):
    import numpy as np

    import concourse.bacc as bacc
    from concourse import mybir as mb
    from concourse.bass_utils import run_bass_kernel_spmd

    a = {k: np.asarray(v) for k, v in inputs.items()}
    c = np.ascontiguousarray
    t = {
        "x": a["x"],
        "ctxT": c(a["ctx_1024"].transpose(0, 2, 1)),
        "mask_q": c(a["mask_1x1xSxS2_ik0"][0, 0]),
        "mask_T": c(a["mask_1x1xSxS2_ik0"][0, 0].T),
        "mask_k": c(a["mask_Bx1x1xS2_if1"][:, 0, 0]),
        "mask_kT": c(a["mask_Bx1x1xS2_if1"][:, 0, 0].reshape(8, 4, 128).transpose(0, 2, 1)),
        "ln1_scale": a["L2_ffn_ln1_scale"], "ln1_shift": a["L2_ffn_ln1_shift"],
        "ln2_scale": a["L2_ffn_ln2_scale"], "ln2_shift": a["L2_ffn_ln2_shift"],
        "ln_w": a["L3_ffn_ln_w"], "ln_b": a["L3_ffn_ln_b"],
        "F0_w1": a["L0_ffn_W_in"], "F0_b1": c(a["L0_ffn_b_in"].reshape(4, 128).T),
        "F0_w2": a["L0_ffn_W_out"], "F0_b2": a["L0_ffn_b_out"],
        "F1_gate": a["L1_ffn_gate_w"], "F1_gate_b": a["L1_ffn_gate_b"],
        "F1_w1": a["L1_ffn_w1"], "F1_b1": c(a["L1_ffn_b1"].reshape(8, 4, 128).transpose(2, 0, 1).reshape(128, 32)),
        "F1_w2": a["L1_ffn_w2"], "F1_b2": a["L1_ffn_b2"],
        "F1_ws1": a["L1_ffn_ws1"], "F1_bs1": c(a["L1_ffn_bs1"].reshape(4, 128).T),
        "F1_ws2": a["L1_ffn_ws2"], "F1_bs2": a["L1_ffn_bs2"],
        "F2_gate": a["L2_ffn_gate_w"], "F2_w1": a["L2_ffn_w1"], "F2_w2": a["L2_ffn_w2"], "F2_w3": a["L2_ffn_w3"],
        "F3_gate": c(a["L3_ffn_Wr"].T), "F3_gate_b": a["L3_ffn_br"],
        "F3_w1": c(a["L3_ffn_W1"].transpose(0, 2, 1)),
        "F3_b1": c(a["L3_ffn_b1"].reshape(8, 4, 128).transpose(2, 0, 1).reshape(128, 32)),
        "F3_w2": c(a["L3_ffn_W2"].transpose(0, 2, 1)), "F3_b2": a["L3_ffn_b2"],
    }
    for ph, pre in (("A0", "L0_xattn_w{}"), ("A1", "L1_xattn_w{}"), ("A2", "L2_xattn_W{}_w")):
        for w in "qkvo":
            t[f"{ph}_{w}"] = c(a[pre.format(w)].T)
    for ph, pre in (("A0", "L0_xattn_b{}"), ("A1", "L1_xattn_b{}"), ("A2", "L2_xattn_W{}_b")):
        for w in "qkvo":
            t[f"{ph}_b{w}"] = a[pre.format(w)]
    for w in "qkvo":
        t[f"AS_{w}"] = a[f"L2_ffn_w{w}"]
    t["AS_bo"] = a["L2_ffn_bo"]
    for w in "qkv":
        t[f"A3_{w}"] = c(a[f"L3_xattn_W{w}"].T)
    t["A3_o"], t["A3_bo"] = c(a["L3_xattn_Wo"].T), a["L3_xattn_bo"]

    nc = bacc.Bacc("TRN2", target_bir_lowering=False, num_devices=1)
    arrays = {f"in_{n}": np.ascontiguousarray(v) for n, v in t.items()}
    aps = {n: nc.dram_tensor(f"in_{n}", v.shape, mb.dt.from_np(v.dtype), kind="ExternalInput").ap() for n, v in
           ((n[3:], v) for n, v in arrays.items())}
    out = nc.dram_tensor("out_x", (8, 256, 128), mb.dt.float32, kind="ExternalOutput").ap()
    build(nc, aps, out)
    r = run_bass_kernel_spmd(nc, [arrays], core_ids=[0])
    return r.results[0]["out_x"]
```

```python
from contextlib import ExitStack

import concourse.bass as bass
from concourse import mybir

F32 = mybir.dt.float32
F32R = mybir.dt.float32r
BF16 = mybir.dt.bfloat16
I32 = mybir.dt.int32
U32 = mybir.dt.uint32
ALU = mybir.AluOpType
ACT = mybir.ActivationFunctionType
AX = mybir.AxisListType

B, S, D, SK = 8, 256, 128, 512
H, DH = 16, 8
NT = B * S // 128
QT = S // 128
HG = 4
ROWS = 3 * DH
NG = H // HG
TB = 4
NBLK = NT // TB
E = 8
MASKED = -float(2 ** 100)
ROUND = 1.5 * 2 ** 23
A8, A16 = 127.0, 32767.0
EPS = 1e-5

ATT = {
    "A0": dict(nk=SK, scale=DH ** -0.5, mask=None),
    "A1": dict(nk=SK, scale=DH ** -0.5, mask=None),
    "A2": dict(nk=SK, scale=DH ** -0.5, mask="full"),
    "AS": dict(nk=S, scale=DH ** -0.5, mask="causal"),
    "A3": dict(nk=SK, scale=D ** -0.5, mask="keys"),
}
TURN = [0, 1, 2, 0, 1, 2, 0, 1]
BACK = [2, 2, 5, 3, 3, 3, 3, 3]
PHASES = ["A0", "F0", "A1", "F1", "A2", "AS", "F2", "A3", "F3"]


def att_counts(ph):
    nkt = ATT[ph]["nk"] // 128
    stats = 2 if ph == "A2" else 1
    return dict(
        s_ready=8 * NG, st_ready=2 * nkt * NG, av_ready=nkt * NG, mt_ready=NG, xt_ready=1, q_ready=1,
        k_ready=1, v_ready=1, avt_ready=2, ont_ready=1, o_ready=1,
        exp_done=2 * nkt * NG, mt_read=NG, xt_read=1, q_read=1, k_read=1,
        max_done=8 * NG, msplit=NG, av_read=NG, v_read=1, on_done=2, ont_read=1, x_new=1,
        var_done=stats, xn_done=1, kh_done=1, ql_done=1,
        rstd_done=stats, mask_conv=1 if ph == "A3" else 0,
    )


def ffn_counts(ph):
    if ph == "F0":
        return dict(var_done=1, rstd_done=1, xn_done=1, fxt_ready=1, fxt_read=1, h_ready=4, h_done=4,
                    hq_done=1, y_ready=1, x_new=1)
    shared = ph == "F1"
    n = E + (ph != "F2")
    ne = E + shared
    return dict(
        var_done=int(ph != "F3"), rstd_done=int(ph != "F3"), xn_done=1, fxt_ready=1,
        fxt_read=1, lg_ready=1, lg_read=1, th_done=1, comb_done=1,
        h_ready=4 * ne, h_done=4 * ne if ph != "F2" else 2 * ne, g_done=2 * ne if ph == "F2" else 0,
        wh_done=ne, wl_done=ne, xl_done=1,
        y_ready=n, acc_done=n, ct_ready=int(ph != "F2"), ct_read=int(ph != "F2"), x_new=1,
        var2_done=int(ph == "F3"), rstd2_done=int(ph == "F3"),
    )


N_FIRST = 8
N_LOADED = 5 + 6 + 4 + 4 + 3 + 2 + 2 + 1 + 2
W_PARTS = {"F0": 3, "F1": 15, "F2": 10, "F3": 11}
LINKS = {'A0': 14, 'A1': 8, 'A2': 14, 'AS': 8, 'A3': 8, 'F1': 8, 'F2': 9, 'F3': 12}
POOL_LINKS = {'A0': 32, 'A1': 32, 'A2': 32, 'AS': 32, 'A3': 32}


class Counts:

    def __init__(self):
        self.credit = {"var_done": NBLK, "rstd_done": NBLK, "acc_done": 2, "g_done": 2, "y_ready": 2,
                       "h_done": 4, "h_ready": 1, "fxt_ready": 1, "fxt_read": 1, "lg_read": 1, "o_ready": 1}
        self.per, self.base, total = {}, {}, dict(self.credit)
        for ph in PHASES:
            self.per[ph] = att_counts(ph) if ph in ATT else ffn_counts(ph)
            self.base[ph] = dict(total)
            for name, n in self.per[ph].items():
                total[name] = total.get(name, 0) + n * (B if ph in ATT else NBLK)
        self.names = sorted(total)

    def start(self, name, ph):
        return self.base[ph].get(name, 0)

    def at(self, name, ph, b, k=0):
        b = b.b if isinstance(b, Batch) else b
        return self.base[ph].get(name, 0) + b * self.per[ph][name] + (k + 1)


class Batch:

    def __init__(self, i, off):
        self.i, self.off = i, off
        self.b, self.half, self.parity = i * 2 + off, i + off // 2, off % 2
        self.known = isinstance(i, int)

    def __add__(self, n):
        return Batch(self.i, self.off + n)


class Links:

    def __init__(self, eng, sem):
        self.eng, self.sem, self.n, self.loop = eng, sem, 0, None

    def __call__(self, ins, after=None):
        self.until(self.mark(ins), after)

    def mark(self, ins):
        self.n += 1
        ins.then_inc(self.sem, 1)
        return self.n

    def until(self, mark, after=None):
        value = mark if self.loop is None else self.loop[0] * self.loop[1] + mark
        self.eng.wait_ge(self.sem, value)
        if after:
            after(self.eng)

    def enter(self, i, per):
        self.loop, self.begin = (i, per), self.n

    def leave(self, turns):
        i, per = self.loop
        assert self.n - self.begin == per, ("links in the loop", self.n - self.begin, per)
        self.loop, self.n = None, self.begin + turns * per


def batches(eng, body, links=None, per=0):
    body(Batch(0, 0), True, False)
    with eng.Fori(0, B // 2 - 1) as i:
        if links:
            links.enter(i, per)
        body(Batch(i, 1), False, False)
        body(Batch(i, 2), False, False)
    if links:
        links.leave(B // 2 - 1)
    body(Batch(B // 2 - 1, 1), False, True)


def blocks(eng, n, body, links=None, per=0):
    with eng.Fori(0, n) as i:
        if links:
            links.enter(i, per)
        body(i)
    if links:
        links.leave(n)


def build(nc, t, out):
    cnt = Counts()
    with ExitStack() as ctx:
        def sb(name, shape, dt=F32):
            return ctx.enter_context(nc.sbuf_tensor(name, shape, dt))

        def sem(name):
            return ctx.enter_context(nc.semaphore(name))

        sig = {n: sem(n) for n in cnt.names}

        x_tok = sb("x_tok", [128, NT, D])
        y_tok = sb("y_tok", [128, NT, D])
        ctxT = sb("ctxT", [128, 2, SK])
        xn = sb("xn", [128, QT, D])
        xnT = sb("xnT", [128, S])
        qf = sb("qf", [128, S])
        q_hi = sb("q_hi", [128, S], F32R)
        q_lo = sb("q_lo", [128, S], F32R)
        kf = sb("kf", [128, SK])
        k_hi = sb("k_hi", [128, SK], F32R)
        k_lo = sb("k_lo", [128, SK], F32R)
        qz = [sb(f"qz{p}", [128, NG, HG, S], F32R) for p in range(2)]
        kst = [sb(f"kst{p}", [128, NG, SK], F32R) for p in range(2)]
        vaug = [sb(f"vaug{p}", [128, 4, H, 32]) for p in range(2)]
        prob = sb("prob", [128, 2, 4, HG * S])
        avs = sb("avs", [128, NG, S])
        o_n = sb("o_n", [128, QT, D])
        o_nT = sb("o_nT", [128, S])
        mx = sb("mx", [128, 2, 8])
        mrest = sb("mrest", [128, 2, 8])
        mpart = sb("mpart", [128, 2, 2, 128], BF16)
        rsum = sb("rsum", [128, H])
        junk = sb("junk", [128, 3, SK], BF16)
        st6 = sb("st6", [128, TB, 6])
        mv = sb("mv", [128, TB, 2])
        st6b = sb("st6b", [128, TB, 6])
        mvb = sb("mvb", [128, TB, 2])
        means = sb("means", [128, NT])
        veps = sb("veps", [128, NT])
        rstd = sb("rstd", [128, NT])
        vepsb = sb("vepsb", [128, TB])
        rstdb = sb("rstdb", [128, TB])
        neg_half = sb("neg_half", [128, TB])
        w_ffn = sb("w_ffn", [128, 9 * 1024])
        mask_q = sb("mask_q", [128, 2, SK])
        mask_T = sb("mask_T", [128, 4, S], BF16)
        caus_q = sb("caus_q", [128, 2, S])
        caus_T = sb("caus_T", [128, 2, S], BF16)
        mask_T_i = w_ffn[:, 6656:7680].bitcast(I32).rearrange("p (c q) -> p c q", c=4)
        mrow_i = caus_q[:, :, :].rearrange("p c k -> p (c k)").bitcast(I32)
        mrow = mask_q
        mcol_i = sb("mcol_i", [128, 4], I32)
        mcol = sb("mcol", [128, 2, 4])
        ident = sb("ident", [128, 128])
        ident_b = sb("ident_b", [128, 128], BF16)
        ones_row = sb("ones_row", [1, 128])
        iota_e = sb("iota_e", [128, E])
        w_att = {a: sb(f"w_{a}", [128, 4, 128]) for a in ("A0", "A1", "A3")}
        w_att |= {"A2": w_att["A0"], "AS": w_att["A1"]}
        b_att = {a: sb(f"b_{a}", [128, 2]) for a in ATT}
        bv_att = {a: sb(f"bv_{a}", [128, D]) for a in ("A0", "A1", "A2")}
        bo_att = {a: sb(f"bo_{a}", [1, D]) for a in ATT}
        ln_cols = sb("ln_cols", [128, 4])
        xf = avs[:, 0:2, :].rearrange("p g (q d) -> p (g q) d", d=D)
        acc = avs[:, 2:4, :].rearrange("p g (q d) -> p (g q) d", d=D)
        xfT = ctxT[:, 1, :]
        x_hi, x_lo = k_hi, k_lo
        w_parts = [(kst[p][:, n, :], kst[p][:, n + 1, :]) for p, n in ((1, 0), (1, 2), (0, 0))]
        gate = sb("gate", [128, 3, E])
        gate_bb = sb("gate_bb", [128, 2, E])
        lg = sb("lg", [128, TB, E])
        top = sb("top", [128, TB, E])
        topi = sb("topi", [128, TB, E], U32)
        topf = sb("topf", [128, TB, 2])
        dlt = sb("dlt", [128, TB])
        th = sb("th", [128, TB])
        w2 = sb("w2", [128, 2, TB])
        eq = sb("eq", [128, 2, TB, E])
        comb = sb("comb", [128, TB, E + 1])
        combT = kf[0:E + 1, :]
        b1c = sb("b1c", [128, 9 * 4])
        b2r = sb("b2r", [E + 1, D])
        lnw = sb("lnw", [128, 2, D])
        amx = sb("amx", [128, 8])
        aall = sb("aall", [128, 8])
        awq = w_ffn[:, 5120:5632]
        awo = sb("awo", [128, 2, 4])
        svec = sb("svec", [128, 8])
        boutb = sb("boutb", [128, D])

        ps_s = [ctx.enter_context(nc.psum_tensor(f"ps_s{i}", [128, 512], F32)) for i in range(3)]
        ps_t = [ctx.enter_context(nc.psum_tensor(f"ps_t{i}", [128, 512], F32)) for i in range(3)]
        ps_h = [*ps_t, ps_s[2]]
        ps_av = ctx.enter_context(nc.psum_tensor("ps_av", [128, 512], F32))
        ps_m = ctx.enter_context(nc.psum_tensor("ps_m", [128, 512], F32))
        ps_mb = ps_m[:, :].bitcast(BF16)

        scratch = {n: nc.dram_tensor(f"{n}_parts", (2, 3 * 128, w), F32).ap() for n, w in (("q", S), ("k", SK))}
        ctx_in = [sem(f"ctx_in{p}") for p in range(2)]
        q_saved = [sem(f"q_saved{p}") for p in range(2)]
        k_saved = [sem(f"k_saved{p}") for p in range(2)]
        q_stacked = [sem(f"q_stacked{p}") for p in range(2)]
        k_stacked = [sem(f"k_stacked{p}") for p in range(2)]
        mask_in = sem("mask_in")
        loaded_first = sem("loaded_first")
        loaded = sem("loaded")
        bd_loaded = sem("bd_loaded")
        watt_in = {a: sem(f"watt_in_{a}") for a in ("A2", "AS")}
        w_in = {ph: sem(f"w_in_{ph}") for ph in ("F0", "F1", "F2", "F3")}
        setup_pool = sem("setup_pool")
        pool_chain = sem("pool_chain")
        dve_chain = sem("dve_chain")
        col_absmax = sem("col_absmax")
        w_cols = sem("w_cols")
        max_given = sem("max_given")
        max_all = sem("max_all")
        svec_done = sem("svec_done")
        bias_scaled = sem("bias_scaled")
        x_loaded = sem("x_loaded")
        stored = sem("stored")
        apart_waits = sem("apart_waits")

        ATTS = [p for p in PHASES if p in ATT]

        def stacked(ph, bt, dmas):
            return 16 * dmas * (ATTS.index(ph) * (B // 2) + bt.half + 1)

        def saved(ph, bt):
            return 16 * 3 * (ATTS.index(ph) * (B // 2) + bt.half + 1)

        def context_in(ph, bt):
            n = sum(a != "AS" for a in ATTS[:ATTS.index(ph)])
            return 16 * (n * (B // 2) + bt.half + 1)

        def wait(eng, name, value):
            if not (isinstance(value, int) and value <= 0):
                eng.wait_ge(sig[name], value)

        def apart(eng):
            eng.sem_inc(apart_waits, 1)

        def seen(ph, kt):
            return 128 * kt if ph == "AS" else 0

        def turn_of(ph, g, kt, half):
            return (2 * (ATT[ph]["nk"] // 128 * g + kt) + half) % 8

        def slots(ph):
            s = {(g, 1, 1): "MT" for g in range(1, NG)}
            s[(0, 3, 0) if ph == "AS" else (0, 0, 0)] = "K"
            return s | {(0, 0, 1): "XT", (0, 1, 0): "Q", (0, 2, 0): "MT", (1, 2, 1): "AVT0", (1, 3, 1): "AVT1",
                        (2, 0, 1): "ONT", (2, 2, 1): "V", (2, 3, 1): "O"}

        def following(ph, bt, last):
            if not last:
                return ph, bt + 1
            return ("AS" if ph == "A2" else None), Batch(0, 0)

        def unit_after(ph, bt, last, g, n):
            return (ph, bt, g + n) if g + n < NG else (*following(ph, bt, last), g + n - NG)

        def later(bt, g, n):
            return bt + (g + n) // NG, (g + n) % NG

        def turns(ph):
            return (E + 1, 3) if ph == "F1" else (E, 2)

        def first_weights(ph, e):
            if ph == "F2":
                return w_ffn[:, 0:4096].rearrange("p (t e f) -> p t e f", t=2, e=E)[:, :, e, :]
            return w_ffn[:, 512 * e:512 * (e + 1)].rearrange("p (t f) -> p t f", t=2)

        def halves(buf):
            return buf.rearrange("p (t f) -> p t f", t=2)

        def kt_of(ph, k):
            if ATT[ph]["nk"] == SK:
                return k
            return k // 2 if k % 2 == 0 else None

        block = ctx.enter_context(nc.Block())

        @block.sync
        def _(sp):
            sp.dma_start(x_tok[:, :, :], t["x"].rearrange("b (q p) d -> p (b q) d", p=128)).then_inc(x_loaded, 16)

            def load_attention(a, done):
                for i, w in enumerate("qkvo"):
                    if a in ("A0", "A1") or a == "A3" and w == "o":
                        sp.dma_start(w_att[a][:, i, :], t[f"{a}_{w}"]).then_inc(done, 16)
                if a in bv_att:
                    for i, w in enumerate("qk"):
                        sp.dma_start(b_att[a][:, i:i + 1], t[f"{a}_b{w}"].rearrange("(d o) -> d o", o=1)).then_inc(done, 16)
                    sp.dma_start(bv_att[a][:, :], t[f"{a}_bv"].rearrange("(o d) -> o d", o=1).to_broadcast([128, D])).then_inc(done, 16)
                sp.dma_start(bo_att[a][:, :], t[f"{a}_bo"].rearrange("(o d) -> o d", o=1)).then_inc(done, 16)

            load_attention("A0", loaded_first)

            def load_rest():
                for a in ("A1", "A2", "AS", "A3"):
                    load_attention(a, loaded)
                for i, w in enumerate(("ln1_scale", "ln1_shift", "ln2_scale", "ln2_shift")):
                    sp.dma_start(ln_cols[:, i:i + 1], t[w].rearrange("(d o) -> d o", o=1)).then_inc(loaded, 16)
                for i, w in enumerate(("F1_gate", "F2_gate", "F3_gate")):
                    sp.dma_start(gate[:, i, :], t[w]).then_inc(loaded, 16)
                for i, w in enumerate(("F1_gate_b", "F3_gate_b")):
                    sp.dma_start(gate_bb[:, i, :], t[w].rearrange("(o e) -> o e", o=1).to_broadcast([128, E])).then_inc(loaded, 16)
                for i, w in enumerate(("ln_w", "ln_b")):
                    sp.dma_start(lnw[:, i, :], t[w].rearrange("(o e) -> o e", o=1).to_broadcast([128, D])).then_inc(loaded, 16)
                sp.dma_start(boutb[:, :], t["F0_b2"].rearrange("(o e) -> o e", o=1).to_broadcast([128, D])).then_inc(loaded, 16)
                sp.dma_start(mask_q[:, :, :].bitcast(I32), t["mask_q"].rearrange("(c p) k -> p c k", p=128)).then_inc(loaded, 16)
                sp.dma_start(mask_T_i, t["mask_T"].rearrange("(c p) q -> p c q", p=128)).then_inc(loaded, 16)
                sp.wait_ge(setup_pool, 1)
                for i, w in enumerate("qkv"):
                    for h in range(H):
                        sp.dma_start(w_att["A3"][DH * h:DH * h + DH, i, DH * h:DH * h + DH], t[f"A3_{w}"]).then_inc(bd_loaded, 16)

            def load_ffn(ph):
                if ph != "F0":
                    wait(sp, "y_ready", cnt.start("y_ready", ph))
                    wait(sp, "h_done", cnt.start("h_done", ph))
                done = w_in[ph]
                if ph == "F0":
                    sp.dma_start(w_ffn[:, 0:512], t["F0_w1"]).then_inc(done, 16)
                    sp.dma_start(w_ffn[:, 512:1024].rearrange("p (c d) -> p c d", c=4), t["F0_w2"].rearrange("(c p) d -> p c d", p=128)).then_inc(done, 16)
                    sp.dma_start(b1c[:, 0:4], t["F0_b1"]).then_inc(done, 16)
                if ph in ("F1", "F3"):
                    ne = 9 if ph == "F1" else 8
                    sp.dma_start(w_ffn[:, 0:4096].rearrange("p (e f) -> p e f", e=E), t[f"{ph}_w1"].rearrange("e d f -> d e f")).then_inc(done, 16)
                    for e in range(E):
                        sp.dma_start(w_ffn[:, 512 * (ne + e):512 * (ne + e + 1)].rearrange("p (c d) -> p c d", c=4), t[f"{ph}_w2"][e].rearrange("(c p) d -> p c d", p=128)).then_inc(done, 16)
                    sp.dma_start(b1c[:, 0:32], t[f"{ph}_b1"]).then_inc(done, 16)
                    sp.dma_start(b2r[0:E, :], t[f"{ph}_b2"]).then_inc(done, 16)
                if ph == "F1":
                    sp.dma_start(w_ffn[:, 4096:4608], t["F1_ws1"]).then_inc(done, 16)
                    sp.dma_start(w_ffn[:, 512 * 17:512 * 18].rearrange("p (c d) -> p c d", c=4), t["F1_ws2"].rearrange("(c p) d -> p c d", p=128)).then_inc(done, 16)
                    sp.dma_start(b1c[:, 32:36], t["F1_bs1"]).then_inc(done, 16)
                    sp.dma_start(b2r[E:E + 1, :], t["F1_bs2"].rearrange("(o d) -> o d", o=1)).then_inc(done, 16)
                if ph == "F2":
                    for i, w in enumerate(("F2_w1", "F2_w2")):
                        sp.dma_start(w_ffn[:, 2048 * i:2048 * (i + 1)].rearrange("p (e f) -> p e f", e=E), t[w].rearrange("e d f -> d e f")).then_inc(done, 16)
                    for e in range(E):
                        sp.dma_start(w_ffn[:, 4096 + 256 * e:4096 + 256 * (e + 1)].rearrange("p (c d) -> p c d", c=2), t["F2_w3"][e].rearrange("(c p) d -> p c d", p=128)).then_inc(done, 16)

            def load_context(ph, bt):
                if ph == "AS":
                    return
                p = bt.parity
                sp.dma_start(ctxT[:, p, :], t["ctxT"][bass.ds(bt.b, 1)].rearrange("o d k -> d (o k)")).then_inc(ctx_in[p], 16)
                if ph == "A3":
                    sp.dma_start(mrow_i[:, :], t["mask_k"][bass.ds(bt.b, 1)].to_broadcast([128, SK])).then_inc(mask_in, 16)
                    sp.dma_start(mcol_i[:, :], t["mask_kT"][bass.ds(bt.b, 1)].rearrange("o p c -> p (o c)")).then_inc(mask_in, 16)

            def save(n, p, part, width, src, done):
                rows = scratch[n][p].rearrange("(h b c) w -> b h c w", h=H, b=3)[part][:, :, 0:width]
                sp.dma_start(rows, src[:, 0:width].bitcast(F32)).then_inc(done[p], 16)

            def save_k(ph, bt):
                p, nk = bt.parity, ATT[ph]["nk"]
                wait(sp, "k_read", cnt.at("k_read", ph, bt))
                save("k", p, 0, nk, k_hi, k_saved)
                save("k", p, 2, nk, k_hi, k_saved)
                wait(sp, "kh_done", cnt.at("kh_done", ph, bt))
                save("k", p, 1, nk, k_lo, k_saved)

            def load_k(ph, bt):
                p, nk = bt.parity, ATT[ph]["nk"]
                sp.wait_ge(k_saved[p], saved(ph, bt))
                rows = scratch["k"][p].rearrange("(g r) w -> r g w", g=NG)[:, :, 0:nk]
                sp.dma_start(kst[p][0:HG * ROWS, :, 0:nk].bitcast(F32), rows).then_inc(k_stacked[p], 16)

            def save_q(ph, bt):
                p = bt.parity
                wait(sp, "q_read", cnt.at("q_read", ph, bt))
                save("q", p, 0, S, q_hi, q_saved)
                save("q", p, 1, S, q_hi, q_saved)
                wait(sp, "ql_done", cnt.at("ql_done", ph, bt))
                save("q", p, 2, S, q_lo, q_saved)

            def load_q(ph, bt):
                p = bt.parity
                sp.wait_ge(q_saved[p], saved(ph, bt))
                for j in range(HG):
                    rows = scratch["q"][p].rearrange("(g j r) w -> j r g w", g=NG, j=HG)[j]
                    sp.dma_start(qz[p][ROWS * j:ROWS * (j + 1), :, j, :].bitcast(F32), rows).then_inc(q_stacked[p], 16)

            def stack(ph, bt, released):
                wait(sp, "st_ready", released)
                apart(sp)
                for f in ((save_q, save_k, load_q, load_k) if ph == "AS" else (save_k, save_q, load_k, load_q)):
                    f(ph, bt)

            for ph in PHASES:
                if ph not in ATT:
                    continue
                units_before = cnt.start("st_ready", ph)
                if ph == "AS":
                    units_before = cnt.at("st_ready", "A2", B - 2, cnt.per["A2"]["st_ready"] - 1)
                wait(sp, "k_ready", cnt.start("k_ready", ph))
                wait(sp, "v_ready", cnt.start("v_ready", ph))
                if ph == "A3":
                    wait(sp, "max_done", cnt.start("max_done", ph))
                if ph in ("A1", "A2"):
                    wait(sp, "o_ready", cnt.start("o_ready", ph))
                    a = {"A1": "A2", "A2": "AS"}[ph]
                    for i, w in enumerate("qkvo"):
                        sp.dma_start(w_att[a][:, i, :], t[f"{a}_{w}"]).then_inc(watt_in[a], 16)
                load_context(ph, Batch(0, 0))
                if ph == "A0":
                    load_ffn("F0")
                stack(ph, Batch(0, 0), units_before)
                if ph not in ("A0", "AS"):
                    load_ffn({"A1": "F1", "A2": "F2", "A3": "F3"}[ph])

                def body(bt, first, last):
                    if last:
                        return
                    if not first:
                        wait(sp, "v_ready", cnt.at("v_ready", ph, bt + -1))
                        apart(sp)
                    if ph == "A3":
                        wait(sp, "mask_conv", cnt.at("mask_conv", ph, bt))
                    load_context(ph, bt + 1)
                    stack(ph, bt + 1, cnt.start("st_ready", ph) if first else cnt.at("st_ready", ph, bt + -1, cnt.per[ph]["st_ready"] - 1))

                batches(sp, body)
                if ph == "A0":
                    load_rest()
            out_tiles = out.rearrange("b (q p) d -> p (b q) d", p=128)
            with sp.Fori(0, NBLK) as blk:
                sp.wait_ge(sig["x_new"], cnt.at("x_new", "F3", blk))
                sp.dma_start(out_tiles[:, bass.ds(blk * TB, TB), :], x_tok[:, bass.ds(blk * TB, TB), :]).then_inc(stored, 16)
            sp.wait_ge(stored, 16 * NBLK)

        @block.gpsimd
        def _(pool):
            link = Links(pool, pool_chain)

            link(pool.memset(neg_half[:, :], -0.5))
            pool.memset(w_att["A3"][:, 0:3, :], 0.0).then_inc(setup_pool, 1)
            link(pool.memset(ident[:, :], 0.0))
            link(pool.affine_select(out=ident[:, :], in_=ident[:, :], compare_op=ALU.not_equal, fill=1.0, base=0, pattern=[[-1, 128]], channel_multiplier=1))
            link(pool.memset(ident_b[:, :], 0.0))
            link(pool.affine_select(out=ident_b[:, :], in_=ident_b[:, :], compare_op=ALU.not_equal, fill=1.0, base=0, pattern=[[-1, 128]], channel_multiplier=1))
            link(pool.memset(caus_q[:, :, :], 0.0))
            link(pool.memset(caus_T[:, :, :], 0.0))
            link(pool.affine_select(out=caus_q[:, :, :], in_=caus_q[:, :, :], compare_op=ALU.is_ge, fill=MASKED, base=0, pattern=[[128, 2], [-1, S]], channel_multiplier=1))
            link(pool.affine_select(out=caus_T[:, :, :], in_=caus_T[:, :, :], compare_op=ALU.is_ge, fill=MASKED, base=0, pattern=[[-128, 2], [1, S]], channel_multiplier=-1))
            link(pool.iota(iota_e[:, :], pattern=[[1, E]], base=0, channel_multiplier=0, allow_small_or_imprecise_dtypes=True))
            link(pool.memset(ones_row[:, :], 1.0))
            for a in ("AS", "A3"):
                link(pool.memset(b_att[a][:, :], 0.0))
            for p in range(2):
                link(pool.memset(qz[p][:, :, :, :].bitcast(F32), 0.0))
                link(pool.memset(kst[p][96:128, :, :].bitcast(F32), 1.0))
            link(pool.memset(mpart[:, :, :, :], 0.0))
            pool.memset(comb[:, :, E:E + 1], 1.0).then_inc(setup_pool, 1)

            def power(ph, b, k, first, n):
                pool.wait_ge(sig["var_done"], cnt.at("var_done", ph, b, k))
                apart(pool)
                pool.tensor_tensor(rstd[:, bass.ds(first, n)], veps[:, bass.ds(first, n)], neg_half[:, 0:n], ALU.pow)\
                    .then_inc(sig["rstd_done"], 1)

            def power_of_result(blk):
                pool.wait_ge(sig["var2_done"], cnt.at("var2_done", "F3", blk))
                pool.tensor_tensor(rstdb[:, :], vepsb[:, :], neg_half[:, :], ALU.pow).then_inc(sig["rstd2_done"], 1)

            def prepare_masks(bt):
                pool.wait_ge(mask_in, 32 * (bt.b + 1))
                if not bt.known or bt.b >= 2:
                    pool.wait_ge(sig["max_done"], cnt.at("max_done", "A3", bt + -2, 8 * NG - 1))
                    pool.wait_ge(sig["exp_done"], cnt.at("exp_done", "A3", bt + -2, 8 * NG - 1))
                apart(pool)
                pool.tensor_scalar(mrow[:, bt.parity, :], mrow_i[:, :], 0.0, MASKED, ALU.is_equal, ALU.mult)
                pool.tensor_scalar(mcol[:, bt.parity, :], mcol_i[:, :], 0.0, MASKED, ALU.is_equal, ALU.mult).then_inc(sig["mask_conv"], 1)

            def split_k(ph, bt):
                nk = ATT[ph]["nk"]
                pool.wait_ge(sig["k_read"], cnt.at("k_read", ph, bt))
                pool.tensor_tensor(k_lo[:, 0:nk], kf[:, 0:nk], k_hi[:, 0:nk].bitcast(F32), ALU.subtract).then_inc(sig["kh_done"], 1)

            def split_q(ph, bt):
                pool.wait_ge(sig["q_read"], cnt.at("q_read", ph, bt))
                pool.tensor_tensor(q_lo[:, :], qf[:, :], q_hi[:, :].bitcast(F32), ALU.subtract).then_inc(sig["ql_done"], 1)

            def split_maxima(ph, bt, g):
                buf = g % 2
                m = mx[:, buf, :].rearrange("p (j q) -> p q j", q=QT)
                neg, rest = (mrest[:, i, :].rearrange("p (j q) -> p q j", q=QT) for i in range(2))
                part = [mpart[:, buf, :, c:c + 3 * (32 + DH) + 1:32 + DH] for c in range(3)]
                pool.wait_ge(sig["max_done"], cnt.at("max_done", ph, bt, 8 * g + 7))
                wait(pool, "mt_ready", cnt.at("mt_ready", ph, bt, g) - 2)
                apart(pool)
                link(pool.tensor_scalar(neg, m, -1.0, None, ALU.mult), apart)
                link(pool.tensor_copy(part[0], neg))
                link(pool.tensor_tensor(rest, neg, part[0], ALU.subtract), apart)
                link(pool.tensor_copy(part[1], rest))
                pool.tensor_tensor(part[2], rest, part[1], ALU.subtract).then_inc(sig["msplit"], 1)

            def attention(ph):
                b0 = Batch(0, 0)

                def prepare(ph, bt):
                    for f in ((split_q, split_k) if ph == "AS" else (split_k, split_q)):
                        f(ph, bt)

                if ph == "A3":
                    pool.wait_ge(sig["max_done"], cnt.start("max_done", ph))
                    prepare_masks(b0)
                if ph != "AS":
                    prepare(ph, b0)
                if ph in ("A2", "A3"):
                    pool.wait_ge(sig["ql_done"], cnt.at("ql_done", ph, b0))
                    for p in range(2):
                        link(pool.memset(kst[p][96:128, :, :].bitcast(F32), 1.0))
                for g in range(0 if ph == "AS" else 2):
                    split_maxima(ph, b0, g)

                def result_power(bt):
                    for k in range(cnt.per[ph]["var_done"]):
                        power(ph, bt, k, bt.b * QT, QT)

                def body(bt, first, last):
                    for g in range(NG):
                        nph, nbt = following(ph, bt, last)
                        ahead = unit_after(ph, bt, last, g, 2)
                        if nph and g == 0:
                            prepare(nph, nbt)
                            if ph == "A3":
                                prepare_masks(bt + 1)
                        if not first and g == 3:
                            result_power(bt + -1)
                        if ahead[0]:
                            split_maxima(*ahead)

                batches(pool, body, link, POOL_LINKS[ph])
                result_power(Batch(B // 2 - 1, 1))

            def experts(ph):
                ne, turn = turns(ph)

                def low_weights(blk, e):
                    wh, wl = w_parts[e % turn]
                    pool.wait_ge(sig["wh_done"], cnt.at("wh_done", ph, blk, e))
                    pool.tensor_tensor(halves(wl), first_weights(ph, e), halves(wh.bitcast(F32)), ALU.subtract).then_inc(sig["wl_done"], 1)

                def low_tokens(blk):
                    pool.wait_ge(sig["fxt_read"], cnt.at("fxt_read", ph, blk))
                    pool.tensor_tensor(x_lo[:, :], xfT[:, :], x_hi[:, :].bitcast(F32), ALU.subtract).then_inc(sig["xl_done"], 1)

                def body(blk, last):
                    for e in range(turn, ne if last else ne + turn):
                        low_weights(blk + e // ne, e % ne)
                    if not last:
                        low_tokens(blk + 1)
                    if ph == "F3":
                        power_of_result(blk)
                    else:
                        power(ph, blk, 0, blk * TB, TB)

                pool.wait_ge(w_in[ph], W_PARTS[ph] * 16)
                for e in range(turn):
                    low_weights(0, e)
                low_tokens(0)
                blocks(pool, NBLK - 1, lambda blk: body(blk, False))
                body(NBLK - 1, True)

            for blk in range(NBLK):
                pool.wait_ge(sig["var_done"], blk + 1)
                pool.tensor_tensor(rstd[:, TB * blk:TB * (blk + 1)], veps[:, TB * blk:TB * (blk + 1)], neg_half[:, :], ALU.pow)\
                    .then_inc(sig["rstd_done"], 1)

            pool.wait_ge(w_in["F0"], 48)
            pool.partition_all_reduce(awq[:, :], w_ffn[:, 0:512], 128, bass.bass_isa.ReduceOp.absmax).then_inc(col_absmax, 1)
            for ph in PHASES:
                if ph in ATT:
                    attention(ph)
                elif ph == "F0":
                    for i in range(2):
                        pool.wait_ge(max_given, i + 1)
                        pool.partition_all_reduce(aall[:, i:i + 1], amx[:, i:i + 1], 128, bass.bass_isa.ReduceOp.absmax).then_inc(max_all, 1)
                    blocks(pool, NBLK, lambda blk: power(ph, blk, 0, blk * TB, TB))
                else:
                    experts(ph)

        @block.scalar
        def _(act):
            def exponentials(ph, bt, g, kt, half):
                p, nkt, q0 = bt.parity, ATT[ph]["nk"] // 128, seen(ph, kt)
                bias = mcol[:, p, kt:kt + 1] if ATT[ph]["mask"] == "keys" else 0.0
                wait(act, "st_ready", cnt.at("st_ready", ph, bt, 2 * (nkt * g + kt) + half))
                if half == 0:
                    wait(act, "av_ready", cnt.at("av_ready", ph, bt, nkt * g + kt) - 2 * nkt)
                dst = prob[:, g % 2, kt, 2 * S * half:2 * S * (half + 1)].rearrange("p (j s) -> p j s", j=2)[:, :, q0:]
                src = ps_t[TURN[turn_of(ph, g, kt, half)]][:, 0:2 * (S - q0)].rearrange("p (j s) -> p j s", j=2)
                nc.scalar.activation(dst, src, ACT.Exp, bias=bias).then_inc(sig["exp_done"], 1)

            def misc(what, ph, bt):
                nk = ATT[ph]["nk"]
                if what == "XT":
                    wait(act, "xt_ready", cnt.at("xt_ready", ph, bt))
                    wait(act, "v_ready", cnt.at("v_ready", ph, bt) - 1)
                    wait(act, "q_ready", cnt.at("q_ready", ph, bt) - 1)
                    if ph == "AS":
                        nc.scalar.activation(xnT[:, :], ps_m[:, 0:S], ACT.Identity, bias=ln_cols[:, 1:2],
                                             scale=ln_cols[:, 0:1]).then_inc(sig["xt_read"], 1)
                    else:
                        nc.scalar.activation(xnT[:, :], ps_m[:, 0:S], ACT.Copy).then_inc(sig["xt_read"], 1)
                elif what == "Q":
                    wait(act, "q_ready", cnt.at("q_ready", ph, bt))
                    wait(act, "ql_done", cnt.at("ql_done", ph, bt) - 1)
                    nc.scalar.activation(q_hi[:, :], ps_m[:, 0:S], ACT.Identity, bias=b_att[ph][:, 0:1], scale=ATT[ph]["scale"])
                    nc.scalar.activation(qf[:, :], ps_m[:, 0:S], ACT.Identity, bias=b_att[ph][:, 0:1],
                                         scale=ATT[ph]["scale"]).then_inc(sig["q_read"], 1)
                elif what == "K":
                    wait(act, "k_ready", cnt.at("k_ready", ph, bt))
                    wait(act, "kh_done", cnt.at("kh_done", ph, bt) - 1)
                    nc.scalar.activation(k_hi[:, 0:nk], ps_m[:, 0:nk], ACT.Identity, bias=b_att[ph][:, 1:2])
                    nc.scalar.activation(kf[:, 0:nk], ps_m[:, 0:nk], ACT.Identity, bias=b_att[ph][:, 1:2]).then_inc(sig["k_read"], 1)

                elif what == "ONT":
                    wait(act, "ont_ready", cnt.at("ont_ready", ph, bt))
                    wait(act, "o_ready", cnt.at("o_ready", ph, bt) - 1)
                    nc.scalar.activation(o_nT[:, :], ps_m[:, 0:S], ACT.Copy).then_inc(sig["ont_read"], 1)

            def read_values(ph, bt, g):
                wait(act, "av_ready", cnt.at("av_ready", ph, bt, (g + 1) * (ATT[ph]["nk"] // 128) - 1))
                if g == 0:
                    wait(act, "avt_ready", cnt.at("avt_ready", ph, bt) - 1)
                nc.scalar.activation(avs[:, g, :], ps_av[:, 0:S], ACT.Copy).then_inc(sig["av_read"], 1)

            def maxima_T(ph, bt, g):
                wait(act, "mt_ready", cnt.at("mt_ready", ph, bt, g))
                nc.scalar.activation(qz[bt.parity][96:128, g, :, :], ps_mb[96:128, :].rearrange("p (j s) -> p j s", j=HG),
                                     ACT.Copy).then_inc(sig["mt_read"], 1)

            def attention(ph):
                b0 = Batch(0, 0)
                if ph != "AS":
                    for what in ("K", "XT", "Q"):
                        misc(what, ph, b0)
                    maxima_T(ph, b0, 0)

                def body(bt, first, last):
                    nph, nbt = following(ph, bt, last)
                    table = slots(nph)
                    for g in range(NG):
                        nxt = unit_after(ph, bt, last, g, 1)
                        past, g_past = later(bt, g, -2)
                        if not (first and g < 2):
                            read_values(ph, past, g_past)
                        for k in range(4):
                            for half in range(2):
                                if kt_of(ph, k) is not None:
                                    exponentials(ph, bt, g, kt_of(ph, k), half)
                                what = table.get((g, k, half))
                                if what == "MT":
                                    if nxt[0]:
                                        maxima_T(*nxt)
                                elif what in ("XT", "Q", "K") and nph:
                                    misc(what, nph, nbt)
                                elif what == "ONT" and not first:
                                    misc(what, ph, bt + -1)

                batches(act, body)
                end = Batch(B // 2 - 1, 1)
                for g in (2, 3):
                    read_values(ph, end, g)
                misc("ONT", ph, end)

            def read_block(ph, blk):
                wait(act, "fxt_ready", cnt.at("fxt_ready", ph, blk))
                wait(act, "h_ready", cnt.at("h_ready", ph, blk, -1))
                for dst in (x_hi, xfT):
                    if ph == "F2":
                        ins = nc.scalar.activation(dst[:, :], ps_m[:, :], ACT.Identity, bias=ln_cols[:, 3:4], scale=ln_cols[:, 2:3])
                    else:
                        ins = nc.scalar.activation(dst[:, :], ps_m[:, :], ACT.Copy)
                ins.then_inc(sig["fxt_read"], 1)

            def quantised_ffn():
                ph = "F0"
                hid = prob[:, :, :, :].rearrange("p a c s -> p (a c s)").rearrange("p (c s) -> p c s", c=4)
                act.wait_ge(max_all, 1)
                act.wait_ge(svec_done, 1)

                def body(blk):
                    for c in range(4):
                        wait(act, "h_ready", cnt.at("h_ready", ph, blk, c))
                        nc.scalar.activation(hid[:, c, bass.ds(blk * 512, 512)], ps_h[c][:, :],
                                             ACT.Gelu, bias=b1c[:, c:c + 1], scale=svec[:, c:c + 1]).then_inc(sig["h_done"], 1)

                blocks(act, NBLK, body)

            def experts(ph):
                ne, turn = turns(ph)

                def high_weights(e):
                    nc.scalar.activation(halves(w_parts[e % turn][0]), first_weights(ph, e), ACT.Copy).then_inc(sig["wh_done"], 1)

                def body(blk, last):
                    read_block(ph, blk)
                    for e in range(ne):
                        h = prob[:, e % 2, :, :].rearrange("p c s -> p (c s)")[:, 0:2048].rearrange("p (c s) -> p c s", c=4)
                        for c in range(2 if ph == "F2" else 4):
                            wait(act, "h_ready", cnt.at("h_ready", ph, blk, 4 * e + c))
                            if c == 0:
                                wait(act, "y_ready", cnt.at("y_ready", ph, blk, e) - 2)
                            src = ps_h[c][:, :]
                            if ph == "F2":
                                nc.scalar.activation(h[:, 2 + c, :], src, ACT.Silu).then_inc(sig["h_done"], 1)
                            else:
                                nc.scalar.activation(h[:, c, :], src, ACT.Gelu, bias=b1c[:, 4 * e + c:4 * e + c + 1]).then_inc(sig["h_done"], 1)
                        if e + turn < ne or not last:
                            wait(act, "h_ready", cnt.at("h_ready", ph, blk, 4 * e + 3))
                            high_weights((e + turn) % ne)
                        if e == (0 if ph == "F2" else 1):
                            wait(act, "lg_read", cnt.at("lg_read", ph, blk))
                            nc.scalar.activation(th[:, :], dlt[:, :], ACT.Tanh, scale=0.5).then_inc(sig["th_done"], 1)

                act.wait_ge(w_in[ph], W_PARTS[ph] * 16)
                wait(act, "x_new", cnt.start("x_new", ph))
                for e in range(turn):
                    high_weights(e)
                blocks(act, NBLK - 1, lambda blk: body(blk, False))
                body(NBLK - 1, True)

            act.wait_ge(loaded_first, 16 * N_FIRST)
            act.wait_ge(setup_pool, 2)
            act.wait_ge(bias_scaled, 1)
            for ph in PHASES:
                if ph in ATT:
                    attention(ph)
                elif ph == "F0":
                    act.wait_ge(loaded, 16 * N_LOADED)
                    act.wait_ge(bias_scaled, 3)
                    quantised_ffn()
                else:
                    experts(ph)

        @block.tensor
        def _(pe):
            misc_reader = [None]

            def take_misc(reader, value):
                if misc_reader[0]:
                    wait(pe, *misc_reader[0])
                misc_reader[0] = (reader, value)

            def scores(ph, bt, g, i):
                p, nk, j, q = bt.parity, ATT[ph]["nk"], i // 2, i % 2
                if g == 0 and i == 0:
                    pe.wait_ge(q_stacked[p], stacked(ph, bt, HG))
                    pe.wait_ge(k_stacked[p], stacked(ph, bt, 1))
                if ph == "AS":
                    nk = 128 * (q + 1)
                wait(pe, "max_done", cnt.at("max_done", ph, bt, 8 * g + i) - BACK[i])
                pe.matmul(ps_s[TURN[i]][:, 0:nk], qz[p][0:96, g, j, q * 128:(q + 1) * 128], kst[p][0:96, g, 0:nk],
                          start=True, stop=True).then_inc(sig["s_ready"], 1)

            def scores_T(ph, bt, g, kt, half):
                p, nkt, mask = bt.parity, ATT[ph]["nk"] // 128, ATT[ph]["mask"]
                turn, q0 = turn_of(ph, g, kt, half), seen(ph, kt)
                if kt == 0 and half == 0:
                    wait(pe, "mt_read", cnt.at("mt_read", ph, bt, g))
                wait(pe, "exp_done", cnt.at("exp_done", ph, bt, 2 * (nkt * g + kt) + half) - BACK[turn])
                dst = ps_t[TURN[turn]][:, 0:2 * (S - q0)].rearrange("p (j s) -> p j s", j=2)
                mm = pe.matmul(dst, kst[p][:, g, kt * 128:(kt + 1) * 128], qz[p][:, g, 2 * half:2 * half + 2, q0:],
                               start=True, stop=mask in (None, "keys"))
                if mask == "full":
                    mm = pe.matmul(dst, ident_b[:, :], mask_T[:, kt:kt + 1, :].to_broadcast([128, 2, S]), start=False, stop=True)
                if mask == "causal":
                    mm = pe.matmul(dst[:, :, 0:128], ident_b[:, :], caus_T[:, kt:kt + 1, q0:q0 + 128].to_broadcast([128, 2, 128]),
                                   start=False, stop=True)
                mm.then_inc(sig["st_ready"], 1)

            def values(ph, bt, g, kt):
                p, nkt, q0 = bt.parity, ATT[ph]["nk"] // 128, seen(ph, kt)
                if kt == 0:
                    wait(pe, "av_read", cnt.at("av_read", ph, bt, g) - 1)
                    if g == 0:
                        wait(pe, "v_read", cnt.at("v_read", ph, bt))
                wait(pe, "exp_done", cnt.at("exp_done", ph, bt, 2 * (nkt * g + kt) + 1))
                buf = g % 2
                for j in range(HG):
                    mm = pe.matmul(ps_av[32 * j:32 * j + 32, q0:S], vaug[p][:, kt, HG * g + j, :],
                                   prob[:, buf, kt, S * j + q0:S * (j + 1)], start=(kt == 0), stop=(kt == nkt - 1))
                mm.then_inc(sig["av_ready"], 1)

            def maxima_T(ph, bt, g):
                take_misc("mt_read", cnt.at("mt_read", ph, bt, g))
                wait(pe, "msplit", cnt.at("msplit", ph, bt, g))
                for j in range(HG):
                    for q in range(QT):
                        mm = pe.transpose(ps_mb[96:128, S * j + 128 * q:S * j + 128 * (q + 1)],
                                          mpart[:, g % 2, q, 32 * j:32 * j + 32], ident_b[:, :])
                mm.then_inc(sig["mt_ready"], 1)

            def misc(what, ph, bt):
                nk, p = ATT[ph]["nk"], bt.parity
                w = w_att[ph]
                if what == "XT":
                    take_misc("xt_read", cnt.at("xt_read", ph, bt))
                    wait(pe, "xn_done", cnt.at("xn_done", ph, bt))
                    for q in range(QT):
                        mm = pe.transpose(ps_m[:, 128 * q:128 * (q + 1)], xn[:, q, :], ident[:, :])
                    mm.then_inc(sig["xt_ready"], 1)
                elif what == "Q":
                    take_misc("q_read", cnt.at("q_read", ph, bt))
                    wait(pe, "xt_read", cnt.at("xt_read", ph, bt))
                    pe.matmul(ps_m[:, 0:S], w[:, 0, :], xnT[:, :], start=True, stop=True).then_inc(sig["q_ready"], 1)
                elif what == "K":
                    take_misc("k_read", cnt.at("k_read", ph, bt))
                    if ph == "AS":
                        wait(pe, "xt_read", cnt.at("xt_read", ph, bt))
                    else:
                        pe.wait_ge(ctx_in[p], context_in(ph, bt))
                    pe.matmul(ps_m[:, 0:nk], w[:, 1, :], xnT[:, :] if ph == "AS" else ctxT[:, p, :],
                              start=True, stop=True).then_inc(sig["k_ready"], 1)
                elif what == "V":
                    take_misc("v_read", cnt.at("v_read", ph, bt))
                    for kt in range(nk // 128):
                        src = (xnT if ph == "AS" else ctxT[:, p, :])
                        mm = pe.matmul(ps_m[:, 128 * kt:128 * (kt + 1)], src[:, 128 * kt:128 * (kt + 1)], w[:, 2, :],
                                       start=True, stop=True)
                    mm.then_inc(sig["v_ready"], 1)
                elif what in ("AVT0", "AVT1"):
                    q = int(what[-1])
                    take_misc("on_done", cnt.at("on_done", ph, bt, q))
                    wait(pe, "av_read", cnt.at("av_read", ph, bt, NG - 1))
                    for g in range(NG):
                        mm = pe.transpose(ps_m[:, 128 * g:128 * (g + 1)], avs[:, g, 128 * q:128 * (q + 1)], ident[:, :])
                    mm.then_inc(sig["avt_ready"], 1)
                elif what == "ONT":
                    take_misc("ont_read", cnt.at("ont_read", ph, bt))
                    wait(pe, "on_done", cnt.at("on_done", ph, bt, 1))
                    for q in range(QT):
                        mm = pe.transpose(ps_m[:, 128 * q:128 * (q + 1)], o_n[:, q, :], ident[:, :])
                    mm.then_inc(sig["ont_ready"], 1)
                elif what == "O":
                    take_misc("x_new", cnt.at("x_new", ph, bt))
                    wait(pe, "ont_read", cnt.at("ont_read", ph, bt))
                    for q in range(QT):
                        dst = ps_m[:, 128 * q:128 * (q + 1)]
                        pe.matmul(dst, o_nT[:, 128 * q:128 * (q + 1)], w[:, 3, :], start=True, stop=False)
                        mm = pe.matmul(dst, ones_row[:, :], bo_att[ph][:, :], start=False, stop=True)
                    mm.then_inc(sig["o_ready"], 1)

            def attention(ph):
                wait(pe, "acc_done", cnt.start("acc_done", ph))
                wait(pe, "h_done", cnt.start("h_done", ph))
                wait(pe, "x_new", cnt.start("x_new", ph))
                misc_reader[0] = None
                if ph == "A2":
                    for a in watt_in:
                        pe.wait_ge(watt_in[a], 64)
                b0 = Batch(0, 0)
                for what in () if ph == "AS" else ("K", "XT", "Q", "V"):
                    misc(what, ph, b0)
                if ph == "A0":
                    pe.wait_ge(col_absmax, 1)
                    for c in range(4):
                        mm = pe.matmul(ps_av[:, c:c + 1], awq[0:1, 128 * c:128 * (c + 1)], ones_row[:, 0:1], start=True, stop=True)
                    mm.then_inc(w_cols, 1)
                for g in range(0 if ph == "AS" else 2):
                    for i in range(8):
                        scores(ph, b0, g, i)
                        if (g, i) == (1, 4):
                            maxima_T(ph, b0, 0)

                def body(bt, first, last):
                    nph, nbt = following(ph, bt, last)
                    table = slots(nph)
                    for g in range(NG):
                        ahead = unit_after(ph, bt, last, g, 2)
                        nxt = unit_after(ph, bt, last, g, 1)
                        past, g_past = later(bt, g, -1)
                        for k in range(4):
                            kt = kt_of(ph, k)
                            for half in range(2):
                                if ahead[0]:
                                    scores(*ahead, 2 * k + half)
                                if kt is not None:
                                    scores_T(ph, bt, g, kt, half)
                                if half == 1 and kt is not None and not (first and g == 0):
                                    values(ph, past, g_past, kt)
                                what = table.get((g, k, half))
                                if what == "MT":
                                    if nxt[0]:
                                        maxima_T(*nxt)
                                elif what in ("XT", "Q", "K", "V"):
                                    if nph:
                                        misc(what, nph, nbt)
                                elif what and not first:
                                    misc(what, ph, bt + -1)

                def loop_body(bt, first, last):
                    misc_reader[0] = ("mt_read", cnt.at("mt_read", ph, bt, 0))
                    body(bt, first, last)

                batches(pe, loop_body)
                end = Batch(B // 2 - 1, 1)
                for kt in range(ATT[ph]["nk"] // 128):
                    values(ph, end, NG - 1, kt)
                for what in ("AVT0", "AVT1", "ONT", "O"):
                    misc(what, ph, end)

            def turn_block(ph, blk):
                wait(pe, "xn_done", cnt.at("xn_done", ph, blk))
                for q in range(TB):
                    mm = pe.transpose(ps_m[:, 128 * q:128 * (q + 1)], xf[:, q, :], ident[:, :])
                mm.then_inc(sig["fxt_ready"], 1)

            def quantised_ffn():
                ph = "F0"
                def hidden(blk):
                    wait(pe, "fxt_read", cnt.at("fxt_read", ph, blk) - 1)
                    turn_block(ph, blk)
                    wait(pe, "fxt_read", cnt.at("fxt_read", ph, blk))
                    for c in range(4):
                        wait(pe, "h_done", cnt.at("h_done", ph, blk, c) - 4)
                        pe.matmul(ps_h[c][:, :], w_ffn[:, 128 * c:128 * (c + 1)],
                                  xfT[:, :], start=True, stop=True).then_inc(sig["h_ready"], 1)

                blocks(pe, NBLK, hidden)

                def output(blk, p):
                    hq = w_ffn[:, 1024 + 2048 * p:1024 + 2048 * (p + 1)].rearrange("p (c s) -> p c s", c=4)
                    wait(pe, "hq_done", cnt.at("hq_done", ph, blk))
                    wait(pe, "x_new", cnt.at("x_new", ph, blk) - 2)
                    for q in range(TB):
                        for c in range(4):
                            mm = pe.matmul(ps_s[p][:, 128 * q:128 * (q + 1)], hq[:, c, 128 * q:128 * (q + 1)],
                                           w_ffn[:, 512 + 128 * c:512 + 128 * (c + 1)], start=(c == 0), stop=(c == 3))
                    mm.then_inc(sig["y_ready"], 1)

                with pe.Fori(0, NBLK, 2) as blk:
                    output(blk, 0)
                    output(blk + 1, 1)

            def experts(ph):
                ne, turn = turns(ph)
                nc_h = 2 if ph == "F2" else 4
                gi = {"F1": 0, "F2": 1, "F3": 2}[ph]
                w2_at = {"F1": 4608, "F2": 4096, "F3": 4096}[ph]

                def first_product(blk, e):
                    w_hi, w_lo = w_parts[e % turn]
                    wait(pe, "wl_done", cnt.at("wl_done", ph, blk, e))
                    for n, (w, x) in enumerate(((w_lo, x_hi), (w_hi, x_hi), (w_hi, x_lo))):
                        if e == 0 and n == 2:
                            wait(pe, "xl_done", cnt.at("xl_done", ph, blk))
                        for c in range(4):
                            if n == 0:
                                name, at, back = ("h_done", 4 * e + c, 4) if ph != "F2" else (("h_done", "g_done")[c // 2], 2 * e + c % 2, 2)
                                wait(pe, name, cnt.at(name, ph, blk, at) - back)
                            mm = pe.matmul(ps_h[c][:, :], w[:, 128 * c:128 * (c + 1)], x[:, :], start=(n == 0), stop=(n == 2))
                            if n == 2:
                                mm.then_inc(sig["h_ready"], 1)

                def second_product(blk, n, e):
                    wait(pe, "acc_done", cnt.at("acc_done", ph, blk, n) - (1 if n == 0 and ph != "F2" else 2))
                    bias = n == E
                    if bias:
                        wait(pe, "ct_read", cnt.at("ct_read", ph, blk))
                    if e is not None:
                        name, at = ("g_done", 2 * e + 1) if ph == "F2" else ("h_done", 4 * e + 3)
                        wait(pe, name, cnt.at(name, ph, blk, at))
                        h = prob[:, e % 2, :, :].rearrange("p c s -> p (c s)")[:, 0:2048].rearrange("p (c s) -> p c s", c=4)
                    for q in range(TB):
                        dst = ps_s[n % 2][:, 128 * q:128 * (q + 1)]
                        if bias:
                            mm = pe.matmul(dst, combT[:, 128 * q:128 * (q + 1)] if ph == "F1" else combT[0:E, 128 * q:128 * (q + 1)],
                                           b2r[:, :] if ph == "F1" else b2r[0:E, :], start=True, stop=e is None)
                        for c in range(nc_h if e is not None else 0):
                            w2c = w_ffn[:, w2_at + 128 * (nc_h * e + c):w2_at + 128 * (nc_h * e + c + 1)]
                            mm = pe.matmul(dst, h[:, c, 128 * q:128 * (q + 1)], w2c,
                                           start=(c == 0 and not bias), stop=(c == nc_h - 1))
                    mm.then_inc(sig["y_ready"], 1)

                def body(blk, last):
                    wait(pe, "fxt_read", cnt.at("fxt_read", ph, blk))
                    first_product(blk, 0)
                    wait(pe, "lg_read", cnt.at("lg_read", ph, blk) - 1)
                    for q in range(TB):
                        mm = pe.matmul(ps_av[:, E * q:E * (q + 1)], xfT[:, 128 * q:128 * (q + 1)], gate[:, gi, :], start=True, stop=True)
                    mm.then_inc(sig["lg_ready"], 1)
                    for e in range(ne):
                        if e + 1 < ne:
                            first_product(blk, e + 1)
                        if e == 5 and ph != "F2":
                            wait(pe, "comb_done", cnt.at("comb_done", ph, blk))
                            for q in range(TB):
                                mm = pe.transpose(ps_av[0:E + 1, 128 * q:128 * (q + 1)], comb[:, q, :], ident[:, :])
                            mm.then_inc(sig["ct_ready"], 1)
                        second_product(blk, e, e)
                        if e == 4 and not last:
                            turn_block(ph, blk + 1)
                    if ph == "F3":
                        second_product(blk, E, None)

                pe.wait_ge(w_in[ph], W_PARTS[ph] * 16)
                turn_block(ph, 0)
                blocks(pe, NBLK - 1, lambda blk: body(blk, False))
                body(NBLK - 1, True)

            pe.wait_ge(setup_pool, 2)
            pe.wait_ge(loaded_first, 16 * N_FIRST)
            for ph in PHASES:
                if ph == "A3":
                    pe.wait_ge(bd_loaded, 16 * 3 * H)
                if ph in ATT:
                    attention(ph)
                elif ph == "F0":
                    pe.wait_ge(loaded, 16 * N_LOADED)
                    quantised_ffn()
                else:
                    experts(ph)

        @block.vector
        def _(dve):
            link = Links(dve, dve_chain)

            def tile_of(buf, b, q):
                return buf[:, bass.ds(b * QT + q, 1), :].rearrange("p o d -> p (o d)")

            since = {}

            def statistics(step, srcs, st=st6, m=mv):
                if step == 0:
                    for q, s in enumerate(srcs):
                        ins = dve.bn_stats(st[:, q, :], s)
                    since["stats"] = link.mark(ins)
                else:
                    link.until(since["stats"], apart)
                    for q in range(len(srcs)):
                        ins = dve.bn_aggr(m[:, q, :], st[:, q, :])
                    since["aggregate"] = link.mark(ins)

            def keep_statistics(first, n):
                link.until(since["aggregate"])
                dve.tensor_scalar(veps[:, bass.ds(first, n)], mv[:, 0:n, 1], EPS, None, ALU.add)
                dve.tensor_copy(means[:, bass.ds(first, n)], mv[:, 0:n, 0]).then_inc(sig["var_done"], 1)

            def all_statistics(srcs, first):
                statistics(0, srcs)
                statistics(1, srcs)
                keep_statistics(first, len(srcs))

            def normalise(srcs, dsts, first):
                for q, (s, d) in enumerate(zip(srcs, dsts)):
                    ins = dve.tensor_scalar(d, s, means[:, bass.ds(first + q, 1)], rstd[:, bass.ds(first + q, 1)],
                                            ALU.subtract, ALU.mult)
                return ins

            def normalise_batch(ph, bt):
                src = y_tok if ph == "AS" else x_tok
                wait(dve, "xt_ready", cnt.at("xt_ready", ph, bt) - 1)
                normalise([tile_of(src, bt.b, q) for q in range(QT)], [xn[:, q, :] for q in range(QT)], bt.b * QT)\
                    .then_inc(sig["xn_done"], 1)

            def result_statistics(ph, bt, step):
                first = bt.b * QT
                tiles = [tile_of(x_tok, bt.b, q) for q in range(QT)]
                tiles_y = [tile_of(y_tok, bt.b, q) for q in range(QT)]
                result = tiles_y if ph == "AS" else tiles
                if step == 0:
                    wait(dve, "x_new", cnt.at("x_new", ph, bt))
                    apart(dve)
                    statistics(0, result)
                elif step == 1:
                    statistics(1, result)
                elif step == 2:
                    keep_statistics(first, QT)
                elif step == 4 and ph in ("A0", "A2"):
                    wait(dve, "rstd_done", cnt.at("rstd_done", ph, bt))
                    since["inner"] = link.mark(normalise(tiles, tiles_y, first))
                elif step == 5 and ph == "A0":
                    link.until(since["inner"], apart)
                    link(dve.tensor_reduce(amx[:, 2:3], y_tok[:, bass.ds(first, QT), :], AX.XY, ALU.max, apply_absolute_value=True))
                    link(dve.tensor_tensor(amx[:, 0:1], amx[:, 0:1], amx[:, 2:3], ALU.max))
                elif step == 5 and ph == "A2":
                    link.until(since["inner"], apart)
                    statistics(0, tiles_y)
                elif step == 6 and ph == "A2":
                    statistics(1, tiles_y)
                elif step == 7 and ph == "A2":
                    keep_statistics(first, QT)

            def lay_v(ph, bt):
                p, nkt = bt.parity, ATT[ph]["nk"] // 128
                wait(dve, "v_ready", cnt.at("v_ready", ph, bt))
                src = ps_m[:, 0:128 * nkt].rearrange("p (k h d) -> p k h d", k=nkt, h=H)
                dst = vaug[p][:, 0:nkt, :, 0:DH]
                if ph in bv_att:
                    bias = bv_att[ph][:, :].rearrange("p (o h d) -> p o h d", o=1, h=H).to_broadcast([128, nkt, H, DH])
                    dve.tensor_tensor(dst, src, bias, ALU.add).then_inc(sig["v_read"], 1)
                else:
                    dve.tensor_copy(dst, src).then_inc(sig["v_read"], 1)

            def maximum(ph, bt, g, i):
                nk, mask, q, buf = ATT[ph]["nk"], ATT[ph]["mask"], i % 2, g % 2
                if i == 0:
                    wait(dve, "msplit", cnt.at("msplit", ph, bt, g) - 2)
                wait(dve, "s_ready", cnt.at("s_ready", ph, bt, 8 * g + i))
                if ph == "AS":
                    nk = 128 * (q + 1)
                src = ps_s[TURN[i]][:, 0:nk]
                if mask is None:
                    dve.tensor_reduce(mx[:, buf, i:i + 1], src, AX.X, ALU.max).then_inc(sig["max_done"], 1)
                    return
                if mask == "keys":
                    if g == 0 and i == 0:
                        wait(dve, "mask_conv", cnt.at("mask_conv", ph, bt))
                    m = mrow[:, bt.parity, :]
                else:
                    m = (mask_q if mask == "full" else caus_q)[:, q, 0:nk]
                apart(dve)
                dve.tensor_tensor_reduce(junk[:, TURN[i], 0:nk], src, m, 1.0, -3.0e38, ALU.add, ALU.max, mx[:, buf, i:i + 1])\
                   .then_inc(sig["max_done"], 1)

            def misc(what, ph, bt):
                if what in ("AVT0", "AVT1"):
                    q = int(what[-1])
                    wait(dve, "avt_ready", cnt.at("avt_ready", ph, bt, q))
                    src = ps_m[:, :].rearrange("p (h r) -> p h r", h=H)
                    link(dve.reciprocal(rsum[:, :].rearrange("p (h o) -> p h o", o=1), src[:, :, DH:DH + 1]))
                    dve.tensor_tensor(o_n[:, q, :].rearrange("p (h d) -> p h d", h=H), src[:, :, 0:DH],
                                      rsum[:, :].rearrange("p (h o) -> p h o", o=1).to_broadcast([128, H, DH]), ALU.mult)\
                       .then_inc(sig["on_done"], 1)
                elif what == "O":
                    wait(dve, "o_ready", cnt.at("o_ready", ph, bt))
                    dst = (y_tok if ph == "AS" else x_tok)[:, bass.ds(bt.b * QT, QT), :]
                    dve.tensor_tensor(dst, ps_m[:, 0:S].rearrange("p (q d) -> p q d", q=QT), dst, ALU.add).then_inc(sig["x_new"], 1)

            def quantise_weights():
                w1, w2w = w_ffn[:, 0:512], w_ffn[:, 512:1024]
                w2v = w2w.rearrange("p (c d) -> p c d", c=4)
                dve.wait_ge(w_in["F0"], 48)
                dve.wait_ge(col_absmax, 1)
                dve.wait_ge(w_cols, 1)
                link(dve.tensor_scalar(svec[:, 0:4], ps_av[:, 0:4], 1e-8, 1.0 / A8, ALU.max, ALU.mult))
                link(dve.tensor_scalar(awq[:, :], awq[:, :], 1e-8, None, ALU.max))
                link(dve.reciprocal(awq[:, :], awq[:, :]))
                link(dve.tensor_scalar(awq[:, :], awq[:, :], A8, None, ALU.mult))
                link(dve.tensor_tensor(w1, w1, awq[:, :], ALU.mult))
                link(dve.tensor_scalar(w1, w1, ROUND, ROUND, ALU.add, ALU.subtract))
                link(dve.tensor_scalar(w1, w1, -A8 - 1.0, A8, ALU.max, ALU.min))
                link(dve.tensor_reduce(awo[:, 0, :], w2v, AX.X, ALU.max, apply_absolute_value=True))
                link(dve.tensor_scalar(awo[:, 0, :], awo[:, 0, :], 1e-8, None, ALU.max))
                link(dve.reciprocal(awo[:, 1, :], awo[:, 0, :]))
                link(dve.tensor_scalar(awo[:, 1, :], awo[:, 1, :], A8, None, ALU.mult))
                link(dve.tensor_tensor(w2v, w2v, awo[:, 1, :].rearrange("p (c o) -> p c o", o=1).to_broadcast([128, 4, D]), ALU.mult))
                link(dve.tensor_scalar(w2w, w2w, ROUND, ROUND, ALU.add, ALU.subtract))
                link(dve.tensor_scalar(w2w, w2w, -A8 - 1.0, A8, ALU.max, ALU.min))
                link(dve.tensor_scalar(awo[:, 0, :], awo[:, 0, :], 1.0 / A8, None, ALU.mult))
                link(dve.tensor_tensor(w2v, w2v, awo[:, 0, :].rearrange("p (c o) -> p c o", o=1).to_broadcast([128, 4, D]), ALU.mult))
                link(dve.memset(amx[:, :], 0.0))

            def convert_rest():
                dve.wait_ge(loaded, 16 * N_LOADED)
                for a in ("A1", "A2"):
                    dve.tensor_scalar(b_att[a][:, 0:1], b_att[a][:, 0:1], ATT[a]["scale"], None, ALU.mult).then_inc(bias_scaled, 1)
                dve.tensor_scalar(mask_q[:, :, :], mask_q[:, :, :].bitcast(I32), 0.0, MASKED, ALU.is_equal, ALU.mult)
                link(dve.tensor_scalar(mask_T[:, :, :], mask_T_i, 0.0, MASKED, ALU.is_equal, ALU.mult))

            def attention(ph):
                b0 = Batch(0, 0)
                wait(dve, "x_new", cnt.start("x_new", ph))
                wait(dve, "rstd_done", cnt.start("rstd_done", ph))
                if ph != "AS":
                    normalise_batch(ph, b0)
                if ph == "A0":
                    quantise_weights()
                if ph != "AS":
                    lay_v(ph, b0)
                for g in range(0 if ph == "AS" else 2):
                    for i in range(8):
                        maximum(ph, b0, g, i)

                def body(bt, first, last):
                    nph, nbt = following(ph, bt, last)
                    table = slots(nph)
                    for g in range(NG):
                        ahead = unit_after(ph, bt, last, g, 2)
                        for k in range(4):
                            if nph and (g, k) == (0, 0):
                                normalise_batch(nph, nbt)
                            for half in range(2):
                                if ahead[0]:
                                    maximum(*ahead, 2 * k + half)
                                if g == 3 and not first:
                                    result_statistics(ph, bt + -1, 2 * k + half)
                                what = table.get((g, k, half))
                                if what == "V" and nph:
                                    lay_v(nph, nbt)
                                elif what in ("AVT0", "AVT1", "O") and not first:
                                    misc(what, ph, bt + -1)

                batches(dve, body, link, LINKS[ph])
                end = Batch(B // 2 - 1, 1)
                if ph == "A0":
                    convert_rest()
                for what in ("AVT0", "AVT1", "O"):
                    misc(what, ph, end)
                for step in range(8):
                    result_statistics(ph, end, step)

            def block_tiles(buf, blk):
                return [buf[:, bass.ds(blk * TB + q, 1), :].rearrange("p o d -> p (o d)") for q in range(TB)]

            def rounded(dst, src, scale):
                link(dve.tensor_scalar(dst, src, scale, -A16 - 1.0, ALU.mult, ALU.max))
                link(dve.tensor_scalar(dst, dst, A16, ROUND, ALU.min, ALU.add))
                return dve.tensor_scalar(dst, dst, ROUND, None, ALU.subtract)

            def quantised_ffn():
                ph = "F0"
                hid = prob[:, :, :, :].rearrange("p a c s -> p (a c s)").rearrange("p (c s) -> p c s", c=4)
                dve.tensor_copy(amx[:, 3:4], amx[:, 0:1]).then_inc(max_given, 1)

                def scales(i):
                    dve.wait_ge(max_all, i + 1)
                    link(dve.tensor_scalar(aall[:, 2:3], aall[:, i:i + 1], 1e-8, None, ALU.max))
                    link(dve.reciprocal(svec[:, 4:5], aall[:, 2:3]))
                    link(dve.tensor_scalar(svec[:, 4:5], svec[:, 4:5], A16, None, ALU.mult))
                    link(dve.tensor_scalar(svec[:, 5:6], aall[:, 2:3], 1.0 / A16, None, ALU.mult))

                scales(0)
                dve.tensor_scalar(svec[:, 0:4], svec[:, 0:4], svec[:, 5:6], None, ALU.mult).then_inc(svec_done, 1)

                def quantise_x(blk):
                    wait(dve, "fxt_ready", cnt.at("fxt_ready", ph, blk) - 1)
                    rounded(xf[:, :, :], y_tok[:, bass.ds(blk * TB, TB), :], svec[:, 4:5]).then_inc(sig["xn_done"], 1)
                    wait(dve, "fxt_ready", cnt.at("fxt_ready", ph, blk))
                    wait(dve, "h_ready", cnt.at("h_ready", ph, blk, -1))
                    dve.tensor_copy(xfT[:, :], ps_m[:, :]).then_inc(sig["fxt_read"], 1)

                def hidden_maximum(blk):
                    wait(dve, "h_done", cnt.at("h_done", ph, blk, 3))
                    apart(dve)
                    link(dve.tensor_reduce(amx[:, 4:5], hid[:, :, bass.ds(blk * 512, 512)], AX.XY, ALU.max, apply_absolute_value=True))
                    link(dve.tensor_tensor(amx[:, 5:6], amx[:, 5:6], amx[:, 4:5], ALU.max))

                quantise_x(0)
                with dve.Fori(0, NBLK - 1) as i:
                    link.enter(i, 4)
                    quantise_x(i + 1)
                    hidden_maximum(i)
                link.leave(NBLK - 1)
                hidden_maximum(NBLK - 1)
                dve.tensor_copy(amx[:, 1:2], amx[:, 5:6]).then_inc(max_given, 1)
                scales(1)

                def quantise_h(blk, p):
                    hq = w_ffn[:, 1024 + 2048 * p:1024 + 2048 * (p + 1)].rearrange("p (c s) -> p c s", c=4)
                    wait(dve, "y_ready", cnt.at("y_ready", ph, blk) - 2)
                    rounded(hq, hid[:, :, bass.ds(blk * 512, 512)], svec[:, 4:5]).then_inc(sig["hq_done"], 1)

                def add(blk, p):
                    wait(dve, "y_ready", cnt.at("y_ready", ph, blk))
                    wait(dve, "x_new", cnt.at("x_new", ph, blk) - 1)
                    dst = x_tok[:, bass.ds(blk * TB, TB), :]
                    link(dve.scalar_tensor_tensor(out=acc[:, :, :], in0=ps_s[p][:, :].rearrange("p (q d) -> p q d", q=TB), scalar=svec[:, 5:6],
                                                  in1=boutb[:, :].rearrange("p (o d) -> p o d", o=1).to_broadcast([128, TB, D]),
                                                  op0=ALU.mult, op1=ALU.add))
                    dve.tensor_tensor(dst, dst, acc[:, :, :], ALU.add).then_inc(sig["x_new"], 1)
                    wait(dve, "x_new", cnt.at("x_new", ph, blk))
                    apart(dve)
                    all_statistics(block_tiles(x_tok, blk), blk * TB)

                with dve.Fori(0, NBLK // 2) as i:
                    link.enter(i, 10)
                    quantise_h(i * 2, 0)
                    quantise_h(i * 2 + 1, 1)
                    add(i * 2, 0)
                    add(i * 2 + 1, 1)
                link.leave(NBLK // 2)

            def experts(ph):
                ne = 9 if ph == "F1" else 8
                src_of = y_tok if ph == "F2" else x_tok
                gb = {"F1": 0, "F2": None, "F3": 1}[ph]

                def norm(blk):
                    wait(dve, "fxt_ready", cnt.at("fxt_ready", ph, blk) - 1)
                    ins = normalise(block_tiles(src_of, blk), [xf[:, q, :] for q in range(TB)], blk * TB)
                    ins.then_inc(sig["xn_done"], 1)
                    if ph == "F3":
                        wait(dve, "xn_done", cnt.at("xn_done", ph, blk))
                        dve.tensor_copy(y_tok[:, bass.ds(blk * TB, TB), :], xf[:, :, :])

                def gates(blk):
                    wait(dve, "lg_ready", cnt.at("lg_ready", ph, blk))
                    logits = ps_av[:, 0:TB * E].rearrange("p (q e) -> p q e", q=TB)
                    if gb is None:
                        link(dve.tensor_copy(lg[:, :, :], logits), apart)
                    else:
                        link(dve.tensor_tensor(lg[:, :, :], logits, gate_bb[:, gb:gb + 1, :].to_broadcast([128, TB, E]), ALU.add), apart)
                    for q in range(TB):
                        ins = dve.max(top[:, q, :], lg[:, q, :])
                    link(ins, apart)
                    for q in range(TB):
                        ins = dve.max_index(topi[:, q, :], top[:, q, :], lg[:, q, :])
                    link(ins)
                    dve.tensor_tensor(dlt[:, :], top[:, :, 1], top[:, :, 0], ALU.subtract).then_inc(sig["lg_read"], 1)
                    link(dve.tensor_copy(topf[:, :, :], topi[:, :, 0:2]))
                    for n in range(2):
                        ins = dve.tensor_tensor(eq[:, n, :, :], iota_e[:, :].rearrange("p (o e) -> p o e", o=1).to_broadcast([128, TB, E]),
                                                topf[:, :, n:n + 1].to_broadcast([128, TB, E]), ALU.is_equal)
                    wait(dve, "th_done", cnt.at("th_done", ph, blk))
                    dve.tensor_scalar(w2[:, 0, :], th[:, :], -0.5, 0.5, ALU.mult, ALU.add)
                    link(dve.tensor_scalar(w2[:, 1, :], th[:, :], 0.5, 0.5, ALU.mult, ALU.add))
                    for n in range(2):
                        ins = dve.tensor_tensor(eq[:, n, :, :], eq[:, n, :, :],
                                                w2[:, n, :].rearrange("p (q o) -> p q o", o=1).to_broadcast([128, TB, E]), ALU.mult)
                    link(ins)
                    dve.tensor_tensor(comb[:, :, 0:E], eq[:, 0, :, :], eq[:, 1, :, :], ALU.add).then_inc(sig["comb_done"], 1)
                    wait(dve, "comb_done", cnt.at("comb_done", ph, blk))

                def gated(blk, e):
                    h = prob[:, e % 2, :, :].rearrange("p c s -> p (c s)")[:, 0:2048].rearrange("p (c s) -> p c s", c=4)
                    wait(dve, "h_ready", cnt.at("h_ready", ph, blk, 4 * e + 3))
                    for c in range(2):
                        wait(dve, "h_done", cnt.at("h_done", ph, blk, 2 * e + c))
                        dve.tensor_tensor(h[:, c, :], ps_h[2 + c][:, :], h[:, 2 + c, :], ALU.mult).then_inc(sig["g_done"], 1)

                def accumulate(blk, n):
                    wait(dve, "y_ready", cnt.at("y_ready", ph, blk, n))
                    if n:
                        wait(dve, "acc_done", cnt.at("acc_done", ph, blk, n) - 1)
                    if n == E:
                        dve.tensor_tensor(acc[:, :, :], ps_s[n % 2][:, :].rearrange("p (q d) -> p q d", q=TB), acc[:, :, :], ALU.add)\
                           .then_inc(sig["acc_done"], 1)
                        return
                    for q in range(TB):
                        src = ps_s[n % 2][:, 128 * q:128 * (q + 1)]
                        if n == 0:
                            ins = dve.tensor_scalar(acc[:, q, :], src, comb[:, q, 0:1], None, ALU.mult)
                        else:
                            ins = dve.scalar_tensor_tensor(out=acc[:, q, :], in0=src, scalar=comb[:, q, n:n + 1], in1=acc[:, q, :],
                                                           op0=ALU.mult, op1=ALU.add)
                    ins.then_inc(sig["acc_done"], 1)

                def result(blk, n_last):
                    dst = x_tok[:, bass.ds(blk * TB, TB), :]
                    inner = y_tok[:, bass.ds(blk * TB, TB), :]
                    wait(dve, "acc_done", cnt.at("acc_done", ph, blk, n_last))
                    if ph != "F1":
                        link(dve.tensor_tensor(acc[:, :, :], acc[:, :, :], inner, ALU.add))
                    if ph == "F3":
                        tiles = [acc[:, q, :] for q in range(TB)]
                        for step in range(2):
                            statistics(step, tiles, st6b, mvb)
                        link.until(since["aggregate"])
                        dve.tensor_scalar(vepsb[:, :], mvb[:, :, 1], 1e-12, None, ALU.add).then_inc(sig["var2_done"], 1)
                        wait(dve, "rstd2_done", cnt.at("rstd2_done", ph, blk))
                        for q, s in enumerate(tiles):
                            ins = dve.tensor_scalar(s, s, mvb[:, q, 0:1], rstdb[:, q:q + 1], ALU.subtract, ALU.mult)
                        link(ins)
                        for i, op in enumerate((ALU.mult, ALU.add)):
                            link(dve.tensor_tensor(acc[:, :, :], acc[:, :, :], lnw[:, i:i + 1, :].to_broadcast([128, TB, D]), op))
                    dve.tensor_tensor(dst, dst, acc[:, :, :], ALU.add).then_inc(sig["x_new"], 1)
                    if ph != "F3":
                        wait(dve, "x_new", cnt.at("x_new", ph, blk))
                        apart(dve)
                        all_statistics(block_tiles(x_tok, blk), blk * TB)

                def body(blk, last):
                    if ph == "F2":
                        gated(blk, 0)
                    gates(blk)
                    for e in range(ne):
                        if ph == "F2" and e + 1 < ne:
                            gated(blk, e + 1)
                        if e == 5 and ph != "F2":
                            wait(dve, "ct_ready", cnt.at("ct_ready", ph, blk))
                            dve.tensor_copy(combT[:, :], ps_av[0:E + 1, :]).then_inc(sig["ct_read"], 1)
                        accumulate(blk, e)
                        if not last and e == 3:
                            norm(blk + 1)
                    if ph == "F3":
                        accumulate(blk, E)
                    result(blk, E if ph != "F2" else E - 1)

                wait(dve, "x_new", cnt.start("x_new", ph))
                wait(dve, "rstd_done", cnt.start("rstd_done", ph))
                norm(0)
                blocks(dve, NBLK - 1, lambda blk: body(blk, False), link, LINKS[ph])
                body(NBLK - 1, True)

            dve.wait_ge(x_loaded, 16)
            for blk in range(NBLK):
                all_statistics([x_tok[:, TB * blk + q, :] for q in range(TB)], blk * TB)
            for p in range(2):
                link(dve.memset(vaug[p][:, :, :, :], 0.0))
                link(dve.memset(vaug[p][:, :, :, DH:DH + 1], 1.0))
            dve.memset(junk[:, :, :], 0.0)
            dve.wait_ge(loaded_first, 16 * N_FIRST)
            dve.tensor_scalar(b_att["A0"][:, 0:1], b_att["A0"][:, 0:1], ATT["A0"]["scale"], None, ALU.mult).then_inc(bias_scaled, 1)
            dve.wait_ge(setup_pool, 2)
            for name, n in cnt.credit.items():
                if name not in ("var_done", "rstd_done"):
                    dve.sem_inc(sig[name], n)
            for ph in PHASES:
                if ph in ATT:
                    attention(ph)
                elif ph == "F0":
                    quantised_ffn()
                else:
                    experts(ph)




def kernel(**inputs):
    import numpy as np

    import concourse.bacc as bacc
    from concourse import mybir as mb
    from concourse.bass_utils import run_bass_kernel_spmd

    a = {k: np.asarray(v) for k, v in inputs.items()}
    c = np.ascontiguousarray
    t = {
        "x": a["x"],
        "ctxT": c(a["ctx_1024"].transpose(0, 2, 1)),
        "mask_q": c(a["mask_1x1xSxS2_ik0"][0, 0]),
        "mask_T": c(a["mask_1x1xSxS2_ik0"][0, 0].T),
        "mask_k": c(a["mask_Bx1x1xS2_if1"][:, 0, 0]),
        "mask_kT": c(a["mask_Bx1x1xS2_if1"][:, 0, 0].reshape(8, 4, 128).transpose(0, 2, 1)),
        "ln1_scale": a["L2_ffn_ln1_scale"], "ln1_shift": a["L2_ffn_ln1_shift"],
        "ln2_scale": a["L2_ffn_ln2_scale"], "ln2_shift": a["L2_ffn_ln2_shift"],
        "ln_w": a["L3_ffn_ln_w"], "ln_b": a["L3_ffn_ln_b"],
        "F0_w1": a["L0_ffn_W_in"], "F0_b1": c(a["L0_ffn_b_in"].reshape(4, 128).T),
        "F0_w2": a["L0_ffn_W_out"], "F0_b2": a["L0_ffn_b_out"],
        "F1_gate": a["L1_ffn_gate_w"], "F1_gate_b": a["L1_ffn_gate_b"],
        "F1_w1": a["L1_ffn_w1"], "F1_b1": c(a["L1_ffn_b1"].reshape(8, 4, 128).transpose(2, 0, 1).reshape(128, 32)),
        "F1_w2": a["L1_ffn_w2"], "F1_b2": a["L1_ffn_b2"],
        "F1_ws1": a["L1_ffn_ws1"], "F1_bs1": c(a["L1_ffn_bs1"].reshape(4, 128).T),
        "F1_ws2": a["L1_ffn_ws2"], "F1_bs2": a["L1_ffn_bs2"],
        "F2_gate": a["L2_ffn_gate_w"], "F2_w1": a["L2_ffn_w1"], "F2_w2": a["L2_ffn_w2"], "F2_w3": a["L2_ffn_w3"],
        "F3_gate": c(a["L3_ffn_Wr"].T), "F3_gate_b": a["L3_ffn_br"],
        "F3_w1": c(a["L3_ffn_W1"].transpose(0, 2, 1)),
        "F3_b1": c(a["L3_ffn_b1"].reshape(8, 4, 128).transpose(2, 0, 1).reshape(128, 32)),
        "F3_w2": c(a["L3_ffn_W2"].transpose(0, 2, 1)), "F3_b2": a["L3_ffn_b2"],
    }
    for ph, pre in (("A0", "L0_xattn_w{}"), ("A1", "L1_xattn_w{}"), ("A2", "L2_xattn_W{}_w")):
        for w in "qkvo":
            t[f"{ph}_{w}"] = c(a[pre.format(w)].T)
    for ph, pre in (("A0", "L0_xattn_b{}"), ("A1", "L1_xattn_b{}"), ("A2", "L2_xattn_W{}_b")):
        for w in "qkvo":
            t[f"{ph}_b{w}"] = a[pre.format(w)]
    for w in "qkvo":
        t[f"AS_{w}"] = a[f"L2_ffn_w{w}"]
    t["AS_bo"] = a["L2_ffn_bo"]
    for w in "qkv":
        t[f"A3_{w}"] = c(a[f"L3_xattn_W{w}"].T)
    t["A3_o"], t["A3_bo"] = c(a["L3_xattn_Wo"].T), a["L3_xattn_bo"]

    nc = bacc.Bacc("TRN2", target_bir_lowering=False, num_devices=1)
    arrays = {f"in_{n}": np.ascontiguousarray(v) for n, v in t.items()}
    aps = {n: nc.dram_tensor(f"in_{n}", v.shape, mb.dt.from_np(v.dtype), kind="ExternalInput").ap() for n, v in
           ((n[3:], v) for n, v in arrays.items())}
    out = nc.dram_tensor("out_x", (8, 256, 128), mb.dt.float32, kind="ExternalOutput").ap()
    build(nc, aps, out)
    r = run_bass_kernel_spmd(nc, [arrays], core_ids=[0])
    return r.results[0]["out_x"]
```
